# Optimizing a Trainium2 kernel written in Bass

```python
import numpy as np
import jax
import jax.numpy as jnp

def _softmax(x, axis=-1):
    return jax.nn.softmax(x, axis=axis)

def _gelu(x):
    return jax.nn.gelu(x, approximate=True)

def _silu(x):
    return jax.nn.silu(x)

def _sigmoid(x):
    return jax.nn.sigmoid(x)

def _layernorm(x, axis=-1, eps=1e-05):
    m = jnp.mean(x, axis=axis, keepdims=True)
    v = jnp.var(x, axis=axis, keepdims=True)
    return (x - m) / jnp.sqrt(v + eps)

def _scatter_add(tgt, idx, src, axis=0):
    return tgt.at[idx].add(src)

def _segment_sum(src, seg, n):
    return jax.ops.segment_sum(src, seg, n)
kernel_name = 'mk_adj_ffn_d2_adj_r2_8a4814'

def setup_inputs(seed: int=0):
    np.random.seed(seed)
    _w = jnp.asarray

    def _rec_inputs():
        import jax
        import jax.numpy as jnp
        _gk = jax.random.key(seed)
        x = -0.0002928 + 1 * jax.random.normal(jax.random.fold_in(_gk, 1), (128, 128, 128), jnp.float32)
        _a = jax.random.bernoulli(jax.random.fold_in(_gk, 2), 0.03125, (128, 128, 128))
        _a = jnp.logical_or(_a, jnp.swapaxes(_a, -1, -2))
        _a = jnp.logical_or(_a, jnp.eye(128, dtype=bool))
        adj = _a.astype(jnp.int32)
        return (x, adj)
    x, adj = _rec_inputs()

    def _L0_gnn_setup():
        import jax, jax.numpy as jnp
        import numpy as np
        EPS = 1e-05

        def _layernorm(x, w, b):
            m = jnp.mean(x, axis=-1, keepdims=True)
            v = jnp.mean((x - m) ** 2, axis=-1, keepdims=True)
            return (x - m) * jax.lax.rsqrt(v + EPS) * w + b

        def _swish(x):
            return x * jax.nn.sigmoid(x)
        key = jax.random.key(seed)
        ks = jax.random.split(key, 10)
        B, A, D_IN, D_OUT = (8, 1024, 128, 128)
        s_in = 1.0 / np.sqrt(D_IN)
        s_out = 1.0 / np.sqrt(D_OUT)
        return {'x': jax.random.normal(ks[0], (B, A, D_IN), dtype=jnp.float32), 'connectivity': jax.random.randint(ks[1], (B, A, A), 0, 2, dtype=jnp.int32), 'Wq': jax.random.uniform(ks[2], (D_OUT, D_IN), jnp.float32, -s_in, s_in), 'Wk': jax.random.uniform(ks[3], (D_OUT, D_IN), jnp.float32, -s_in, s_in), 'Wv': jax.random.uniform(ks[4], (D_OUT, D_IN), jnp.float32, -s_in, s_in), 'ln1_w': jnp.ones((D_OUT,), jnp.float32), 'ln1_b': jnp.zeros((D_OUT,), jnp.float32), 'W1': jax.random.uniform(ks[5], (D_OUT, D_OUT), jnp.float32, -s_out, s_out), 'b1': jax.random.uniform(ks[6], (D_OUT,), jnp.float32, -s_out, s_out), 'ln2_w': jnp.ones((D_OUT,), jnp.float32), 'ln2_b': jnp.zeros((D_OUT,), jnp.float32), 'W2': jax.random.uniform(ks[7], (D_OUT, D_OUT), jnp.float32, -s_out, s_out), 'b2': jax.random.uniform(ks[8], (D_OUT,), jnp.float32, -s_out, s_out), 'lnf_w': jnp.ones((D_OUT,), jnp.float32), 'lnf_b': jnp.zeros((D_OUT,), jnp.float32)}
    _L0_gnn_all = _L0_gnn_setup()
    _L0_gnn_in = {k: v for k, v in _L0_gnn_all.items() if k in ('Wq', 'Wk', 'Wv', 'ln1_w', 'ln1_b', 'W1', 'b1', 'ln2_w', 'ln2_b', 'W2', 'b2', 'lnf_w', 'lnf_b')}
    del _L0_gnn_all

    def _L0_ffn_setup():
        import jax, jax.numpy as jnp
        import numpy as np
        C = 128
        HID = 512
        E = 8
        TEMP = 1.0
        key = jax.random.key(seed)
        ks = jax.random.split(key, 7)
        x = jax.random.normal(ks[0], (8, 8192, C), dtype=jnp.float32)
        W1 = jax.random.normal(ks[1], (C, HID), dtype=jnp.float32) * 0.02
        b1 = jnp.zeros((HID,), dtype=jnp.float32)
        Wg = jax.random.normal(ks[2], (HID, E), dtype=jnp.float32) * 0.02
        bg = jnp.zeros((E,), dtype=jnp.float32)
        Wd = jax.random.normal(ks[3], (E, HID, C), dtype=jnp.float32) * 0.02
        bd = jnp.zeros((E, C), dtype=jnp.float32)
        return {'x': x, 'W1': W1, 'b1': b1, 'Wg': Wg, 'bg': bg, 'Wd': Wd, 'bd': bd}
    _L0_ffn_all = _L0_ffn_setup()
    _L0_ffn_in = {k: v for k, v in _L0_ffn_all.items() if k in ('W1', 'b1', 'Wg', 'bg', 'Wd', 'bd')}
    del _L0_ffn_all

    def _L1_gnn_setup():
        import jax, jax.numpy as jnp
        import numpy as np
        import math
        IN_DIM = 128
        OUT_DIM = 128
        HEADS = 4
        D_K = OUT_DIM // HEADS
        key = jax.random.key(seed)
        ks = jax.random.split(key, 10)
        B, N = (4, 2048)
        x = jax.random.normal(ks[0], (B, N, IN_DIM), dtype=jnp.float32)
        adj = jax.random.randint(ks[1], (B, N, N), 0, 2, dtype=jnp.int32)
        s = 1.0 / math.sqrt(IN_DIM)
        Wq = jax.random.normal(ks[2], (IN_DIM, OUT_DIM), dtype=jnp.float32) * s
        bq = jnp.zeros((OUT_DIM,), dtype=jnp.float32)
        Wk = jax.random.normal(ks[3], (IN_DIM, OUT_DIM), dtype=jnp.float32) * s
        bk = jnp.zeros((OUT_DIM,), dtype=jnp.float32)
        Wv = jax.random.normal(ks[4], (IN_DIM, OUT_DIM), dtype=jnp.float32) * s
        bv = jnp.zeros((OUT_DIM,), dtype=jnp.float32)
        Wo = jax.random.normal(ks[5], (OUT_DIM, OUT_DIM), dtype=jnp.float32) * (1.0 / math.sqrt(OUT_DIM))
        bo = jnp.zeros((OUT_DIM,), dtype=jnp.float32)
        return {'x': x, 'adj': adj, 'Wq': Wq, 'bq': bq, 'Wk': Wk, 'bk': bk, 'Wv': Wv, 'bv': bv, 'Wo': Wo, 'bo': bo}
    _L1_gnn_all = _L1_gnn_setup()
    _L1_gnn_in = {k: v for k, v in _L1_gnn_all.items() if k in ('Wq', 'bq', 'Wk', 'bk', 'Wv', 'bv', 'Wo', 'bo')}
    del _L1_gnn_all

    def _L1_ffn_setup():
        import jax, jax.numpy as jnp
        import numpy as np
        B, T, D, H, E = (16, 2048, 128, 256, 8)
        key = jax.random.key(seed)
        ks = jax.random.split(key, 5)
        x = jax.random.normal(ks[0], (B, T, D), dtype=jnp.float32)
        gate_w = jax.random.normal(ks[1], (D, E), dtype=jnp.float32) * 0.02
        gate_b = jnp.zeros((E,), dtype=jnp.float32)
        W1 = jax.random.normal(ks[2], (E, D, H), dtype=jnp.float32) * 0.02
        b1 = jnp.zeros((E, H), dtype=jnp.float32)
        W2 = jax.random.normal(ks[3], (E, H, D), dtype=jnp.float32) * 0.02
        b2 = jnp.zeros((E, D), dtype=jnp.float32)
        return {'x': x, 'gate_w': gate_w, 'gate_b': gate_b, 'W1': W1, 'b1': b1, 'W2': W2, 'b2': b2}
    _L1_ffn_all = _L1_ffn_setup()
    _L1_ffn_in = {k: v for k, v in _L1_ffn_all.items() if k in ('gate_w', 'gate_b', 'W1', 'b1', 'W2', 'b2')}
    del _L1_ffn_all
    return {'x': x, 'adj': adj, 'L0_gnn_Wq': _L0_gnn_in['Wq'], 'L0_gnn_Wk': _L0_gnn_in['Wk'], 'L0_gnn_Wv': _L0_gnn_in['Wv'], 'L0_gnn_ln1_w': _L0_gnn_in['ln1_w'], 'L0_gnn_ln1_b': _L0_gnn_in['ln1_b'], 'L0_gnn_W1': _L0_gnn_in['W1'], 'L0_gnn_b1': _L0_gnn_in['b1'], 'L0_gnn_ln2_w': _L0_gnn_in['ln2_w'], 'L0_gnn_ln2_b': _L0_gnn_in['ln2_b'], 'L0_gnn_W2': _L0_gnn_in['W2'], 'L0_gnn_b2': _L0_gnn_in['b2'], 'L0_gnn_lnf_w': _L0_gnn_in['lnf_w'], 'L0_gnn_lnf_b': _L0_gnn_in['lnf_b'], 'L0_ffn_W1': _L0_ffn_in['W1'], 'L0_ffn_b1': _L0_ffn_in['b1'], 'L0_ffn_Wg': _L0_ffn_in['Wg'], 'L0_ffn_bg': _L0_ffn_in['bg'], 'L0_ffn_Wd': _L0_ffn_in['Wd'], 'L0_ffn_bd': _L0_ffn_in['bd'], 'L1_gnn_Wq': _L1_gnn_in['Wq'], 'L1_gnn_bq': _L1_gnn_in['bq'], 'L1_gnn_Wk': _L1_gnn_in['Wk'], 'L1_gnn_bk': _L1_gnn_in['bk'], 'L1_gnn_Wv': _L1_gnn_in['Wv'], 'L1_gnn_bv': _L1_gnn_in['bv'], 'L1_gnn_Wo': _L1_gnn_in['Wo'], 'L1_gnn_bo': _L1_gnn_in['bo'], 'L1_ffn_gate_w': _L1_ffn_in['gate_w'], 'L1_ffn_gate_b': _L1_ffn_in['gate_b'], 'L1_ffn_W1': _L1_ffn_in['W1'], 'L1_ffn_b1': _L1_ffn_in['b1'], 'L1_ffn_W2': _L1_ffn_in['W2'], 'L1_ffn_b2': _L1_ffn_in['b2']}

def reference(x, adj, L0_gnn_Wq, L0_gnn_Wk, L0_gnn_Wv, L0_gnn_ln1_w, L0_gnn_ln1_b, L0_gnn_W1, L0_gnn_b1, L0_gnn_ln2_w, L0_gnn_ln2_b, L0_gnn_W2, L0_gnn_b2, L0_gnn_lnf_w, L0_gnn_lnf_b, L0_ffn_W1, L0_ffn_b1, L0_ffn_Wg, L0_ffn_bg, L0_ffn_Wd, L0_ffn_bd, L1_gnn_Wq, L1_gnn_bq, L1_gnn_Wk, L1_gnn_bk, L1_gnn_Wv, L1_gnn_bv, L1_gnn_Wo, L1_gnn_bo, L1_ffn_gate_w, L1_ffn_gate_b, L1_ffn_W1, L1_ffn_b1, L1_ffn_W2, L1_ffn_b2):
    import jax
    import jax.numpy as jnp

    def _L0_gnn_ref(x, connectivity, Wq, Wk, Wv, ln1_w, ln1_b, W1, b1, ln2_w, ln2_b, W2, b2, lnf_w, lnf_b):
        import jax, jax.numpy as jnp
        import numpy as np
        EPS = 1e-05

        def _layernorm(x, w, b):
            m = jnp.mean(x, axis=-1, keepdims=True)
            v = jnp.mean((x - m) ** 2, axis=-1, keepdims=True)
            return (x - m) * jax.lax.rsqrt(v + EPS) * w + b

        def _swish(x):
            return x * jax.nn.sigmoid(x)
        D_OUT = Wq.shape[0]
        scale = jnp.sqrt(jnp.float32(D_OUT))
        Q = jnp.einsum('bah,oh->bao', x, Wq)
        K = jnp.einsum('bah,oh->bao', x, Wk)
        V = jnp.einsum('bah,oh->bao', x, Wv)
        scores = jnp.einsum('bqd,bkd->bqk', Q, K) / scale
        mask = (connectivity == 0).astype(scores.dtype) * -1000000000.0
        alpha = jax.nn.softmax(scores + mask, axis=-1)
        H = jnp.einsum('bqk,bkd->bqd', alpha, V)
        h = _layernorm(_swish(H), ln1_w, ln1_b)
        h = jnp.einsum('bad,od->bao', h, W1) + b1
        h = _layernorm(_swish(h), ln2_w, ln2_b)
        h = jnp.einsum('bad,od->bao', h, W2) + b2
        return _layernorm(h, lnf_w, lnf_b)

    def _L0_ffn_ref(x, W1, b1, Wg, bg, Wd, bd):
        import jax, jax.numpy as jnp
        import numpy as np
        C = 128
        HID = 512
        E = 8
        TEMP = 1.0
        orig_shape = x.shape
        xf = x.reshape(-1, orig_shape[-1])
        H = jax.nn.gelu(xf @ W1 + b1, approximate=False)
        probs = jax.nn.softmax((H @ Wg + bg) / TEMP, axis=-1)
        assign = jnp.argmax(probs, axis=-1)
        out = jnp.zeros_like(xf)
        for e in range(Wd.shape[0]):
            y = H @ Wd[e] + bd[e]
            sel = (assign == e)[:, None]
            out = out + jnp.where(sel, probs[:, e:e + 1] * y, 0.0)
        return out.reshape(orig_shape)

    def _L1_gnn_ref(x, adj, Wq, bq, Wk, bk, Wv, bv, Wo, bo):
        import jax, jax.numpy as jnp
        import numpy as np
        import math
        IN_DIM = 128
        OUT_DIM = 128
        HEADS = 4
        D_K = OUT_DIM // HEADS
        B, N, _ = x.shape
        q = (x @ Wq + bq).reshape(B, N, HEADS, D_K)
        k = (x @ Wk + bk).reshape(B, N, HEADS, D_K)
        v = (x @ Wv + bv).reshape(B, N, HEADS, D_K)
        scale = 1.0 / math.sqrt(D_K + 1e-09)
        scores = jnp.einsum('bnhd,bmhd->bhnm', q, k) * scale
        eye = jnp.eye(N, dtype=bool)
        mask = (adj.astype(bool) | eye)[:, None, :, :]
        min_val = jnp.finfo(scores.dtype).min
        scores = jnp.where(mask, scores, min_val)
        attn = jax.nn.softmax(scores, axis=-1)
        out = jnp.einsum('bhnm,bmhd->bnhd', attn, v).reshape(B, N, OUT_DIM)
        out = out @ Wo + bo
        return jax.nn.relu(out)

    def _L1_ffn_ref(x, gate_w, gate_b, W1, b1, W2, b2):
        import jax, jax.numpy as jnp
        import numpy as np
        B, T, D, H, E = (16, 2048, 128, 256, 8)
        Bb, Tt, Dd = x.shape
        Ee = gate_w.shape[1]
        xf = x.reshape(-1, Dd)
        N = xf.shape[0]
        logits = xf @ gate_w + gate_b
        probs = jax.nn.softmax(logits, axis=-1)
        top2_vals, top2_idx = jax.lax.top_k(probs, 2)
        cw = jnp.zeros((N, Ee), dtype=xf.dtype).at[jnp.arange(N)[:, None], top2_idx].add(top2_vals)

        def step(acc, params):
            w1, bb1, w2, bb2, we = params
            h = jax.nn.gelu(xf @ w1 + bb1, approximate=False)
            y = h @ w2 + bb2
            return (acc + we[:, None] * y, None)
        out, _ = jax.lax.scan(step, jnp.zeros_like(xf), (W1, b1, W2, b2, cw.T))
        return out.reshape(Bb, Tt, Dd)
    x = x + _L0_gnn_ref(_layernorm(x, axis=-1), adj, L0_gnn_Wq, L0_gnn_Wk, L0_gnn_Wv, L0_gnn_ln1_w, L0_gnn_ln1_b, L0_gnn_W1, L0_gnn_b1, L0_gnn_ln2_w, L0_gnn_ln2_b, L0_gnn_W2, L0_gnn_b2, L0_gnn_lnf_w, L0_gnn_lnf_b)
    x = x + _L0_ffn_ref(_layernorm(x, axis=-1), L0_ffn_W1, L0_ffn_b1, L0_ffn_Wg, L0_ffn_bg, L0_ffn_Wd, L0_ffn_bd)
    x = x + _L1_gnn_ref(_layernorm(x, axis=-1), adj, L1_gnn_Wq, L1_gnn_bq, L1_gnn_Wk, L1_gnn_bk, L1_gnn_Wv, L1_gnn_bv, L1_gnn_Wo, L1_gnn_bo)
    x = x + _L1_ffn_ref(_layernorm(x, axis=-1), L1_ffn_gate_w, L1_ffn_gate_b, L1_ffn_W1, L1_ffn_b1, L1_ffn_W2, L1_ffn_b2)
    return x

_drawn_inputs = setup_inputs


def setup_inputs(seed=0):
    import zlib

    import numpy as np

    out = dict(_drawn_inputs(seed))
    spreads = {'L0_gnn_ln1_w': (1.0, 0.2),
     'L0_gnn_ln1_b': (0.0, 0.1),
     'L0_gnn_ln2_w': (1.0, 0.2),
     'L0_gnn_ln2_b': (0.0, 0.1),
     'L0_gnn_lnf_w': (1.0, 0.2),
     'L0_gnn_lnf_b': (0.0, 0.1),
     'L0_ffn_b1': (0.0, 0.8),
     'L0_ffn_bg': (0.0, 0.592),
     'L0_ffn_bd': (0.0, 0.769),
     'L1_gnn_bq': (0.0, 0.532),
     'L1_gnn_bk': (0.0, 0.8),
     'L1_gnn_bv': (0.0, 0.1),
     'L1_gnn_bo': (0.0, 0.1),
     'L1_ffn_gate_b': (0.0, 0.8),
     'L1_ffn_b1': (0.0, 0.8),
     'L1_ffn_b2': (0.0, 0.517)}
    factors = {'L0_ffn_W1': 7.082,
     'L0_ffn_Wg': 6.604,
     'L0_ffn_Wd': 8.0,
     'L1_ffn_gate_w': 3.921,
     'L1_ffn_W1': 8.0,
     'L1_ffn_W2': 8.0}
    for name, (base, spread) in spreads.items():
        noise = np.random.default_rng([zlib.crc32(name.encode()), seed]).standard_normal(out[name].shape)
        drawn = base * np.exp(spread * noise) if base else spread * noise
        out[name] = jnp.asarray(drawn.astype(out[name].dtype))
    for name, factor in factors.items():
        out[name] = (out[name] * factor).astype(out[name].dtype)
    return out
```

```python
import math
from contextlib import ExitStack

import concourse.bass as bass
from concourse import mybir

F32 = mybir.dt.float32
BF16 = mybir.dt.bfloat16
I32 = mybir.dt.int32
ALU = mybir.AluOpType
ACT = mybir.ActivationFunctionType
AX = mybir.AxisListType

P = 128
TILES = 4
W = TILES * P
LANES = (0, 1)
EPS = 1e-5
EXPERTS = 8
HID0 = 512
HID1 = 256
HEADS = 4
DK = P // HEADS
C0 = HID0 // P
C1 = HID1 // P
QK_SCALE = 1.0 / math.sqrt(DK + 1e-09)

PHASES = ("gnn0", "ffn0", "gnn1", "ffn1")

WEIGHTS = [
    "L0_gnn_Wq", "L0_gnn_Wk", "L0_gnn_Wv", "L0_gnn_ln1_w", "L0_gnn_ln1_b", "L0_gnn_W1", "L0_gnn_b1",
    "L0_gnn_ln2_w", "L0_gnn_ln2_b", "L0_gnn_W2", "L0_gnn_b2", "L0_gnn_lnf_w", "L0_gnn_lnf_b",
    "L0_ffn_W1", "L0_ffn_b1", "L0_ffn_Wg", "L0_ffn_bg", "L0_ffn_Wd", "L0_ffn_bd",
    "L1_gnn_Wq", "L1_gnn_bq", "L1_gnn_Wk", "L1_gnn_bk", "L1_gnn_Wv", "L1_gnn_bv", "L1_gnn_Wo", "L1_gnn_bo",
    "L1_ffn_gate_w", "L1_ffn_gate_b", "L1_ffn_W1", "L1_ffn_b1", "L1_ffn_W2", "L1_ffn_b2",
]


def build(nc, x, adj, w, out):
    batches = x.shape[0]
    groups = batches // TILES
    pairs = groups // len(LANES)
    ctx = ExitStack()
    with ctx:
        def sb(name, shape, dt=F32):
            return ctx.enter_context(nc.sbuf_tensor(name, shape, dt))

        def lane_sb(name, shape, dt=F32):
            return [sb(f"{name}_{lane}", shape, dt) for lane in LANES]

        def sem(name):
            return ctx.enter_context(nc.semaphore(name))

        signals = []

        class Signal:

            def __init__(self, name, step=1, **per):
                self.sem = [sem(f"{name}_{lane}") for lane in LANES]
                self.step, self.per, self.base, total = step, per, {}, 1
                for phase in PHASES:
                    self.base[phase] = total
                    total += per.get(phase, 0) * pairs
                signals.append(self)

            def nth(self, phase, i, k=0):
                return (i * self.per[phase] + (self.base[phase] + k + 1)) * self.step

            def before(self, phase, i, k=None):
                left = 0 if k is None or self.base[phase] == 1 else self.per[phase] - 1 - k
                return (i * self.per[phase] + (self.base[phase] - left)) * self.step

            def end(self, phase):
                return (self.base[phase] + self.per.get(phase, 0) * pairs) * self.step

        x1 = nc.dram_tensor("x1", (batches, P, P), F32, kind="Internal").ap()
        x2 = nc.dram_tensor("x2", (batches, P, P), F32, kind="Internal").ap()
        x3 = nc.dram_tensor("x3", (batches, P, P), F32, kind="Internal").ap()
        row_parts = nc.dram_tensor("row_parts", (3, 3, P), BF16, kind="Internal").ap()

        def group(t):
            return t.rearrange("(g t) p f -> g p t f", t=TILES)

        x_g, adj_g, out_g = group(x), group(adj), group(out)
        x1_g, x2_g, x3_g = group(x1), group(x2), group(x3)

        ident = sb("ident", [P, P])
        off_diag = sb("off_diag", [P, P], BF16)
        far0 = sb("far0", [P, 3, P], BF16)
        far1 = sb("far1", [P, P], BF16)
        ones3 = sb("ones3", [3, P], BF16)
        ones1 = sb("ones1", [1, P])
        half_neg = sb("half_neg", [P, TILES])
        eps_tile, eps4_tile = sb("eps_tile", [P, TILES]), sb("eps4_tile", [P, TILES])
        iota_e = sb("iota_e", [P, TILES, EXPERTS])
        NCOL = 10 + C0 + EXPERTS * C1
        rows = sb("rows", [NCOL, P])
        cols = sb("cols", [P, NCOL])
        R_LN1W, R_LN1B, R_LN2W, R_LN2B, R_BQ, R_BK, R_BV, R_L0B1 = 0, 1, 2, 3, 4, 5, 6, 10
        R_L1B1 = R_L0B1 + C0
        wq0, wk0, wv0 = sb("wq0", [P, P]), sb("wk0", [P, P]), sb("wv0", [P, P])
        w10, w20 = sb("w10", [P, P]), sb("w20", [P, P])
        qk0 = sb("qk0", [P, P])
        wv0T, w10T, w20T = sb("wv0T", [P, P]), sb("w10T", [P, P]), sb("w20T", [P, P])
        w10s, w20s = sb("w10s", [P, P]), sb("w20s", [P, P])
        lnf_w = sb("lnf_w", [P, P])
        lnf_b = sb("lnf_b", [P, P])
        bias_in = sb("bias_in", [1, 3, P])
        bias_row = sb("bias_row", [1, 3, P])
        bias_hi = sb("bias_hi", [1, 3, 3, P], BF16)
        bias_rest = sb("bias_rest", [1, 3, P])
        bias_rest2 = sb("bias_rest2", [1, 3, P])
        bias3 = sb("bias3", [3, 3, TILES, P], BF16)
        wq1, wk1, wv1, wo1 = sb("wq1", [P, P]), sb("wk1", [P, P]), sb("wv1", [P, P]), sb("wo1", [P, P])
        bq_s = sb("bq_s", [P, 1])
        f0_w1 = sb("f0_w1", [P, HID0])
        f0_wg = sb("f0_wg", [P, C0, EXPERTS])
        f0_bg = sb("f0_bg", [1, TILES, EXPERTS])
        f0_wd = sb("f0_wd", [P, EXPERTS, C0, P])
        f0_bd = sb("f0_bd", [1, EXPERTS, P])
        f1_wg = sb("f1_wg", [P, EXPERTS])
        f1_bg = sb("f1_bg", [1, TILES, EXPERTS])
        f1_w1 = sb("f1_w1", [P, EXPERTS, HID1])
        f1_w2 = sb("f1_w2", [P, EXPERTS, C1, P])
        f1_b2 = sb("f1_b2", [1, EXPERTS, P])

        x_in = lane_sb("x_in", [P, TILES, P])
        x_res = lane_sb("x_res", [P, TILES, P])
        adj_in = lane_sb("adj_in", [P, TILES, P], I32)
        no_edge = lane_sb("no_edge", [P, TILES, P], BF16)
        no_edge1 = lane_sb("no_edge1", [P, TILES, P], BF16)
        bn = lane_sb("bn", [P, TILES, 6])
        mv = lane_sb("mv", [P, TILES, 2])
        var_eps = lane_sb("var_eps", [P, TILES])
        rstd = lane_sb("rstd", [P, TILES])
        z = lane_sb("z", [P, TILES, P])
        zT = lane_sb("zT", [P, W])
        xnT = lane_sb("xnT", [P, W])
        qT = lane_sb("qT", [P, W])
        kT = lane_sb("kT", [P, W])
        v = lane_sb("v", [P, TILES, P])
        v_one = lane_sb("v_one", [P, TILES, HEADS, DK + 1])
        far = lane_sb("far", [P, HEADS, TILES])
        prob = lane_sb("prob", [P, HEADS, TILES, P])
        probT = lane_sb("probT", [P, HEADS, TILES, P])
        den = lane_sb("den", [P, TILES, HEADS])
        rden = lane_sb("rden", [P, TILES, HEADS])
        hn = lane_sb("hn", [P, TILES, P])
        th = lane_sb("th", [P, TILES, P])
        sw = lane_sb("sw", [P, TILES, P])
        y_out = lane_sb("y_out", [P, TILES, P])
        logit = lane_sb("logit", [P, TILES, EXPERTS])
        top = lane_sb("top", [P, TILES, 8])
        top_i = lane_sb("top_i", [P, TILES, 8], mybir.dt.uint32)
        ediff = lane_sb("ediff", [P, TILES, EXPERTS])
        t_half = lane_sb("t_half", [P, TILES, EXPERTS])
        t_den = lane_sb("t_den", [P, TILES, EXPERTS])
        gate = lane_sb("gate", [P, TILES, EXPERTS])
        gsum = lane_sb("gsum", [P, TILES])

        bank = [[ctx.enter_context(nc.psum_tensor(f"bank{lane}_{b}", [P, W], F32)) for b in range(4)]
                for lane in LANES]

        def tiles_of(t):
            return t[:, :].rearrange("p (t f) -> p t f", t=TILES)

        passed = sem("wait_passed")
        loaded = sem("weights_loaded")
        consts = sem("consts_ready")
        prep_pe = sem("prep_products")
        prep_ev = sem("prep_evacuated")
        prep_dve = sem("prep_vector_steps")
        rows_out = sem("bias_rows_written")
        rows_in = sem("bias_rows_read")

        x_loaded = Signal("x_loaded", 16, gnn0=1, ffn0=1, gnn1=1, ffn1=1)
        adj_loaded = Signal("adj_loaded", 16, gnn0=1, gnn1=1)
        stored = Signal("stored", 16, gnn0=1, ffn0=1, gnn1=1, ffn1=1)
        masked = Signal("mask_ready", gnn0=1, gnn1=2)
        kept = Signal("residual_kept", gnn0=1, gnn1=1)
        ln_stats = Signal("ln_stats", gnn0=4, ffn0=1, gnn1=1, ffn1=1)
        ln_mv = Signal("ln_mean_var", gnn0=4, ffn0=1, gnn1=1, ffn1=1)
        ln_ve = Signal("ln_var_eps", gnn0=4, ffn0=1, gnn1=1, ffn1=1)
        ln_rstd = Signal("ln_rstd", gnn0=4, ffn0=1, gnn1=1, ffn1=1)
        ln_done = Signal("ln_done", gnn0=4, ffn0=1, gnn1=1, ffn1=1)
        z_turned = Signal("z_transposed", gnn0=3, ffn0=1, gnn1=1, ffn1=1)
        zT_ready = Signal("zT_ready", gnn0=3, ffn0=1, gnn1=1, ffn1=1)
        qk_made = Signal("qk_products", gnn0=1, gnn1=2)
        qk_ready = Signal("qk_ready", gnn0=1, gnn1=2)
        v_made = Signal("v_products", gnn0=1, gnn1=1)
        v_ready = Signal("v_ready", gnn0=1, gnn1=1)
        scored = Signal("scores_made", gnn0=1, gnn1=HEADS)
        max_ready = Signal("max_ready", gnn0=1, gnn1=HEADS)
        shifted = Signal("scores_shifted", gnn1=HEADS)
        prob_ready = Signal("prob_ready", gnn0=1, gnn1=HEADS)
        prob_turned = Signal("prob_transposed", gnn0=1, gnn1=HEADS)
        probT_ready = Signal("probT_ready", gnn0=1, gnn1=HEADS)
        mixed = Signal("values_mixed", gnn0=1, gnn1=1)
        rden_ready = Signal("rden_ready", gnn0=1, ffn0=1, gnn1=1, ffn1=1)
        hn_ready = Signal("attention_ready", gnn0=1, gnn1=1)
        o_turned = Signal("attention_transposed", gnn1=1)
        oT_ready = Signal("oT_ready", gnn1=1)
        th_ready = Signal("tanh_ready", gnn0=2)
        sw_ready = Signal("swish_ready", gnn0=2)
        h_made = Signal("linear_made", gnn0=2, gnn1=1)
        scaled = Signal("lnf_scaled", gnn0=1)
        hid_made = Signal("hidden_made", ffn0=C0, ffn1=EXPERTS * C1)
        hid_ready = Signal("hidden_ready", ffn0=C0, ffn1=EXPERTS * C1)
        logits_made = Signal("logits_made", ffn0=1, ffn1=1)
        g_step = Signal("gate_step", ffn0=9, ffn1=9)
        g_tanh = Signal("gate_tanh", ffn0=1, ffn1=1)
        ex_made = Signal("expert_made", ffn0=EXPERTS, ffn1=EXPERTS)
        ex_added = Signal("expert_added", ffn0=EXPERTS, ffn1=EXPERTS)
        y_ready = Signal("y_ready", gnn0=1, gnn1=1)

        weight_loads = [
            (wq0[:, :], w["L0_gnn_Wq"]), (wk0[:, :], w["L0_gnn_Wk"]), (wv0[:, :], w["L0_gnn_Wv"]),
            (w10[:, :], w["L0_gnn_W1"]), (w20[:, :], w["L0_gnn_W2"]),
            (lnf_w[:, :], w["L0_gnn_lnf_w"].rearrange("(a f) -> a f", a=1).to_broadcast((P, P))),
            (lnf_b[:, :], w["L0_gnn_lnf_b"].rearrange("(a f) -> a f", a=1).to_broadcast((P, P))),
            (wq1[:, :], w["L1_gnn_Wq"]), (wk1[:, :], w["L1_gnn_Wk"]), (wv1[:, :], w["L1_gnn_Wv"]),
            (wo1[:, :], w["L1_gnn_Wo"]),
            (rows[R_L0B1:R_L0B1 + C0, :], w["L0_ffn_b1"].rearrange("(c p) -> c p", p=P)),
            (rows[R_L1B1:R_L1B1 + EXPERTS * C1, :], w["L1_ffn_b1"].rearrange("e (c p) -> (e c) p", p=P)),
            (f0_w1[:, :], w["L0_ffn_W1"]),
            (f0_wg[:, :, :], w["L0_ffn_Wg"].rearrange("(c p) e -> p c e", p=P)),
            (f1_w1[:, :, :], w["L1_ffn_W1"].rearrange("e d h -> d e h")),
            (f0_bd[:, :, :], w["L0_ffn_bd"].rearrange("(a e) f -> a e f", a=1)),
            (f1_wg[:, :], w["L1_ffn_gate_w"]),
            (f1_b2[:, :, :], w["L1_ffn_b2"].rearrange("(a e) f -> a e f", a=1)),
        ] + [
            (f0_wd[:, e, :, :], w["L0_ffn_Wd"][e].rearrange("(c p) f -> p c f", p=P)) for e in range(EXPERTS)
        ] + [
            (f1_w2[:, e, :, :], w["L1_ffn_W2"][e].rearrange("(c p) f -> p c f", p=P)) for e in range(EXPERTS)
        ] + [
            (f0_bg[:, t, :], w["L0_ffn_bg"].rearrange("(a e) -> a e", a=1)) for t in range(TILES)
        ] + [
            (f1_bg[:, t, :], w["L1_ffn_gate_b"].rearrange("(a e) -> a e", a=1)) for t in range(TILES)
        ] + [
            (rows[r:r + 1, :], w[n].rearrange("(a p) -> a p", a=1))
            for r, n in ((R_LN1W, "L0_gnn_ln1_w"), (R_LN1B, "L0_gnn_ln1_b"), (R_LN2W, "L0_gnn_ln2_w"),
                         (R_LN2B, "L0_gnn_ln2_b"), (R_BQ, "L1_gnn_bq"), (R_BK, "L1_gnn_bk"), (R_BV, "L1_gnn_bv"),
                         (7, "L1_gnn_bq"), (8, "L1_gnn_bq"), (9, "L1_gnn_bq"))
        ] + [
            (bias_in[:, j, :], w[n].rearrange("(a p) -> a p", a=1))
            for j, n in enumerate(("L0_gnn_b1", "L0_gnn_b2", "L1_gnn_bo"))
        ]
        LOADED = 16 * len(weight_loads)

        block = ctx.enter_context(nc.Block())

        @block.sync
        def _(sp):
            for signal in signals:
                for lane in LANES:
                    sp.sem_inc(signal.sem[lane], signal.step)
            for dst, src in weight_loads:
                sp.dma_start(dst, src).then_inc(loaded, 16)

            sp.wait_ge(prep_dve, PREP_ROWS)
            sp.dma_start(row_parts.rearrange("j b f -> (j b f)").rearrange("(a n) -> a n", a=1),
                         bias_hi[:, :, :, :].rearrange("a j b f -> a (j b f)")).then_inc(rows_out, 16)
            sp.wait_ge(rows_out, 16)
            for b in range(3):
                for t in range(TILES):
                    sp.dma_start(bias3[:, b, t, :], row_parts[:, b, :]).then_inc(rows_in, 16)

            def load(phase, src, i):
                for lane in LANES:
                    sp.wait_ge(ln_done.sem[lane], ln_done.before(phase, i, 0))
                    sp.sem_inc(passed, 1)
                    if phase in ("gnn0", "gnn1"):
                        sp.wait_ge(kept.sem[lane], kept.before(phase, i))
                    else:
                        sp.wait_ge(ex_added.sem[lane], ex_added.before(phase, i, 0))
                    sp.dma_start(x_in[lane][:, :, :], src[i * 2 + lane]).then_inc(x_loaded.sem[lane], 16)
                    if phase not in ("gnn0", "gnn1"):
                        continue
                    sp.wait_ge(masked.sem[lane], masked.before(phase, i, 0))
                    sp.sem_inc(passed, 1)
                    sp.dma_start(adj_in[lane][:, :, :], adj_g[i * 2 + lane]).then_inc(adj_loaded.sem[lane], 16)

            def store(phase, dst, i):
                for lane in LANES:
                    if phase in ("gnn0", "gnn1"):
                        sp.wait_ge(y_ready.sem[lane], y_ready.nth(phase, i))
                    else:
                        sp.wait_ge(ex_added.sem[lane], ex_added.nth(phase, i, EXPERTS - 1))
                    sp.sem_inc(passed, 1)
                    sp.dma_start(dst[i * 2 + lane], y_out[lane][:, :, :]).then_inc(stored.sem[lane], 16)

            for phase, src, dst in (("gnn0", x_g, x1_g), ("ffn0", x1_g, x2_g), ("gnn1", x2_g, x3_g),
                                    ("ffn1", x3_g, out_g)):
                load(phase, src, 0)
                with sp.Fori(1, pairs) as i:
                    load(phase, src, i)
                    store(phase, dst, i - 1)
                store(phase, dst, pairs - 1)
                for lane in LANES:
                    sp.wait_ge(stored.sem[lane], stored.end(phase))

        @block.gpsimd
        def _(pool):
            pool.memset(ident[:, :], 0.0).then_inc(consts, 1)
            pool.memset(off_diag[:, :], 1.0).then_inc(consts, 1)
            pool.memset(far0[:, :, :], 0.0).then_inc(consts, 1)
            pool.memset(far1[:, :], 0.0).then_inc(consts, 1)
            pool.memset(ones3[:, :], 1.0).then_inc(consts, 1)
            pool.memset(ones1[:, :], 1.0).then_inc(consts, 1)
            pool.memset(half_neg[:, :], -0.5).then_inc(consts, 1)
            pool.memset(eps_tile[:, :], EPS).then_inc(consts, 1)
            pool.memset(eps4_tile[:, :], 4 * EPS).then_inc(consts, 1)
            for e in range(EXPERTS):
                pool.memset(iota_e[:, :, e:e + 1], float(e)).then_inc(consts, 1)
            for lane in LANES:
                pool.memset(v_one[lane][:, :, :, DK:DK + 1], 1.0).then_inc(consts, 1)
            pool.wait_ge(consts, 19)
            fills = [(ident[:, :], 1.0), (off_diag[:, :], 0.0), (far1[:, :], -1e30)]
            fills += [(far0[:, j, :], part) for j, part in enumerate(bf16_parts(-1e9))]
            for tile, fill in fills:
                pool.affine_select(out=tile, in_=tile, compare_op=ALU.not_equal, fill=fill, base=0,
                                   pattern=[[-1, P]], channel_multiplier=1).then_inc(consts, 1)

            def rstd_of(phase, i, lane, k, eps):
                pool.wait_ge(ln_mv.sem[lane], ln_mv.nth(phase, i, k))
                pool.tensor_tensor(var_eps[lane][:, :], mv[lane][:, :, 1], eps[:, :], ALU.add)\
                    .then_inc(ln_ve.sem[lane], 1)
                pool.wait_ge(ln_ve.sem[lane], ln_ve.nth(phase, i, k))
                pool.tensor_tensor(rstd[lane][:, :], var_eps[lane][:, :], half_neg[:, :], ALU.pow)\
                    .then_inc(ln_rstd.sem[lane], 1)

            with pool.Fori(0, pairs) as i:
                for lane in LANES:
                    rstd_of("gnn0", i, lane, 0, eps_tile)
                for lane in LANES:
                    pool.wait_ge(adj_loaded.sem[lane], adj_loaded.nth("gnn0", i))
                    pool.wait_ge(scored.sem[lane], scored.before("gnn0", i))
                    pool.sem_inc(passed, 1)
                    pool.tensor_scalar(no_edge[lane][:, :, :], adj_in[lane][:, :, :], 0.0, None, ALU.is_equal)\
                        .then_inc(masked.sem[lane], 1)
                    pool.wait_ge(y_ready.sem[lane], y_ready.before("gnn0", i))
                    pool.tensor_tensor(x_res[lane][:, :, :], x_in[lane][:, :, :],
                                       lnf_b[:, :].unsqueeze(1).to_broadcast((P, TILES, P)), ALU.add)\
                        .then_inc(kept.sem[lane], 1)
                for k in (1, 2, 3):
                    for lane in LANES:
                        rstd_of("gnn0", i, lane, k, eps_tile if k == 3 else eps4_tile)
                for lane in LANES:
                    pool.wait_ge(ln_done.sem[lane], ln_done.nth("gnn0", i, 3))
                    pool.tensor_tensor(hn[lane][:, :, :], z[lane][:, :, :],
                                       lnf_w[:, :].unsqueeze(1).to_broadcast((P, TILES, P)), ALU.mult)\
                        .then_inc(scaled.sem[lane], 1)
                    pool.wait_ge(scaled.sem[lane], scaled.nth("gnn0", i))
                    pool.wait_ge(stored.sem[lane], stored.before("gnn0", i))
                    pool.tensor_tensor(y_out[lane][:, :, :], hn[lane][:, :, :], x_res[lane][:, :, :], ALU.add)\
                        .then_inc(y_ready.sem[lane], 1)

            with pool.Fori(0, pairs) as i:
                for lane in LANES:
                    rstd_of("ffn0", i, lane, 0, eps_tile)

            with pool.Fori(0, pairs) as i:
                for lane in LANES:
                    rstd_of("gnn1", i, lane, 0, eps_tile)
                for lane in LANES:
                    pool.wait_ge(adj_loaded.sem[lane], adj_loaded.nth("gnn1", i))
                    pool.wait_ge(scored.sem[lane], scored.before("gnn1", i, HEADS - 1))
                    pool.sem_inc(passed, 1)
                    pool.tensor_scalar(no_edge[lane][:, :, :], adj_in[lane][:, :, :], 0.0, None, ALU.is_equal)\
                        .then_inc(masked.sem[lane], 1)
                    pool.wait_ge(masked.sem[lane], masked.nth("gnn1", i, 0))
                    pool.tensor_tensor(no_edge1[lane][:, :, :], no_edge[lane][:, :, :],
                                       off_diag[:, :].unsqueeze(1).to_broadcast((P, TILES, P)), ALU.mult)\
                        .then_inc(masked.sem[lane], 1)
                    pool.wait_ge(y_ready.sem[lane], y_ready.before("gnn1", i))
                    pool.sem_inc(passed, 1)
                    pool.tensor_copy(x_res[lane][:, :, :], x_in[lane][:, :, :]).then_inc(kept.sem[lane], 1)

            with pool.Fori(0, pairs) as i:
                for lane in LANES:
                    rstd_of("ffn1", i, lane, 0, eps_tile)

        PREP_T = 6
        @block.tensor
        def _(pe):
            pe.wait_ge(consts, CONSTS)
            pe.wait_ge(loaded, LOADED)
            b0, b1, b2, b3 = (bank[0][k] for k in range(4))
            pe.transpose(b0[:, 0:NCOL], rows[:, :], ident[0:NCOL, 0:NCOL]).then_inc(prep_pe, 1)
            pe.matmul(b1[:, 0:P], wq0[:, :], wk0[:, :], start=True, stop=True).then_inc(prep_pe, 1)
            pe.transpose(b2[:, 0:P], wv0[:, :], ident[:, :])
            pe.transpose(b2[:, P:2 * P], w10[:, :], ident[:, :])
            pe.transpose(b2[:, 2 * P:3 * P], w20[:, :], ident[:, :]).then_inc(prep_pe, 1)
            pe.wait_ge(prep_dve, PREP_COPIED)
            pe.matmul(b3[0:1, 0:P], cols[:, R_LN1B:R_LN1B + 1], w10T[:, :], start=True, stop=True)
            pe.matmul(b3[0:1, P:2 * P], cols[:, R_LN2B:R_LN2B + 1], w20T[:, :], start=True, stop=True)
            pe.matmul(b3[0:1, 2 * P:3 * P], cols[:, R_BV:R_BV + 1], wo1[:, :], start=True, stop=True)\
                .then_inc(prep_pe, 1)
            pe.wait_ge(prep_dve, PREP_END)
            pe.wait_ge(rows_in, 16 * 3 * TILES)

            def turn(phase, i, lane, k, into):
                pe.wait_ge(ln_done.sem[lane], ln_done.nth(phase, i, k))
                for t in range(TILES):
                    last = pe.transpose(into[:, t * P:(t + 1) * P], z[lane][:, t, :], ident[:, :])
                last.then_inc(z_turned.sem[lane], 1)

            def linear(into, lhs, rhs, b):
                pe.matmul(into[:, :], ones3[:, :], bias3[:, b, :, :].rearrange("j t f -> j (t f)"), start=True, stop=False)
                for t in range(TILES):
                    last = pe.matmul(into[:, t * P:(t + 1) * P], lhs[:, t * P:(t + 1) * P], rhs,
                                     start=False, stop=t == TILES - 1)
                return last

            with pe.Fori(0, pairs) as i:
                for lane in LANES:
                    turn("gnn0", i, lane, 0, bank[lane][0])
                for lane in LANES:
                    pe.wait_ge(zT_ready.sem[lane], zT_ready.nth("gnn0", i, 0))
                    pe.matmul(bank[lane][2][:, :], qk0[:, :], xnT[lane][:, :], start=True, stop=True)\
                        .then_inc(qk_made.sem[lane], 1)
                    pe.wait_ge(ln_done.sem[lane], ln_done.before("gnn0", i, 3))
                    for t in range(TILES):
                        last = pe.matmul(bank[lane][1][:, t * P:(t + 1) * P], xnT[lane][:, t * P:(t + 1) * P],
                                         wv0T[:, :], start=True, stop=True)
                    last.then_inc(v_made.sem[lane], 1)
                for lane in LANES:
                    pe.wait_ge(masked.sem[lane], masked.nth("gnn0", i))
                    pe.wait_ge(qk_ready.sem[lane], qk_ready.nth("gnn0", i))
                    for j in range(3):
                        pe.matmul(bank[lane][3][:, :], far0[:, j, :],
                                  no_edge[lane][:, :, :].rearrange("p t f -> p (t f)"), start=j == 0, stop=False)
                    for t in range(TILES):
                        last = pe.matmul(bank[lane][3][:, t * P:(t + 1) * P], qT[lane][:, t * P:(t + 1) * P],
                                         xnT[lane][:, t * P:(t + 1) * P], start=False, stop=t == TILES - 1)
                    last.then_inc(scored.sem[lane], 1)
                for lane in LANES:
                    pe.wait_ge(prob_ready.sem[lane], prob_ready.nth("gnn0", i))
                    for t in range(TILES):
                        last = pe.transpose(bank[lane][0][:, t * P:(t + 1) * P], prob[lane][:, 0, t, :], ident[:, :])
                    last.then_inc(prob_turned.sem[lane], 1)
                for lane in LANES:
                    pe.wait_ge(v_ready.sem[lane], v_ready.nth("gnn0", i))
                    pe.wait_ge(probT_ready.sem[lane], probT_ready.nth("gnn0", i))
                    for t in range(TILES):
                        last = pe.matmul(bank[lane][1][:, t * P:(t + 1) * P], probT[lane][:, 0, t, :],
                                         v[lane][:, t, :], start=True, stop=True)
                    last.then_inc(mixed.sem[lane], 1)
                for k, weights, turned, result in ((1, w10s, 2, 3), (2, w20s, 0, 1)):
                    for lane in LANES:
                        turn("gnn0", i, lane, k, bank[lane][turned])
                    for lane in LANES:
                        pe.wait_ge(zT_ready.sem[lane], zT_ready.nth("gnn0", i, k))
                        linear(bank[lane][result], zT[lane], weights[:, :], k - 1).then_inc(h_made.sem[lane], 1)

            def logits(phase, i, lane, lhs, rhs, bias, chunks):
                into = bank[lane][0][:, 0:TILES * EXPERTS]
                pe.matmul(into, ones1[:, :], bias[:, :, :].rearrange("a t e -> a (t e)"), start=True, stop=False)
                for t in range(TILES):
                    for c in range(chunks):
                        last = pe.matmul(into[:, t * EXPERTS:(t + 1) * EXPERTS], lhs(c, t), rhs(c), start=False,
                                         stop=t == TILES - 1 and c == chunks - 1)
                last.then_inc(logits_made.sem[lane], 1)

            def expert(phase, i, lane, into, e, lhs, rhs, bias, chunks):
                for t in range(TILES):
                    pe.matmul(into[:, t * P:(t + 1) * P], ones1[:, :], bias[:, e, :], start=t == 0, stop=False)
                for t in range(TILES):
                    for c in range(chunks):
                        last = pe.matmul(into[:, t * P:(t + 1) * P], lhs(c, t), rhs(c), start=False,
                                         stop=t == TILES - 1 and c == chunks - 1)
                last.then_inc(ex_made.sem[lane], 1)

            for lane in LANES:
                pe.wait_ge(ln_done.sem[lane], ln_done.end("gnn0"))
            with pe.Fori(0, pairs) as i:
                for lane in LANES:
                    pe.wait_ge(ex_added.sem[lane], ex_added.before("ffn0", i, EXPERTS - 1))
                    turn("ffn0", i, lane, 0, bank[lane][3])
                for c in range(C0):
                    for lane in LANES:
                        pe.wait_ge(zT_ready.sem[lane], zT_ready.nth("ffn0", i, 0))
                        pe.matmul(bank[lane][c][:, :], f0_w1[:, c * P:(c + 1) * P], xnT[lane][:, :],
                                  start=True, stop=True).then_inc(hid_made.sem[lane], 1)
                for lane in LANES:
                    pe.wait_ge(hid_ready.sem[lane], hid_ready.nth("ffn0", i, C0 - 1))
                    logits("ffn0", i, lane, lambda c, t: prob[lane][:, c, t, :], lambda c: f0_wg[:, c, :], f0_bg, C0)
                for e in range(EXPERTS):
                    for lane in LANES:
                        if e >= 2:
                            pe.wait_ge(ex_added.sem[lane], ex_added.nth("ffn0", i, e - 2))
                        expert("ffn0", i, lane, bank[lane][1 + e % 2], e, lambda c, t: prob[lane][:, c, t, :],
                               lambda c: f0_wd[:, e, c, :], f0_bd, C0)

            for lane in LANES:
                pe.wait_ge(ex_added.sem[lane], ex_added.end("ffn0"))
            with pe.Fori(0, pairs) as i:
                for lane in LANES:
                    turn("gnn1", i, lane, 0, bank[lane][0])
                for lane in LANES:
                    pe.wait_ge(zT_ready.sem[lane], zT_ready.nth("gnn1", i, 0))
                    pe.matmul(bank[lane][1][:, :], wq1[:, :], xnT[lane][:, :], start=True, stop=True)\
                        .then_inc(qk_made.sem[lane], 1)
                    pe.matmul(bank[lane][2][:, :], wk1[:, :], xnT[lane][:, :], start=True, stop=True)\
                        .then_inc(qk_made.sem[lane], 1)
                    pe.wait_ge(y_ready.sem[lane], y_ready.before("gnn1", i))
                    for t in range(TILES):
                        last = pe.matmul(bank[lane][3][:, t * P:(t + 1) * P], xnT[lane][:, t * P:(t + 1) * P],
                                         wv1[:, :], start=True, stop=True)
                    last.then_inc(v_made.sem[lane], 1)
                for lane in LANES:
                    pe.wait_ge(masked.sem[lane], masked.nth("gnn1", i, 1))
                    pe.wait_ge(qk_ready.sem[lane], qk_ready.nth("gnn1", i, 1))
                    pe.wait_ge(v_ready.sem[lane], v_ready.nth("gnn1", i))
                    for h in range(HEADS):
                        pe.matmul(bank[lane][h][:, :], far1[:, :],
                                  no_edge1[lane][:, :, :].rearrange("p t f -> p (t f)"), start=True, stop=False)
                    for t in range(TILES):
                        for h in range(HEADS):
                            head = slice(h * DK, (h + 1) * DK)
                            last = pe.matmul(bank[lane][h][:, t * P:(t + 1) * P], qT[lane][head, t * P:(t + 1) * P],
                                             kT[lane][head, t * P:(t + 1) * P], start=False, stop=t == TILES - 1)
                            if t == TILES - 1:
                                last.then_inc(scored.sem[lane], 1)
                for h in range(HEADS):
                    for lane in LANES:
                        pe.wait_ge(prob_ready.sem[lane], prob_ready.nth("gnn1", i, h))
                        for t in range(TILES):
                            last = pe.transpose(bank[lane][h][:, t * P:(t + 1) * P], prob[lane][:, h, t, :], ident[:, :])
                        last.then_inc(prob_turned.sem[lane], 1)
                for lane in LANES:
                    pe.wait_ge(probT_ready.sem[lane], probT_ready.nth("gnn1", i, HEADS - 1))
                    for t in range(TILES):
                        part = bank[lane][t // 2][:, 0:2 * HEADS * (DK + 1)]\
                            .rearrange("p (t h d) -> p t h d", t=2, h=HEADS)
                        for h in range(HEADS):
                            last = pe.matmul(part[:, t % 2, h, :], probT[lane][:, h, t, :], v_one[lane][:, t, h, :],
                                             start=True, stop=True)
                    last.then_inc(mixed.sem[lane], 1)
                for lane in LANES:
                    pe.wait_ge(hn_ready.sem[lane], hn_ready.nth("gnn1", i))
                    for t in range(TILES):
                        last = pe.transpose(bank[lane][2][:, t * P:(t + 1) * P], hn[lane][:, t, :], ident[:, :])
                    last.then_inc(o_turned.sem[lane], 1)
                for lane in LANES:
                    pe.wait_ge(oT_ready.sem[lane], oT_ready.nth("gnn1", i))
                    linear(bank[lane][3], zT[lane], wo1[:, :], 2).then_inc(h_made.sem[lane], 1)

            for lane in LANES:
                pe.wait_ge(y_ready.sem[lane], y_ready.end("gnn1"))
            with pe.Fori(0, pairs) as i:
                for lane in LANES:
                    pe.wait_ge(ex_added.sem[lane], ex_added.before("ffn1", i, EXPERTS - 1))
                    turn("ffn1", i, lane, 0, bank[lane][3])
                for lane in LANES:
                    pe.wait_ge(zT_ready.sem[lane], zT_ready.nth("ffn1", i, 0))
                    logits("ffn1", i, lane, lambda c, t: xnT[lane][:, t * P:(t + 1) * P], lambda c: f1_wg[:, :], f1_bg, 1)
                for e in range(EXPERTS):
                    for lane in LANES:
                        if e:
                            pe.wait_ge(hid_ready.sem[lane], hid_ready.nth("ffn1", i, e * C1 - 1))
                        for c in range(C1):
                            pe.matmul(bank[lane][2 + c][:, :], f1_w1[:, e, c * P:(c + 1) * P], xnT[lane][:, :],
                                      start=True, stop=True).then_inc(hid_made.sem[lane], 1)
                    for lane in LANES:
                        pe.wait_ge(hid_ready.sem[lane], hid_ready.nth("ffn1", i, e * C1 + C1 - 1))
                        if e >= 2:
                            pe.wait_ge(ex_added.sem[lane], ex_added.nth("ffn1", i, e - 2))
                        elif e == 0:
                            pe.wait_ge(g_step.sem[lane], g_step.nth("ffn1", i, 0))
                        expert("ffn1", i, lane, bank[lane][e % 2], e, lambda c, t: prob[lane][:, 2 * (e % 2) + c, t, :],
                               lambda c: f1_w2[:, e, c, :], f1_b2, C1)

        @block.scalar
        def _(act):
            def copy_turned(phase, i, lane, k, src, dst):
                act.wait_ge(z_turned.sem[lane], z_turned.nth(phase, i, k))
                act.activation(dst[:, :], src[:, :], ACT.Copy).then_inc(zT_ready.sem[lane], 1)

            act.preload_act_table(ACT.Exp)
            with act.Fori(0, pairs) as i:
                for lane in LANES:
                    copy_turned("gnn0", i, lane, 0, bank[lane][0], xnT[lane])
                for lane in LANES:
                    act.wait_ge(qk_made.sem[lane], qk_made.nth("gnn0", i))
                    act.activation(qT[lane][:, :], bank[lane][2][:, :], ACT.Copy).then_inc(qk_ready.sem[lane], 1)
                for lane in LANES:
                    act.wait_ge(max_ready.sem[lane], max_ready.nth("gnn0", i))
                    for t in range(TILES):
                        last = act.activation(prob[lane][:, 0, t, :], bank[lane][3][:, t * P:(t + 1) * P], ACT.Exp,
                                              bias=far[lane][:, 0, t:t + 1], accum_out=den[lane][:, t, 0:1])
                    last.then_inc(prob_ready.sem[lane], 1)
                for lane in LANES:
                    act.wait_ge(prob_turned.sem[lane], prob_turned.nth("gnn0", i))
                    act.activation(probT[lane][:, 0, :, :].rearrange("p t f -> p (t f)"), bank[lane][0][:, :],
                                   ACT.Copy).then_inc(probT_ready.sem[lane], 1)
                for lane in LANES:
                    act.wait_ge(hn_ready.sem[lane], hn_ready.nth("gnn0", i))
                    act.activation(th[lane][:, :, :], hn[lane][:, :, :], ACT.Tanh, scale=0.5)\
                        .then_inc(th_ready.sem[lane], 1)
                for lane in LANES:
                    copy_turned("gnn0", i, lane, 1, bank[lane][2], zT[lane])
                for lane in LANES:
                    act.wait_ge(h_made.sem[lane], h_made.nth("gnn0", i, 0))
                    act.activation(th[lane][:, :, :], tiles_of(bank[lane][3]), ACT.Tanh, scale=0.5)\
                        .then_inc(th_ready.sem[lane], 1)
                for lane in LANES:
                    copy_turned("gnn0", i, lane, 2, bank[lane][0], zT[lane])

            act.preload_act_table(ACT.Gelu)
            with act.Fori(0, pairs) as i:
                for lane in LANES:
                    copy_turned("ffn0", i, lane, 0, bank[lane][3], xnT[lane])
                for c in range(C0):
                    for lane in LANES:
                        act.wait_ge(hid_made.sem[lane], hid_made.nth("ffn0", i, c))
                        act.activation(prob[lane][:, c, :, :], tiles_of(bank[lane][c]), ACT.Gelu,
                                       bias=cols[:, R_L0B1 + c:R_L0B1 + c + 1]).then_inc(hid_ready.sem[lane], 1)
                for lane in LANES:
                    act.wait_ge(g_step.sem[lane], g_step.nth("ffn0", i, 2))
                    act.activation(t_half[lane][:, :, :], ediff[lane][:, :, :], ACT.Tanh, scale=0.5)\
                        .then_inc(g_tanh.sem[lane], 1)

            act.preload_act_table(ACT.Exp)
            with act.Fori(0, pairs) as i:
                for lane in LANES:
                    copy_turned("gnn1", i, lane, 0, bank[lane][0], xnT[lane])
                for lane in LANES:
                    act.wait_ge(qk_made.sem[lane], qk_made.nth("gnn1", i, 0))
                    act.activation(qT[lane][:, :], bank[lane][1][:, :], ACT.Identity, bias=bq_s[:, :], scale=QK_SCALE)\
                        .then_inc(qk_ready.sem[lane], 1)
                    act.wait_ge(qk_made.sem[lane], qk_made.nth("gnn1", i, 1))
                    act.activation(kT[lane][:, :], bank[lane][2][:, :], ACT.Identity, bias=cols[:, R_BK:R_BK + 1])\
                        .then_inc(qk_ready.sem[lane], 1)
                for h in range(HEADS):
                    for lane in LANES:
                        act.wait_ge(shifted.sem[lane], shifted.nth("gnn1", i, h))
                        act.activation(prob[lane][:, h, :, :], prob[lane][:, h, :, :], ACT.Exp)\
                            .then_inc(prob_ready.sem[lane], 1)
                for h in range(HEADS):
                    for lane in LANES:
                        act.wait_ge(prob_turned.sem[lane], prob_turned.nth("gnn1", i, h))
                        act.activation(probT[lane][:, h, :, :].rearrange("p t f -> p (t f)"), bank[lane][h][:, :],
                                       ACT.Copy).then_inc(probT_ready.sem[lane], 1)
                for lane in LANES:
                    act.wait_ge(o_turned.sem[lane], o_turned.nth("gnn1", i))
                    act.activation(zT[lane][:, :], bank[lane][2][:, :], ACT.Copy).then_inc(oT_ready.sem[lane], 1)

            act.preload_act_table(ACT.Gelu)
            with act.Fori(0, pairs) as i:
                for lane in LANES:
                    copy_turned("ffn1", i, lane, 0, bank[lane][3], xnT[lane])
                for lane in LANES:
                    act.wait_ge(g_step.sem[lane], g_step.nth("ffn1", i, 2))
                    act.activation(t_half[lane][:, :, :], ediff[lane][:, :, :], ACT.Tanh, scale=0.5)\
                        .then_inc(g_tanh.sem[lane], 1)
                for e in range(EXPERTS):
                    for lane in LANES:
                        if e >= 2:
                            act.wait_ge(ex_made.sem[lane], ex_made.nth("ffn1", i, e - 2))
                        for c in range(C1):
                            act.wait_ge(hid_made.sem[lane], hid_made.nth("ffn1", i, e * C1 + c))
                            r = R_L1B1 + e * C1 + c
                            act.activation(prob[lane][:, 2 * (e % 2) + c, :, :], tiles_of(bank[lane][2 + c]), ACT.Gelu,
                                           bias=cols[:, r:r + 1]).then_inc(hid_ready.sem[lane], 1)

        @block.vector
        def _(dve):
            count = [0]

            def step(ins):
                count[0] += 1
                ins.then_inc(prep_dve, 1)
                dve.wait_ge(prep_dve, count[0])

            dve.wait_ge(prep_pe, 3)
            step(dve.tensor_copy(cols[:, :], bank[0][0][:, 0:NCOL]))
            step(dve.tensor_scalar(qk0[:, :], bank[0][1][:, 0:P], 1.0 / math.sqrt(P), None, ALU.mult))
            step(dve.tensor_copy(wv0T[:, :], bank[0][2][:, 0:P]))
            step(dve.tensor_copy(w10T[:, :], bank[0][2][:, P:2 * P]))
            step(dve.tensor_copy(w20T[:, :], bank[0][2][:, 2 * P:3 * P]))
            assert count[0] == PREP_COPIED
            step(dve.tensor_scalar(w10s[:, :], w10T[:, :], cols[:, R_LN1W:R_LN1W + 1], None, ALU.mult))
            step(dve.tensor_scalar(w20s[:, :], w20T[:, :], cols[:, R_LN2W:R_LN2W + 1], None, ALU.mult))
            step(dve.tensor_scalar(bq_s[:, :], cols[:, R_BQ:R_BQ + 1], QK_SCALE, None, ALU.mult))
            dve.wait_ge(prep_pe, 4)
            step(dve.tensor_tensor(bias_row[:, :, :], bank[0][3][0:1, 0:3 * P].rearrange("a (b f) -> a b f", b=3),
                                   bias_in[:, :, :], ALU.add))
            step(dve.tensor_copy(bias_hi[:, 0, :, :], bias_row[:, :, :]))
            step(dve.tensor_tensor(bias_rest[:, :, :], bias_row[:, :, :], bias_hi[:, 0, :, :], ALU.subtract))
            step(dve.tensor_copy(bias_hi[:, 1, :, :], bias_rest[:, :, :]))
            step(dve.tensor_tensor(bias_rest2[:, :, :], bias_rest[:, :, :], bias_hi[:, 1, :, :], ALU.subtract))
            step(dve.tensor_copy(bias_hi[:, 2, :, :], bias_rest2[:, :, :]))
            assert count[0] == PREP_ROWS == PREP_END

            def norm_stats(phase, i, lane, k, src):
                for t in range(TILES):
                    last = dve.bn_stats(bn[lane][:, t, :], src(t))
                last.then_inc(ln_stats.sem[lane], 1)

            def norm_aggregate(phase, i, lane, k):
                dve.wait_ge(ln_stats.sem[lane], ln_stats.nth(phase, i, k))
                dve.sem_inc(passed, 1)
                for t in range(TILES):
                    last = dve.bn_aggr(mv[lane][:, t, :], bn[lane][:, t, :])
                last.then_inc(ln_mv.sem[lane], 1)

            def norm_apply(phase, i, lane, k, src):
                dve.wait_ge(ln_rstd.sem[lane], ln_rstd.nth(phase, i, k))
                for t in range(TILES):
                    last = dve.tensor_scalar(z[lane][:, t, :], src(t), mv[lane][:, t, 0:1], rstd[lane][:, t:t + 1],
                                             ALU.subtract, ALU.mult)
                last.then_inc(ln_done.sem[lane], 1)

            def norm(phase, i, k, src, ready=None):
                for lane in LANES:
                    if ready:
                        dve.wait_ge(ready.sem[lane], ready.nth(phase, i, k - 1))
                    norm_stats(phase, i, lane, k, lambda t: src(lane, t))
                for lane in LANES:
                    norm_aggregate(phase, i, lane, k)
                for lane in LANES:
                    norm_apply(phase, i, lane, k, lambda t: src(lane, t))

            with dve.Fori(0, pairs) as i:
                for lane in LANES:
                    dve.wait_ge(x_loaded.sem[lane], x_loaded.nth("gnn0", i))
                    dve.wait_ge(scaled.sem[lane], scaled.before("gnn0", i))
                norm("gnn0", i, 0, lambda lane, t: x_in[lane][:, t, :])
                for lane in LANES:
                    dve.wait_ge(v_made.sem[lane], v_made.nth("gnn0", i))
                    dve.tensor_copy(v[lane][:, :, :], tiles_of(bank[lane][1])).then_inc(v_ready.sem[lane], 1)
                for lane in LANES:
                    dve.wait_ge(scored.sem[lane], scored.nth("gnn0", i))
                    dve.tensor_reduce(far[lane][:, 0, :], tiles_of(bank[lane][3]), AX.X, ALU.max, negate=True)\
                        .then_inc(max_ready.sem[lane], 1)
                for lane in LANES:
                    dve.wait_ge(prob_ready.sem[lane], prob_ready.nth("gnn0", i))
                    dve.reciprocal(rden[lane][:, :, 0], den[lane][:, :, 0]).then_inc(rden_ready.sem[lane], 1)
                for lane in LANES:
                    dve.wait_ge(mixed.sem[lane], mixed.nth("gnn0", i))
                    dve.wait_ge(rden_ready.sem[lane], rden_ready.nth("gnn0", i))
                    dve.wait_ge(y_ready.sem[lane], y_ready.before("gnn0", i))
                    dve.tensor_tensor(hn[lane][:, :, :], tiles_of(bank[lane][1]),
                                      rden[lane][:, :, 0:1].to_broadcast((P, TILES, P)), ALU.mult)\
                        .then_inc(hn_ready.sem[lane], 1)
                for lane in LANES:
                    dve.wait_ge(th_ready.sem[lane], th_ready.nth("gnn0", i, 0))
                    dve.scalar_tensor_tensor(sw[lane][:, :, :], th[lane][:, :, :], 1.0, hn[lane][:, :, :],
                                             ALU.add, ALU.mult).then_inc(sw_ready.sem[lane], 1)
                norm("gnn0", i, 1, lambda lane, t: sw[lane][:, t, :], sw_ready)
                for lane in LANES:
                    dve.wait_ge(th_ready.sem[lane], th_ready.nth("gnn0", i, 1))
                    dve.scalar_tensor_tensor(sw[lane][:, :, :], th[lane][:, :, :], 1.0, tiles_of(bank[lane][3]),
                                             ALU.add, ALU.mult).then_inc(sw_ready.sem[lane], 1)
                norm("gnn0", i, 2, lambda lane, t: sw[lane][:, t, :], sw_ready)
                for lane in LANES:
                    dve.wait_ge(h_made.sem[lane], h_made.nth("gnn0", i, 1))
                norm("gnn0", i, 3, lambda lane, t: bank[lane][1][:, t * P:(t + 1) * P])

            def gating(phase, i, chosen):
                def after(lane, k):
                    dve.wait_ge(g_step.sem[lane], g_step.nth(phase, i, k))
                    dve.sem_inc(passed, 1)

                for lane in LANES:
                    dve.wait_ge(logits_made.sem[lane], logits_made.nth(phase, i))
                    dve.tensor_copy(logit[lane][:, :, :], bank[lane][0][:, 0:TILES * EXPERTS]
                                    .rearrange("p (t e) -> p t e", t=TILES)).then_inc(g_step.sem[lane], 1)
                for lane in LANES:
                    after(lane, 0)
                    for t in range(TILES):
                        last = dve.max(top[lane][:, t, :], logit[lane][:, t, :])
                    last.then_inc(g_step.sem[lane], 1)
                for lane in LANES:
                    after(lane, 1)
                    dve.tensor_tensor(ediff[lane][:, :, :], logit[lane][:, :, :],
                                      top[lane][:, :, 0:1].to_broadcast((P, TILES, EXPERTS)), ALU.subtract)\
                        .then_inc(g_step.sem[lane], 1)
                    for t in range(TILES):
                        last = dve.max_index(top_i[lane][:, t, :], top[lane][:, t, :], logit[lane][:, t, :])
                    last.then_inc(g_step.sem[lane], 1)
                for lane in LANES:
                    after(lane, 3)
                    dve.tensor_tensor(gate[lane][:, :, :], iota_e[:, :, :],
                                      top_i[lane][:, :, 0:1].to_broadcast((P, TILES, EXPERTS)), ALU.is_equal)
                    if chosen == 2:
                        dve.tensor_tensor(logit[lane][:, :, :], iota_e[:, :, :],
                                          top_i[lane][:, :, 1:2].to_broadcast((P, TILES, EXPERTS)), ALU.is_equal)
                    dve.wait_ge(g_tanh.sem[lane], g_tanh.nth(phase, i))
                    dve.sem_inc(passed, 1)
                    dve.tensor_scalar(t_den[lane][:, :, :], t_half[lane][:, :, :], -1.0, 1.0, ALU.mult, ALU.add)\
                        .then_inc(g_step.sem[lane], 1)
                for lane in LANES:
                    after(lane, 4)
                    if chosen == 2:
                        dve.tensor_tensor(gate[lane][:, :, :], gate[lane][:, :, :], logit[lane][:, :, :], ALU.add)
                    dve.reciprocal(t_den[lane][:, :, :], t_den[lane][:, :, :]).then_inc(g_step.sem[lane], 1)
                for lane in LANES:
                    after(lane, 5)
                    dve.scalar_tensor_tensor(ediff[lane][:, :, :], t_half[lane][:, :, :], 1.0, t_den[lane][:, :, :],
                                             ALU.add, ALU.mult).then_inc(g_step.sem[lane], 1)
                for lane in LANES:
                    after(lane, 6)
                    dve.tensor_reduce(gsum[lane][:, :], ediff[lane][:, :, :], AX.X, ALU.add)
                    dve.tensor_tensor(gate[lane][:, :, :], gate[lane][:, :, :], ediff[lane][:, :, :], ALU.mult)\
                        .then_inc(g_step.sem[lane], 1)
                for lane in LANES:
                    after(lane, 7)
                    dve.reciprocal(gsum[lane][:, :], gsum[lane][:, :]).then_inc(g_step.sem[lane], 1)

            def experts(phase, i, banks):
                for lane in LANES:
                    dve.wait_ge(g_step.sem[lane], g_step.nth(phase, i, 8))
                    dve.sem_inc(passed, 1)
                    dve.tensor_tensor(gate[lane][:, :, :], gate[lane][:, :, :],
                                      gsum[lane][:, :].unsqueeze(2).to_broadcast((P, TILES, EXPERTS)), ALU.mult)\
                        .then_inc(rden_ready.sem[lane], 1)
                for lane in LANES:
                    dve.wait_ge(stored.sem[lane], stored.before(phase, i))
                for e in range(EXPERTS):
                    for lane in LANES:
                        dve.wait_ge(ex_made.sem[lane], ex_made.nth(phase, i, e))
                        if e:
                            dve.wait_ge(ex_added.sem[lane], ex_added.nth(phase, i, e - 1))
                        else:
                            dve.wait_ge(rden_ready.sem[lane], rden_ready.nth(phase, i))
                        for t in range(TILES):
                            last = dve.scalar_tensor_tensor(
                                y_out[lane][:, t, :], bank[lane][banks(e)][:, t * P:(t + 1) * P], gate[lane][:, t, e:e + 1],
                                (y_out if e else x_in)[lane][:, t, :], ALU.mult, ALU.add)
                        last.then_inc(ex_added.sem[lane], 1)

            with dve.Fori(0, pairs) as i:
                for lane in LANES:
                    dve.wait_ge(x_loaded.sem[lane], x_loaded.nth("ffn0", i))
                norm("ffn0", i, 0, lambda lane, t: x_in[lane][:, t, :])
                gating("ffn0", i, 1)
                experts("ffn0", i, lambda e: 1 + e % 2)

            with dve.Fori(0, pairs) as i:
                for lane in LANES:
                    dve.wait_ge(x_loaded.sem[lane], x_loaded.nth("gnn1", i))
                norm("gnn1", i, 0, lambda lane, t: x_in[lane][:, t, :])
                for lane in LANES:
                    dve.wait_ge(v_made.sem[lane], v_made.nth("gnn1", i))
                    dve.tensor_copy(v_one[lane][:, :, :, 0:DK],
                                    bank[lane][3][:, :].rearrange("p (t h d) -> p t h d", t=TILES, h=HEADS))\
                        .then_inc(v_ready.sem[lane], 1)
                for h in range(HEADS):
                    for lane in LANES:
                        dve.wait_ge(scored.sem[lane], scored.nth("gnn1", i, h))
                        dve.tensor_reduce(far[lane][:, h, :], tiles_of(bank[lane][h]), AX.X, ALU.max)\
                            .then_inc(max_ready.sem[lane], 1)
                    for lane in LANES:
                        dve.wait_ge(max_ready.sem[lane], max_ready.nth("gnn1", i, h))
                        dve.tensor_tensor(prob[lane][:, h, :, :], tiles_of(bank[lane][h]),
                                          far[lane][:, h, :].unsqueeze(2).to_broadcast((P, TILES, P)), ALU.subtract)\
                            .then_inc(shifted.sem[lane], 1)
                for lane in LANES:
                    dve.wait_ge(mixed.sem[lane], mixed.nth("gnn1", i))
                    for half in range(2):
                        part = bank[lane][half][:, 0:2 * HEADS * (DK + 1)].rearrange("p (t h d) -> p t h d", t=2, h=HEADS)
                        last = dve.reciprocal(rden[lane][:, 2 * half:2 * half + 2, :], part[:, :, :, DK])
                    last.then_inc(rden_ready.sem[lane], 1)
                for lane in LANES:
                    dve.wait_ge(rden_ready.sem[lane], rden_ready.nth("gnn1", i))
                    for half in range(2):
                        part = bank[lane][half][:, 0:2 * HEADS * (DK + 1)].rearrange("p (t h d) -> p (t h) d", t=2, h=HEADS)
                        last = dve.tensor_tensor(
                            hn[lane][:, 2 * half:2 * half + 2, :].rearrange("p t (h d) -> p (t h) d", h=HEADS),
                            part[:, :, 0:DK],
                            rden[lane][:, 2 * half:2 * half + 2, :].rearrange("p t h -> p (t h)").unsqueeze(2)
                            .to_broadcast((P, 2 * HEADS, DK)), ALU.mult)
                    last.then_inc(hn_ready.sem[lane], 1)
                for lane in LANES:
                    dve.wait_ge(h_made.sem[lane], h_made.nth("gnn1", i))
                    dve.wait_ge(kept.sem[lane], kept.nth("gnn1", i))
                    dve.wait_ge(stored.sem[lane], stored.before("gnn1", i))
                    dve.scalar_tensor_tensor(y_out[lane][:, :, :], tiles_of(bank[lane][3]), 0.0, x_res[lane][:, :, :],
                                             ALU.max, ALU.add).then_inc(y_ready.sem[lane], 1)

            with dve.Fori(0, pairs) as i:
                for lane in LANES:
                    dve.wait_ge(x_loaded.sem[lane], x_loaded.nth("ffn1", i))
                norm("ffn1", i, 0, lambda lane, t: x_in[lane][:, t, :])
                gating("ffn1", i, 2)
                experts("ffn1", i, lambda e: e % 2)



CONSTS = 25
PREP_COPIED = 5
PREP_ROWS = 14
PREP_END = 14


def bf16_parts(value):
    import numpy as np
    parts, rest = [], np.float32(value)
    for _ in range(3):
        part = ((rest.view(np.uint32) & np.uint32(0xFFFF0000))).view(np.float32)
        parts.append(float(part))
        rest = np.float32(rest - part)
    return parts


def kernel(**inputs):
    import numpy as np
    import concourse.bacc as bacc
    from concourse.bass_utils import run_bass_kernel_spmd

    nc = bacc.Bacc("TRN2", target_bir_lowering=False, num_devices=1)
    arrays, aps = {}, {}
    for name in ["x", "adj"] + WEIGHTS:
        a = np.ascontiguousarray(inputs[name])
        arrays[f"in_{name}"] = a
        aps[name] = nc.dram_tensor(f"in_{name}", a.shape, mybir.dt.from_np(a.dtype), kind="ExternalInput").ap()
    out = nc.dram_tensor("out", inputs["x"].shape, F32, kind="ExternalOutput").ap()
    build(nc, aps["x"], aps["adj"], {n: aps[n] for n in WEIGHTS}, out)
    r = run_bass_kernel_spmd(nc, [arrays], core_ids=[0])
    return r.results[0]["out"]
```

```python
import math
from contextlib import ExitStack

import concourse.bass as bass
from concourse import mybir

F32 = mybir.dt.float32
BF16 = mybir.dt.bfloat16
I32 = mybir.dt.int32
U32 = mybir.dt.uint32
ALU = mybir.AluOpType
ACT = mybir.ActivationFunctionType
AX = mybir.AxisListType

P = 128
TILES = 4
W = TILES * P
NL = 4
LANES = range(NL)
NR = 3
ROUNDS = range(NR)
EPS = 1e-5
EXPERTS = 8
HID = 512
C = HID // P
HALF = HID // 2
HEADS = 4
DK = P // HEADS
QK_SCALE = 1.0 / math.sqrt(DK + 1e-09)
ROW = P + 4
MEAN, RSTD, G0, G1 = P, P + 1, P + 2, P + 3
CLASSES = {"gnn0": EXPERTS, "gnn1": EXPERTS * EXPERTS}
USED = {"gnn0": EXPERTS, "gnn1": EXPERTS * (EXPERTS - 1) // 2}

WEIGHTS = [
    "L0_gnn_Wq", "L0_gnn_Wk", "L0_gnn_Wv", "L0_gnn_ln1_w", "L0_gnn_ln1_b", "L0_gnn_W1", "L0_gnn_b1",
    "L0_gnn_ln2_w", "L0_gnn_ln2_b", "L0_gnn_W2", "L0_gnn_b2", "L0_gnn_lnf_w", "L0_gnn_lnf_b",
    "L0_ffn_W1", "L0_ffn_b1", "L0_ffn_Wg", "L0_ffn_bg", "L0_ffn_Wd", "L0_ffn_bd",
    "L1_gnn_Wq", "L1_gnn_bq", "L1_gnn_Wk", "L1_gnn_bk", "L1_gnn_Wv", "L1_gnn_bv", "L1_gnn_Wo", "L1_gnn_bo",
    "L1_ffn_gate_w", "L1_ffn_gate_b", "L1_ffn_W1", "L1_ffn_b1", "L1_ffn_W2", "L1_ffn_b2",
]

RANKING = ("rank_all", "base", "rank_own", "rank", "slot")
GATE0 = ("logit", "top", "diff", "index", "class", "inv", "onehot", "recip", "ex", "sum", "weights") + RANKING
GATE1 = ("logit", "top", "diff", "index", "idx", "inv", "pair", "class", "onehot", "recip", "ex", "sum", "p0", "p1",
         "pdiff", "swap", "weights") + RANKING
EVENTS = {
    "x_loaded": dict(gnn0=("x",), exp0=("ids0", "ids1", "ids2"), gnn1=("x",), exp1=("ids0", "ids1", "ids2")),
    "adj_loaded": dict(gnn0=("adj",), gnn1=("adj",)),
    "stored": dict(gnn0=("y",), gnn1=("y",)),
    "transposed": dict(gnn0=("xn", "prob", "z1", "z2", "gate"), exp0=("z0", "z1", "z2"),
                       gnn1=("xn", "prob0", "prob1", "prob2", "prob3", "o", "gate"), exp1=("z0", "z1", "z2")),
    "copied": dict(gnn0=("xn", "prob", "z1", "z2", "gate"), exp0=("z0", "z1", "z2"),
                   gnn1=("xn", "prob0", "prob1", "prob2", "prob3", "o", "gate"), exp1=("z0", "z1", "z2")),
    "product": dict(gnn0=("qk", "v", "scores", "mixed", "h1", "h2", "hid0", "hid1", "hid2", "hid3", "logits", "ranks"),
                    exp0=("hid0", "y0", "hid1", "y1", "hid2", "y2"),
                    gnn1=("q", "k", "v", "scores0", "scores1", "scores2", "scores3", "mixed", "h", "logits", "ranks"),
                    exp1=("hid0", "y0", "hid1", "y1", "hid2", "y2")),
    "activated": dict(gnn0=("qk", "prob", "th0", "th1", "hid0", "hid1", "hid2", "hid3", "gate"),
                      exp0=("hid0", "hid1", "hid2"),
                      gnn1=("q", "k", "prob0", "prob1", "prob2", "prob3", "gate"), exp1=("up0", "hid0", "up1", "hid1", "up2", "hid2")),
    "stats": dict(gnn0=("0", "1", "2", "3", "gate"), gnn1=("0", "gate")),
    "mean_var": dict(gnn0=("0", "1", "2", "3", "gate"), gnn1=("0", "gate")),
    "var_eps": dict(gnn0=("0", "1", "2", "3", "gate"), gnn1=("0", "gate")),
    "rstd": dict(gnn0=("0", "1", "2", "3", "gate"), gnn1=("0", "gate")),
    "normed": dict(gnn0=("0", "1", "2", "3", "gate"), exp0=("z0", "z1", "z2"), gnn1=("0", "gate"),
                   exp1=("z0", "z1", "z2")),
    "pooled": dict(gnn0=("mask", "kept", "scaled", "y", "numbered"), gnn1=("mask", "mask_self", "numbered")),
    "vector": dict(gnn0=("v", "max", "rden", "hn", "sw0", "sw1") + GATE0,
                   exp0=("out0", "out1", "out2"),
                   gnn1=("v", "max0", "shift0", "max1", "shift1", "max2", "shift2", "max3", "shift3", "rden", "hn", "y")
                   + GATE1,
                   exp1=("part0", "out0", "part1", "out1", "part2", "out2")),
}
PHASES = ("gnn0", "exp0", "gnn1", "exp1")

STAGES = {
    "gnn0": ("ln0_stats", "ln0_rstd", "ln0_apply", "xn_turn", "xn_copy", "qk_v", "qk_v_copy", "scores", "max", "prob",
             "prob_turn", "prob_copy", "mix", "attention", "tanh1", "swish1", "ln1_rstd", "ln1_apply", "z1_turn",
             "z1_copy", "linear1", "tanh2", "swish2", "ln2_rstd", "ln2_apply", "z2_turn", "z2_copy", "linear2",
             "ln3_stats", "ln3_rstd", "ln3_apply", "residual", "gate_stats", "gate_rstd", "gate_apply", "gate_turn",
             "gate_copy", "hidden01", "gelu01", "hidden23", "gelu23", "logits", "pick", "gate_tanh", "weigh", "ranks",
             "slots", "scatter", "number"),
    "gnn1": ("ln0_stats", "ln0_rstd", "ln0_apply", "xn_turn", "xn_copy", "qk", "qk_copy", "values", "v_copy",
             "scores01", "shift01", "prob01", "scores23", "shift23", "prob23", "prob_turn01", "prob_copy01",
             "prob_turn23", "prob_copy23", "mix", "attention", "o_turn", "o_copy", "linear", "residual", "gate_rstd",
             "gate_apply", "gate_turn", "gate_copy", "logits", "pick", "gate_tanh", "weigh", "ranks", "slots",
             "scatter", "number"),
}
CREDIT = 32


def bf16_parts(value):
    import numpy as np
    parts, rest = [], np.float32(value)
    for _ in range(3):
        part = (rest.view(np.uint32) & np.uint32(0xFFFF0000)).view(np.float32)
        parts.append(float(part))
        rest = np.float32(rest - part)
    return parts


def build(nc, x, adj, w, out):
    batches = x.shape[0]
    tokens = batches * P
    groups = batches // TILES
    blocks = {}
    for phase, gate in (("exp0", "gnn0"), ("exp1", "gnn1")):
        need = tokens // P + USED[gate] - 1
        blocks[phase] = -(-need // (NR * NL)) * NR * NL
    iters = {"gnn0": groups // NL, "gnn1": groups // NL,
             "exp0": blocks["exp0"] // (NR * NL), "exp1": blocks["exp1"] // (NR * NL)}
    ctx = ExitStack()
    with ctx:
        def sb(name, shape, dt=F32):
            return ctx.enter_context(nc.sbuf_tensor(name, shape, dt))

        def lane_sb(name, shape, dt=F32):
            return [sb(f"{name}_{lane}", shape, dt) for lane in LANES]

        def sem(name):
            return ctx.enter_context(nc.semaphore(name))

        class Signal:

            def __init__(self, name, step=1):
                self.sems = [sem(f"{name}_{lane}") for lane in LANES]
                self.events, self.step, self.base, total = EVENTS[name], step, {}, CREDIT
                for phase in PHASES:
                    self.base[phase] = total
                    total += len(self.events.get(phase, ())) * iters[phase]

            def __getitem__(self, lane):
                return self.sems[lane]

            def nth(self, phase, i, event):
                names = self.events[phase]
                return (i * len(names) + (self.base[phase] + names.index(event) + 1)) * self.step

            def before(self, phase, i, event):
                names = self.events[phase]
                return (i * len(names) + (self.base[phase] + names.index(event) + 1 - len(names))) * self.step

            def end(self, phase):
                return (self.base[phase] + len(self.events.get(phase, ())) * iters[phase]) * self.step

        def dram(name, shape, dt=F32):
            return nc.dram_tensor(name, shape, dt, kind="Internal").ap()

        rows1, rows3 = dram("rows1", (tokens, ROW)), dram("rows3", (tokens, ROW))
        x2 = dram("x2", (tokens, P))
        out_rows = out.rearrange("b p f -> (b p) f")
        ids_len = {g: CLASSES[g] * tokens + blocks["exp" + g[-1]] * P for g in CLASSES}
        ids = {g: dram(f"ids_{g}", (ids_len[g], 1), I32) for g in CLASSES}
        row_parts = dram("row_parts", (3, 3, P), BF16)
        out_bias = {"exp0": dram("bd_parts", (3, EXPERTS, P), BF16), "exp1": dram("b2_parts", (3, EXPERTS, P), BF16)}
        hid_bias = {"exp0": dram("b1_parts0", (3, C, P), BF16), "exp1": dram("b1_parts1", (3, EXPERTS * 2, P), BF16)}

        def group(t):
            return t.rearrange("(g t p) f -> g p t f", t=TILES, p=P)

        x_g, x2_g = group(x.rearrange("b p f -> (b p) f")), group(x2)
        adj_g = group(adj.rearrange("b p f -> (b p) f"))
        rows_g = {"gnn0": group(rows1), "gnn1": group(rows3)}

        ident = sb("ident", [P, P])
        off_diag = sb("off_diag", [P, P], BF16)
        far0 = sb("far0", [P, 3, P], BF16)
        far1 = sb("far1", [P, P], BF16)
        earlier = sb("earlier", [P, P], BF16)
        all_ones = sb("all_ones", [P, P], BF16)
        upto = sb("upto", [64, 64])
        ones_col = sb("ones_col", [64, 1])
        ones3 = sb("ones3", [3, P], BF16)
        ones1 = sb("ones1", [1, P])
        half_neg = sb("half_neg", [P, TILES])
        eps_tile, eps4_tile = sb("eps_tile", [P, TILES]), sb("eps4_tile", [P, TILES])
        iota_c = sb("iota_c", [P, TILES, 64])
        NB = max(blocks.values())
        iota_b = sb("iota_b", [64, NB])
        empty_slot = sb("empty_slot", [P, 260], I32)
        number_step = sb("number_step", [P, TILES], I32)
        NCOL = 7 + C
        R_LN1W, R_LN1B, R_LN2W, R_LN2B, R_BQ, R_BK, R_BV, R_L0B1 = range(8)
        rows = sb("rows", [NCOL, P])
        cols = sb("cols", [P, NCOL])
        wq0, wk0, wv0 = sb("wq0", [P, P]), sb("wk0", [P, P]), sb("wv0", [P, P])
        w10, w20 = sb("w10", [P, P]), sb("w20", [P, P])
        qk0 = sb("qk0", [P, P])
        wv0T, w10T, w20T = sb("wv0T", [P, P]), sb("w10T", [P, P]), sb("w20T", [P, P])
        w10s, w20s = sb("w10s", [P, P]), sb("w20s", [P, P])
        lnf_w, lnf_b = sb("lnf_w", [P, P]), sb("lnf_b", [P, P])
        bias_hi = sb("bias_hi", [1, 3, 3, P], BF16)
        bias3 = sb("bias3", [3, 3, TILES, P], BF16)
        NV = 2 * EXPERTS + C + 2 * EXPERTS
        V_BD, V_B2, V_B10, V_B11 = 0, EXPERTS, 2 * EXPERTS, 2 * EXPERTS + C
        vec_parts = sb("vec_parts", [NV, 3, P], BF16)
        wq1, wk1, wv1, wo1 = sb("wq1", [P, P]), sb("wk1", [P, P]), sb("wv1", [P, P]), sb("wo1", [P, P])
        bq_s = sb("bq_s", [P, 1])
        f0_w1 = sb("f0_w1", [P, HID])
        gate_w = {"gnn0": sb("f0_wg", [P, C, EXPERTS]), "gnn1": sb("f1_wg", [P, 1, EXPERTS])}
        gate_b = {"gnn0": sb("f0_bg", [1, TILES, EXPERTS]), "gnn1": sb("f1_bg", [1, TILES, EXPERTS])}
        b10 = sb("b10", [3, C, P], BF16)

        base = sb("base", [P, 64])
        cnt_i, cnt_s = sb("cnt_i", [64, 1], I32), sb("cnt_s", [64, 1], I32)
        nblk, ends = sb("nblk", [64, 1]), sb("ends", [64, 1])
        b_w = sb("b_w", [1, NB], I32)
        t_off = {p: sb(f"t_off_{p}", [1, NB], I32) for p in ("exp0", "exp1")}
        t_lo = {p: sb(f"t_lo_{p}", [1, NB], I32) for p in ("exp0", "exp1")}
        t_hi = sb("t_hi", [1, NB], I32)

        x_in = lane_sb("x_in", [P, TILES, P])
        adj_in = lane_sb("adj_in", [P, TILES, P], I32)
        no_edge_all, no_edge1_all = (sb(n, [P, NL * TILES, P], BF16) for n in ("no_edge", "no_edge1"))
        no_edge, no_edge1 = ([t[:, lane * TILES:(lane + 1) * TILES, :] for lane in LANES]
                             for t in (no_edge_all, no_edge1_all))
        x_res = lane_sb("x_res", [P, TILES, P])
        bn = lane_sb("bn", [P, TILES, 6])
        mv = lane_sb("mv", [P, TILES, 2])
        var_eps, rstd_t = lane_sb("var_eps_t", [P, TILES]), lane_sb("rstd_t", [P, TILES])
        z = lane_sb("z", [P, TILES, P])
        zT = lane_sb("zT", [P, W])
        flat_z = [t[:, :, :].rearrange("p t f -> p (t f)") for t in z]
        past = flat_z[0][0:64, 0:NB]
        b_cls, b_off, b_tmp = flat_z[1][0:1, 0:NB], flat_z[2][0:1, 0:NB], flat_z[3][0:1, 0:NB]
        xnT = lane_sb("xnT", [P, W])
        qT, kT = lane_sb("qT", [P, W]), lane_sb("kT", [P, W])
        v_one = lane_sb("v_one", [P, TILES, HEADS, DK + 1])
        far = lane_sb("far", [P, HEADS, TILES])
        prob = lane_sb("prob", [P, HEADS, TILES, P])
        probT_all = sb("probT", [P, NL, HEADS, TILES, P])
        probT = [probT_all[:, lane, :, :, :] for lane in LANES]
        bias_in, bias_row, bias_rest = (prob[0][0:1, h, 0:3, :] for h in range(3))
        bias_rest2 = prob[0][0:1, 3, 0:3, :]
        vec, vec_rest, vec_rest2 = (prob[1][0:NV, h, 0, :] for h in range(3))
        hidden = prob
        v = [t[:, 1, :, :] for t in probT]
        th = [t[:, 2, :, :] for t in probT]
        sw = [t[:, 3, :, :] for t in probT]
        den = lane_sb("den", [P, TILES])
        rden = lane_sb("rden", [P, TILES, HEADS])
        hn = lane_sb("hn", [P, TILES, P])
        y_out = lane_sb("y_out", [P, TILES, ROW])
        logit, top, ediff, t_half, t_inv = (lane_sb(n, [P, TILES, EXPERTS])
                                            for n in ("logit", "top", "ediff", "t_half", "t_inv"))
        top_i = lane_sb("top_i", [P, TILES, 8], U32)
        idx, pair = lane_sb("idx", [P, TILES, 2]), lane_sb("pair", [P, TILES, 2])
        gsum, p0, p1, flip, cls, rank, slot_f = (lane_sb(n, [P, TILES])
                                                 for n in ("gsum", "p0", "p1", "flip", "cls", "rank", "slot_f"))
        pdiff, swap = lane_sb("pdiff", [P, TILES]), lane_sb("swap", [P, TILES])
        slot, number = lane_sb("slot", [P, TILES], I32), lane_sb("number", [P, TILES], I32)
        onehot = lane_sb("onehot", [P, TILES, 64], BF16)
        ranks = [t[:, 0:2, :].rearrange("p a b -> p (a b)") for t in hn]
        row_in = [[sb(f"row_in_{lane}_{r}", [P, ROW]) for r in ROUNDS] for lane in LANES]
        id_in = [[sb(f"id_in_{lane}_{r}", [P, 1], I32) for r in ROUNDS] for lane in LANES]
        zb = [[z[lane][:, r, :] for r in ROUNDS] for lane in LANES]
        zbT = [[zT[lane][:, r * P:(r + 1) * P] for r in ROUNDS] for lane in LANES]
        yb = [[y_out[lane][:, r, 0:P] for r in ROUNDS] for lane in LANES]
        half_all = probT_all[:, 0:2, :, :, :].rearrange("p l h t f -> p (l h t) f")
        w_down0 = half_all
        w_down1 = half_all[:, 0:2 * EXPERTS, :]
        w_up_all = half_all[:, 2 * EXPERTS:4 * EXPERTS, :].rearrange("p (e c) f -> p e (c f)", e=EXPERTS)
        w_up = [[probT_all[:, 2 + r, lane, :, :].rearrange("p t f -> p (t f)") for r in range(2)] + [qT[lane][:, :]]
                for lane in LANES]
        hb = [[prob[lane][:, r, :, :] for r in ROUNDS] for lane in LANES]
        part = [[prob[lane][:, NR, r, :] for r in ROUNDS] for lane in LANES]
        up_b = no_edge_all[0:3, 0:2 * EXPERTS, :]
        down_b = no_edge1_all[0:3, 0:EXPERTS, :]

        bank = [[ctx.enter_context(nc.psum_tensor(f"bank{lane}_{b}", [P, W], F32)) for b in range(2)] for lane in LANES]

        def tiles_of(t):
            return t[:, :].rearrange("p (t f) -> p t f", t=TILES)

        passed = sem("wait_passed")
        loaded, consts, prep_pe, prep_dve = (sem(n) for n in ("weights_loaded", "consts_ready", "prep_products",
                                                              "prep_vector_steps"))
        parts_out, parts_in, cleared = sem("bias_parts_written"), sem("bias_parts_read"), sem("lists_cleared")
        plan_pe, plan_dve = sem("plan_products"), sem("plan_vector_steps")
        gathered = [sem(f"rows_gathered_{lane}") for lane in LANES]
        scattered = [sem(f"rows_scattered_{lane}") for lane in LANES]
        numbered = [sem(f"ids_scattered_{lane}") for lane in LANES]

        x_loaded, adj_loaded = Signal("x_loaded", 16), Signal("adj_loaded", 16)
        stored = Signal("stored", 16)
        transposed, copied, product, activated = (Signal(n) for n in ("transposed", "copied", "product", "activated"))
        stats, mean_var, normed = Signal("stats"), Signal("mean_var"), Signal("normed")
        ve_ready, rstd = Signal("var_eps"), Signal("rstd")
        pooled, vector = Signal("pooled"), Signal("vector")

        def vrow(name):
            return w[name].rearrange("(a p) -> a p", a=1)

        weight_loads = [
            (wq0[:, :], w["L0_gnn_Wq"]), (wk0[:, :], w["L0_gnn_Wk"]), (wv0[:, :], w["L0_gnn_Wv"]),
            (w10[:, :], w["L0_gnn_W1"]), (w20[:, :], w["L0_gnn_W2"]),
            (lnf_w[:, :], vrow("L0_gnn_lnf_w").to_broadcast((P, P))),
            (lnf_b[:, :], vrow("L0_gnn_lnf_b").to_broadcast((P, P))),
            (wq1[:, :], w["L1_gnn_Wq"]), (wk1[:, :], w["L1_gnn_Wk"]), (wv1[:, :], w["L1_gnn_Wv"]),
            (wo1[:, :], w["L1_gnn_Wo"]),
            (rows[R_L0B1:R_L0B1 + C, :], w["L0_ffn_b1"].rearrange("(c p) -> c p", p=P)),
            (f0_w1[:, :], w["L0_ffn_W1"]),
            (gate_w["gnn0"][:, :, :], w["L0_ffn_Wg"].rearrange("(c p) e -> p c e", p=P)),
            (gate_w["gnn1"][:, 0, :], w["L1_ffn_gate_w"]),
            (vec[V_BD:V_BD + EXPERTS, :], w["L0_ffn_bd"]), (vec[V_B2:V_B2 + EXPERTS, :], w["L1_ffn_b2"]),
            (vec[V_B10:V_B10 + C, :], w["L0_ffn_b1"].rearrange("(c p) -> c p", p=P)),
            (vec[V_B11:V_B11 + 2 * EXPERTS, :], w["L1_ffn_b1"].rearrange("e (c p) -> (e c) p", p=P)),
        ] + [
            (gate_b[g][:, t, :], w[n].rearrange("(a e) -> a e", a=1))
            for g, n in (("gnn0", "L0_ffn_bg"), ("gnn1", "L1_ffn_gate_b")) for t in range(TILES)
        ] + [
            (rows[r:r + 1, :], vrow(n))
            for r, n in ((R_LN1W, "L0_gnn_ln1_w"), (R_LN1B, "L0_gnn_ln1_b"), (R_LN2W, "L0_gnn_ln2_w"),
                         (R_LN2B, "L0_gnn_ln2_b"), (R_BQ, "L1_gnn_bq"), (R_BK, "L1_gnn_bk"), (R_BV, "L1_gnn_bv"))
        ] + [
            (bias_in[:, j, :], vrow(n)) for j, n in enumerate(("L0_gnn_b1", "L0_gnn_b2", "L1_gnn_bo"))
        ]
        LOADED = 16 * len(weight_loads)
        N_CLEAR = sum(-(-n // P // 260) for n in ids_len.values())

        def enter(eng, phase):
            last = PHASES[PHASES.index(phase) - 1]
            for signal in (x_loaded, adj_loaded, stored, product, copied, activated, vector, pooled):
                for lane in LANES:
                    eng.wait_ge(signal[lane], signal.end(last))
            for lane in LANES:
                if last.startswith("gnn"):
                    eng.wait_ge(numbered[lane], numbers(last, iters[last] - 1))
                else:
                    eng.wait_ge(scattered[lane], scatters(last, iters[last] - 1, NR - 1))

        def numbers(phase, i):
            return (i + (0 if phase == "gnn0" else iters["gnn0"]) + 1) * TILES * 16

        def gathers(phase, i, r):
            return (i * NR + (NR * iters["exp0"] if phase == "exp1" else 0) + r + 1) * 16

        scatters = gathers

        def stages(phase, i, step):
            names = STAGES[phase]
            for slot in range(len(names)):
                for lane in LANES:
                    s = slot - lane * len(names) // NL
                    j = i if s >= 0 else i - 1
                    if not isinstance(i, int) or 0 <= j < iters[phase]:
                        step(names[s], j, lane)

        def staggered(phase, eng, step):
            stages(phase, 0, step)
            if iters[phase] > 1:
                with eng.Fori(1, iters[phase]) as i:
                    stages(phase, i, step)
            stages(phase, iters[phase], step)

        def later(phase, i, r, k):
            j, rr = i + (r + k) // NR, (r + k) % NR
            return [] if isinstance(i, int) and not 0 <= j < iters[phase] else [(j, rr)]

        def rounds(phase, eng, step):
            with eng.Fori(0, iters[phase] - 1) as i:
                for r in ROUNDS:
                    step(i, r)
            for r in ROUNDS:
                step(iters[phase] - 1, r)

        block = ctx.enter_context(nc.Block())

        @block.sync
        def _(sp):
            for signal in (x_loaded, adj_loaded, stored, transposed, copied, product, activated, stats, mean_var,
                           ve_ready, rstd, normed, pooled, vector):
                for lane in LANES:
                    sp.sem_inc(signal[lane], CREDIT * signal.step)
            for dst, src in weight_loads:
                sp.dma_start(dst, src).then_inc(loaded, 16)

            def load(phase, src, i, lane):
                sp.wait_ge(normed[lane], normed.before(phase, i, "0"))
                sp.sem_inc(passed, 1)
                if phase == "gnn0":
                    sp.wait_ge(pooled[lane], pooled.before(phase, i, "kept"))
                else:
                    sp.wait_ge(vector[lane], vector.before(phase, i, "y"))
                sp.sem_inc(passed, 1)
                sp.dma_start(x_in[lane][:, :, :], src[i * NL + lane]).then_inc(x_loaded[lane], 16)
                sp.wait_ge(pooled[lane], pooled.before(phase, i, "mask"))
                sp.sem_inc(passed, 1)
                sp.dma_start(adj_in[lane][:, :, :], adj_g[i * NL + lane]).then_inc(adj_loaded[lane], 16)

            def gnn(phase, src):
                n = iters[phase]

                def step(stage, i, lane):
                    if stage == {"gnn0": "attention", "gnn1": "gate_apply"}[phase] and not (isinstance(i, int) and i == n - 1):
                        load(phase, src, i + 1, lane)
                    if stage == "ranks":
                        sp.wait_ge(vector[lane], vector.nth(phase, i, "weights"))
                        sp.sem_inc(passed, 1)
                        sp.dma_start(rows_g[phase][i * NL + lane], y_out[lane][:, :, :]).then_inc(stored[lane], 16)

                for lane in LANES:
                    load(phase, src, 0, lane)
                stages(phase, 0, step)
                if n > 2:
                    with sp.Fori(1, n - 1) as i:
                        stages(phase, i, step)
                if n > 1:
                    stages(phase, n - 1, step)
                stages(phase, n, step)

            gate_of = {"exp0": "gnn0", "exp1": "gnn1"}

            def number_load(phase, i, r, lane):
                at = sp.value_load(t_off[phase][0:1, bass.ds(i * NR * NL + (r * NL + lane), 1)], min_val=0,
                                   max_val=ids_len[gate_of[phase]] - P)
                if not isinstance(i, int) or i or r:
                    (j, q), = later(phase, i, r, -1)
                    sp.wait_ge(x_loaded[lane], x_loaded.nth(phase, j, f"ids{q}"))
                    sp.sem_inc(passed, 1)
                if not isinstance(i, int) or i:
                    sp.wait_ge(scattered[lane], scatters(phase, i - 1, r))
                    sp.sem_inc(passed, 1)
                sp.dma_start(id_in[lane][r][:, :], ids[gate_of[phase]][bass.ds(at, P), :]).then_inc(x_loaded[lane], 16)

            def exp(phase):
                if phase == "exp0":
                    sp.dma_start(w_down0, w["L0_ffn_Wd"].rearrange("e (c p) f -> p (e c) f", p=P)).then_inc(loaded, 16)
                else:
                    sp.dma_start(w_up_all, w["L1_ffn_W1"].rearrange("e d h -> d e h")).then_inc(loaded, 16)
                    sp.dma_start(w_down1, w["L1_ffn_W2"].rearrange("e (c p) f -> p (e c) f", p=P)).then_inc(loaded, 16)
                    sp.dma_start(up_b[:, :, :], hid_bias[phase]).then_inc(loaded, 16)
                sp.dma_start(down_b[:, :, :], out_bias[phase]).then_inc(loaded, 16)
                for r in ROUNDS:
                    for lane in LANES:
                        number_load(phase, 0, r, lane)
                with sp.Fori(1, iters[phase]) as i:
                    for r in ROUNDS:
                        for lane in LANES:
                            number_load(phase, i, r, lane)

            sp.wait_ge(prep_dve, PREP_END)
            sp.dma_start(row_parts.rearrange("j b f -> (j b f)").rearrange("(a n) -> a n", a=1),
                         bias_hi[:, :, :, :].rearrange("a j b f -> a (j b f)")).then_inc(parts_out, 16)
            for dst, at, n in ((out_bias["exp0"], V_BD, EXPERTS), (out_bias["exp1"], V_B2, EXPERTS),
                               (hid_bias["exp0"], V_B10, C), (hid_bias["exp1"], V_B11, 2 * EXPERTS)):
                sp.dma_start(dst.rearrange("j e f -> e j f"), vec_parts[at:at + n, :, :]).then_inc(parts_out, 16)
            sp.wait_ge(parts_out, 16 * 5)
            sp.dma_start(b10[:, :, :], hid_bias["exp0"]).then_inc(parts_in, 16)
            for b in range(3):
                for t in range(TILES):
                    sp.dma_start(bias3[:, b, t, :], row_parts[:, b, :]).then_inc(parts_in, 16)

            gnn("gnn0", x_g)
            enter(sp, "exp0")
            sp.wait_ge(plan_dve, PLAN_STEPS["gnn0"])
            exp("exp0")
            enter(sp, "gnn1")
            gnn("gnn1", x2_g)
            enter(sp, "exp1")
            sp.wait_ge(plan_dve, PLAN_STEPS["gnn0"] + PLAN_STEPS["gnn1"])
            exp("exp1")

        @block.gpsimd
        def _(pool):
            def fixed(ins):
                ins.then_inc(consts, 1)

            fixed(pool.memset(ident[:, :], 0.0))
            fixed(pool.memset(off_diag[:, :], 1.0))
            fixed(pool.memset(far0[:, :, :], 0.0))
            fixed(pool.memset(far1[:, :], 0.0))
            fixed(pool.memset(earlier[:, :], 1.0))
            fixed(pool.memset(upto[:, :], 1.0))
            fixed(pool.memset(all_ones[:, :], 1.0))
            fixed(pool.memset(ones_col[:, :], 1.0))
            fixed(pool.memset(ones3[:, :], 1.0))
            fixed(pool.memset(ones1[:, :], 1.0))
            fixed(pool.memset(half_neg[:, :], -0.5))
            fixed(pool.memset(eps_tile[:, :], EPS))
            fixed(pool.memset(eps4_tile[:, :], 4 * EPS))
            fixed(pool.memset(empty_slot[:, :], tokens))
            fixed(pool.memset(number_step[:, :], NL * W))
            fixed(pool.iota(iota_c[:, :, :], [[0, TILES], [1, 64]], base=0, channel_multiplier=0,
                            allow_small_or_imprecise_dtypes=True))
            fixed(pool.iota(iota_b[:, :], [[1, NB]], base=0, channel_multiplier=0,
                            allow_small_or_imprecise_dtypes=True))
            for lane in LANES:
                fixed(pool.iota(number[lane][:, :], [[P, TILES]], base=lane * W, channel_multiplier=1))
                fixed(pool.memset(v_one[lane][:, :, :, DK:DK + 1], 1.0))
                fixed(pool.memset(y_out[lane][:, :, :], 0.0))
                for r in ROUNDS:
                    fixed(pool.memset(row_in[lane][r][:, :], 0.0))
            pool.wait_ge(consts, CONSTS - 8)
            fills = [(ident[:, :], 1.0), (off_diag[:, :], 0.0), (far1[:, :], -1e30)]
            fills += [(far0[:, j, :], value) for j, value in enumerate(bf16_parts(-1e9))]
            for tile, fill in fills:
                fixed(pool.affine_select(out=tile, in_=tile, compare_op=ALU.not_equal, fill=fill, base=0,
                                         pattern=[[-1, P]], channel_multiplier=1))
            fixed(pool.affine_select(out=earlier[:, :], in_=earlier[:, :], compare_op=ALU.is_gt, fill=0.0, base=0,
                                     pattern=[[1, P]], channel_multiplier=-1))
            fixed(pool.affine_select(out=upto[:, :], in_=upto[:, :], compare_op=ALU.is_ge, fill=0.0, base=0,
                                     pattern=[[1, 64]], channel_multiplier=-1))

            def rstd_of(phase, lane, i, k, eps, var=None, to=None):
                pool.wait_ge(mean_var[lane], mean_var.nth(phase, i, k))
                pool.tensor_tensor(var_eps[lane][:, :], mv[lane][:, :, 1] if var is None else var, eps[:, :], ALU.add)\
                    .then_inc(ve_ready[lane], 1)
                pool.wait_ge(ve_ready[lane], ve_ready.nth(phase, i, k))
                pool.tensor_tensor(rstd_t[lane][:, :] if to is None else to, var_eps[lane][:, :], half_neg[:, :],
                                   ALU.pow).then_inc(rstd[lane], 1)

            def scatter(phase, i, lane):
                pool.wait_ge(vector[lane], vector.nth(phase, i, "slot"))
                pool.sem_inc(passed, 1)
                for t in range(TILES):
                    pool.indirect_dma_start(ids[phase], bass.IndirectOffsetOnAxis(slot[lane][:, t:t + 1], 0),
                                            number[lane][:, t:t + 1], None).then_inc(numbered[lane], 16)

            def next_numbers(phase, i, lane):
                pool.wait_ge(numbered[lane], numbers(phase, i))
                pool.tensor_tensor(number[lane][:, :], number[lane][:, :], number_step[:, :], ALU.add)\
                    .then_inc(pooled[lane], 1)

            def mask(phase, i, lane, scores):
                pool.wait_ge(adj_loaded[lane], adj_loaded.nth(phase, i, "adj"))
                pool.wait_ge(product[lane], product.before(phase, i, scores))
                pool.sem_inc(passed, 1)
                pool.tensor_scalar(no_edge[lane], adj_in[lane][:, :, :], 0.0, None, ALU.is_equal)\
                    .then_inc(pooled[lane], 1)

            def gate_rstd(phase, i, lane):
                rstd_of(phase, lane, i, "gate", eps_tile, y_out[lane][:, :, RSTD], y_out[lane][:, :, RSTD])

            def gnn0_step(stage, i, lane):
                if stage == "ln0_rstd":
                    rstd_of("gnn0", lane, i, "0", eps_tile)
                    mask("gnn0", i, lane, "scores")
                elif stage == "scores":
                    pool.wait_ge(pooled[lane], pooled.before("gnn0", i, "y"))
                    pool.wait_ge(x_loaded[lane], x_loaded.nth("gnn0", i, "x"))
                    pool.tensor_tensor(x_res[lane][:, :, :], x_in[lane][:, :, :],
                                       lnf_b[:, :].unsqueeze(1).to_broadcast((P, TILES, P)), ALU.add)\
                        .then_inc(pooled[lane], 1)
                elif stage in ("ln1_rstd", "ln2_rstd"):
                    rstd_of("gnn0", lane, i, stage[2], eps4_tile)
                elif stage == "ln3_rstd":
                    rstd_of("gnn0", lane, i, "3", eps_tile)
                elif stage == "residual":
                    pool.wait_ge(normed[lane], normed.nth("gnn0", i, "3"))
                    pool.tensor_tensor(hn[lane][:, :, :], z[lane][:, :, :],
                                       lnf_w[:, :].unsqueeze(1).to_broadcast((P, TILES, P)), ALU.mult)\
                        .then_inc(pooled[lane], 1)
                    pool.wait_ge(pooled[lane], pooled.nth("gnn0", i, "scaled"))
                    pool.wait_ge(stored[lane], stored.before("gnn0", i, "y"))
                    pool.tensor_tensor(y_out[lane][:, :, 0:P], hn[lane][:, :, :], x_res[lane][:, :, :], ALU.add)\
                        .then_inc(pooled[lane], 1)
                elif stage == "gate_rstd":
                    gate_rstd("gnn0", i, lane)
                elif stage == "scatter":
                    scatter("gnn0", i, lane)
                elif stage == "number":
                    next_numbers("gnn0", i, lane)

            def gnn1_step(stage, i, lane):
                if stage == "ln0_rstd":
                    rstd_of("gnn1", lane, i, "0", eps_tile)
                    mask("gnn1", i, lane, "scores3")
                elif stage == "xn_copy":
                    pool.wait_ge(pooled[lane], pooled.nth("gnn1", i, "mask"))
                    pool.tensor_tensor(no_edge1[lane], no_edge[lane],
                                       off_diag[:, :].unsqueeze(1).to_broadcast((P, TILES, P)), ALU.mult)\
                        .then_inc(pooled[lane], 1)
                elif stage == "gate_rstd":
                    gate_rstd("gnn1", i, lane)
                elif stage == "scatter":
                    scatter("gnn1", i, lane)
                elif stage == "number":
                    next_numbers("gnn1", i, lane)

            pool.wait_ge(consts, CONSTS)
            pool.wait_ge(cleared, 16 * N_CLEAR)
            staggered("gnn0", pool, gnn0_step)

            def fetch(phase, i, r, lane):
                pool.wait_ge(x_loaded[lane], x_loaded.nth(phase, i, f"ids{r}"))
                if not isinstance(i, int) or i or r:
                    (j, q), = later(phase, i, r, -1)
                    pool.wait_ge(gathered[lane], gathers(phase, j, q))
                pool.sem_inc(passed, 1)
                pool.indirect_dma_start(row_in[lane][r][:, :], None, {"exp0": rows1, "exp1": rows3}[phase],
                                        bass.IndirectOffsetOnAxis(id_in[lane][r][:, 0:1], 0),
                                        bounds_check=tokens - 1, oob_is_err=False).then_inc(gathered[lane], 16)

            def put_back(phase, i, r, lane):
                pool.wait_ge(vector[lane], vector.nth(phase, i, f"out{r}"))
                pool.sem_inc(passed, 1)
                pool.indirect_dma_start({"exp0": x2, "exp1": out_rows}[phase],
                                        bass.IndirectOffsetOnAxis(id_in[lane][r][:, 0:1], 0), yb[lane][r], None,
                                        bounds_check=tokens - 1, oob_is_err=False).then_inc(scattered[lane], 16)

            def exp(phase):
                for r in ROUNDS:
                    for lane in LANES:
                        fetch(phase, 0, r, lane)

                def step(i, r):
                    for lane in LANES:
                        put_back(phase, i, r, lane)
                    for j, q in later(phase, i, r, NR):
                        for lane in LANES:
                            fetch(phase, j, q, lane)

                rounds(phase, pool, step)

            enter(pool, "exp0")
            exp("exp0")
            enter(pool, "gnn1")
            for lane in LANES:
                fixed(pool.iota(number[lane][:, :], [[P, TILES]], base=lane * W, channel_multiplier=1))
            pool.wait_ge(consts, CONSTS + NL)
            staggered("gnn1", pool, gnn1_step)
            enter(pool, "exp1")
            exp("exp1")
            for lane in LANES:
                pool.wait_ge(scattered[lane], scatters("exp1", iters["exp1"] - 1, NR - 1))

        @block.tensor
        def _(pe):
            pe.wait_ge(consts, CONSTS)
            pe.wait_ge(loaded, LOADED)
            b0, b1, b2, b3 = bank[0][0], bank[0][1], bank[1][0], bank[1][1]
            pe.transpose(b0[:, 0:NCOL], rows[:, :], ident[0:NCOL, 0:NCOL])
            pe.matmul(b1[:, 0:P], wq0[:, :], wk0[:, :], start=True, stop=True)
            pe.transpose(b2[:, 0:P], wv0[:, :], ident[:, :])
            pe.transpose(b2[:, P:2 * P], w10[:, :], ident[:, :])
            pe.transpose(b2[:, 2 * P:3 * P], w20[:, :], ident[:, :]).then_inc(prep_pe, 1)
            pe.wait_ge(prep_dve, PREP_COPIED)
            pe.matmul(b3[0:1, 0:P], cols[:, R_LN1B:R_LN1B + 1], w10T[:, :], start=True, stop=True)
            pe.matmul(b3[0:1, P:2 * P], cols[:, R_LN2B:R_LN2B + 1], w20T[:, :], start=True, stop=True)
            pe.matmul(b3[0:1, 2 * P:3 * P], cols[:, R_BV:R_BV + 1], wo1[:, :], start=True, stop=True)\
                .then_inc(prep_pe, 1)
            pe.wait_ge(prep_dve, PREP_END)
            pe.wait_ge(parts_in, 16 * (3 * TILES + 1))

            def turn(phase, i, lane, k, event):
                pe.wait_ge(normed[lane], normed.nth(phase, i, k))
                for t in range(TILES):
                    last = pe.transpose(bank[lane][0][:, t * P:(t + 1) * P], z[lane][:, t, :], ident[:, :])
                last.then_inc(transposed[lane], 1)

            def linear(into, lhs, rhs, b):
                pe.matmul(into[:, :], ones3[:, :], bias3[:, b, :, :].rearrange("j t f -> j (t f)"), start=True, stop=False)
                for t in range(TILES):
                    last = pe.matmul(into[:, t * P:(t + 1) * P], lhs[:, t * P:(t + 1) * P], rhs,
                                     start=False, stop=t == TILES - 1)
                return last

            def values(lane, weights):
                for t in range(TILES):
                    last = pe.matmul(bank[lane][1][:, t * P:(t + 1) * P], xnT[lane][:, t * P:(t + 1) * P], weights,
                                     start=True, stop=True)
                return last

            def logits(phase, i, lane, lhs, chunks):
                into = bank[lane][1][:, 0:TILES * EXPERTS]
                pe.matmul(into, ones1[:, :], gate_b[phase][:, :, :].rearrange("a t e -> a (t e)"), start=True, stop=False)
                for t in range(TILES):
                    for c in range(chunks):
                        last = pe.matmul(into[:, t * EXPERTS:(t + 1) * EXPERTS], lhs(c, t), gate_w[phase][:, c, :],
                                         start=False, stop=t == TILES - 1 and c == chunks - 1)
                last.then_inc(product[lane], 1)

            def rank_products(phase, i, lane):
                n = CLASSES[phase]
                pe.wait_ge(vector[lane], vector.nth(phase, i, "onehot"))
                hot = onehot[lane][:, :, 0:n]
                into = bank[lane][0][:, 0:TILES * n].rearrange("p (t c) -> p t c", t=TILES)
                pe.matmul(into, earlier[:, :], hot, start=True, stop=False)
                for t in range(TILES - 1):
                    pe.matmul(into[:, t + 1:TILES, :], all_ones[:, :],
                              hot[:, t:t + 1, :].to_broadcast((P, TILES - 1 - t, n)), start=False, stop=t == TILES - 2)
                total = bank[lane][0][:, TILES * 64:TILES * 64 + n]
                for t in range(TILES):
                    last = pe.matmul(total, all_ones[:, :], hot[:, t, :], start=t == 0, stop=t == TILES - 1,
                                     skip_group_check=True)
                last.then_inc(product[lane], 1)

            def plan(phase):
                n, nb = CLASSES[phase], blocks["exp" + phase[-1]]
                at = 0 if phase == "gnn0" else PLAN_STEPS["gnn0"]
                pe.wait_ge(plan_dve, at + 1)
                pe.transpose(bank[0][0][0:n, 0:P], base[:, 0:n], ident[:, :]).then_inc(plan_pe, 1)
                pe.wait_ge(plan_dve, at + 4)
                pe.matmul(bank[0][1][0:n, 0:1], upto[0:n, 0:n], nblk[0:n, :], start=True, stop=True).then_inc(plan_pe, 1)
                pe.wait_ge(plan_dve, at + 6)
                pe.matmul(bank[1][0][0:1, 0:nb], ones_col[0:n, :], past[0:n, 0:nb], start=True, stop=True)
                pe.matmul(bank[1][1][0:1, 0:nb], nblk[0:n, :], past[0:n, 0:nb], start=True, stop=True)\
                    .then_inc(plan_pe, 1)

            def gnn0_step(stage, i, lane):
                if stage == "xn_turn":
                    pe.wait_ge(vector[lane], vector.before("gnn0", i, "base"))
                    turn("gnn0", i, lane, "0", "xn")
                elif stage == "qk_v":
                    pe.wait_ge(copied[lane], copied.nth("gnn0", i, "xn"))
                    pe.matmul(bank[lane][0][:, :], qk0[:, :], xnT[lane][:, :], start=True, stop=True)\
                        .then_inc(product[lane], 1)
                    values(lane, wv0T[:, :]).then_inc(product[lane], 1)
                elif stage == "scores":
                    pe.wait_ge(pooled[lane], pooled.nth("gnn0", i, "mask"))
                    pe.wait_ge(activated[lane], activated.nth("gnn0", i, "qk"))
                    pe.wait_ge(vector[lane], vector.nth("gnn0", i, "v"))
                    for j in range(3):
                        pe.matmul(bank[lane][1][:, :], far0[:, j, :],
                                  no_edge[lane].rearrange("p t f -> p (t f)"), start=j == 0, stop=False)
                    for t in range(TILES):
                        last = pe.matmul(bank[lane][1][:, t * P:(t + 1) * P], qT[lane][:, t * P:(t + 1) * P],
                                         xnT[lane][:, t * P:(t + 1) * P], start=False, stop=t == TILES - 1)
                    last.then_inc(product[lane], 1)
                elif stage == "prob_turn":
                    pe.wait_ge(activated[lane], activated.nth("gnn0", i, "prob"))
                    for t in range(TILES):
                        last = pe.transpose(bank[lane][0][:, t * P:(t + 1) * P], prob[lane][:, 0, t, :], ident[:, :])
                    last.then_inc(transposed[lane], 1)
                elif stage == "mix":
                    pe.wait_ge(copied[lane], copied.nth("gnn0", i, "prob"))
                    for t in range(TILES):
                        last = pe.matmul(bank[lane][1][:, t * P:(t + 1) * P], probT[lane][:, 0, t, :], v[lane][:, t, :],
                                         start=True, stop=True)
                    last.then_inc(product[lane], 1)
                elif stage in ("z1_turn", "z2_turn"):
                    turn("gnn0", i, lane, stage[1], stage[:2])
                elif stage in ("linear1", "linear2"):
                    k = int(stage[-1])
                    pe.wait_ge(copied[lane], copied.nth("gnn0", i, f"z{k}"))
                    linear(bank[lane][1], zT[lane], (w10s, w20s)[k - 1][:, :], k - 1).then_inc(product[lane], 1)
                elif stage == "gate_turn":
                    turn("gnn0", i, lane, "gate", "gate")
                elif stage in ("hidden01", "hidden23"):
                    if stage == "hidden01":
                        pe.wait_ge(copied[lane], copied.nth("gnn0", i, "gate"))
                    for c in (int(stage[-2]), int(stage[-1])):
                        if c >= 2:
                            pe.wait_ge(activated[lane], activated.nth("gnn0", i, f"hid{c - 2}"))
                        pe.matmul(bank[lane][1 - c % 2][:, :], f0_w1[:, c * P:(c + 1) * P], xnT[lane][:, :],
                                  start=True, stop=True).then_inc(product[lane], 1)
                elif stage == "logits":
                    pe.wait_ge(activated[lane], activated.nth("gnn0", i, f"hid{C - 1}"))
                    logits("gnn0", i, lane, lambda c, t: hidden[lane][:, c, t, :], C)
                elif stage == "ranks":
                    rank_products("gnn0", i, lane)

            staggered("gnn0", pe, gnn0_step)
            plan("gnn0")

            def exp(phase):
                two = phase == "exp1"

                def chosen(table, i, r, lane):
                    return pe.value_load(table[0:1, bass.ds(i * NR * NL + (r * NL + lane), 1)], min_val=0,
                                         max_val=EXPERTS - 1)

                def row(table, at):
                    return table[:, bass.ds(at, 1), :].rearrange("p a f -> p (a f)")

                def z_turn(i, r, lane):
                    pe.wait_ge(normed[lane], normed.nth(phase, i, f"z{r}"))
                    for j, q in later(phase, i, r, -2):
                        pe.wait_ge(vector[lane], vector.nth(phase, j, f"out{q}"))
                    pe.transpose(bank[lane][0][:, 0:P], zb[lane][r], ident[:, :]).then_inc(transposed[lane], 1)

                def up(i, r, lane):
                    experts = [chosen(t, i, r, lane) for t in (t_lo[phase], t_hi)] if two else []
                    pe.wait_ge(copied[lane], copied.nth(phase, i, f"z{r}"))
                    if two:
                        pe.wait_ge(activated[lane], activated.nth(phase, i, f"up{r}"))
                    weights = w_up[lane][r] if two else f0_w1[:, :]
                    for c in range(C):
                        to = bank[lane][1][:, c * P:(c + 1) * P]
                        bias = row(up_b, experts[c // 2] * 2 + c % 2) if two else b10[:, c, :]
                        pe.matmul(to, bias, ones3[:, :], start=True, stop=False)
                        last = pe.matmul(to, weights[:, c * P:(c + 1) * P], zbT[lane][r], start=False, stop=True)
                    last.then_inc(product[lane], 1)

                def down(i, r, lane):
                    experts = [chosen(t, i, r, lane) for t in ((t_lo[phase], t_hi) if two else (t_lo[phase],))]
                    pe.wait_ge(activated[lane], activated.nth(phase, i, f"hid{r}"))
                    for j, q in later(phase, i, r, -1):
                        pe.wait_ge(vector[lane], vector.nth(phase, j, f"out{q}"))
                    for j, q in later(phase, i, r, 1):
                        pe.wait_ge(copied[lane], copied.nth(phase, j, f"z{q}"))
                    n = C // len(experts)
                    for k, e in enumerate(experts):
                        to = bank[lane][0][:, (k + 1) * P:(k + 2) * P]
                        pe.matmul(to, ones3[:, :], row(down_b, e), start=True, stop=False)
                        for c in range(n):
                            last = pe.matmul(to, hb[lane][r][:, k * n + c, :],
                                             row(w_down1 if two else w_down0, e * n + c), start=False, stop=c == n - 1)
                    last.then_inc(product[lane], 1)

                def step(i, r):
                    for lane in LANES:
                        down(i, r, lane)
                    for lane in LANES:
                        for j, q in later(phase, i, r, 1):
                            up(j, q, lane)
                        for j, q in later(phase, i, r, 2):
                            z_turn(j, q, lane)

                for lane in LANES:
                    z_turn(0, 0, lane)
                pe.wait_ge(loaded, LOADED + 16 * (6 if two else 2))
                for lane in LANES:
                    up(0, 0, lane)
                    z_turn(0, 1, lane)
                rounds(phase, pe, step)

            enter(pe, "exp0")
            exp("exp0")
            enter(pe, "gnn1")
            def gnn1_step(stage, i, lane):
                if stage == "xn_turn":
                    pe.wait_ge(vector[lane], vector.before("gnn1", i, "base"))
                    turn("gnn1", i, lane, "0", "xn")
                elif stage == "qk":
                    pe.wait_ge(copied[lane], copied.nth("gnn1", i, "xn"))
                    pe.matmul(bank[lane][1][:, :], wq1[:, :], xnT[lane][:, :], start=True, stop=True)\
                        .then_inc(product[lane], 1)
                    pe.matmul(bank[lane][0][:, :], wk1[:, :], xnT[lane][:, :], start=True, stop=True)\
                        .then_inc(product[lane], 1)
                elif stage == "values":
                    pe.wait_ge(activated[lane], activated.nth("gnn1", i, "q"))
                    values(lane, wv1[:, :]).then_inc(product[lane], 1)
                elif stage in ("scores01", "scores23"):
                    two = (int(stage[-2]), int(stage[-1]))
                    if two[0] == 0:
                        pe.wait_ge(pooled[lane], pooled.nth("gnn1", i, "mask_self"))
                        pe.wait_ge(activated[lane], activated.nth("gnn1", i, "k"))
                        pe.wait_ge(vector[lane], vector.nth("gnn1", i, "v"))
                    for h in two:
                        if h >= 2:
                            pe.wait_ge(vector[lane], vector.nth("gnn1", i, f"shift{h - 2}"))
                        pe.matmul(bank[lane][h % 2][:, :], far1[:, :],
                                  no_edge1[lane].rearrange("p t f -> p (t f)"), start=True, stop=False)
                    for t in range(TILES):
                        for h in two:
                            head = slice(h * DK, (h + 1) * DK)
                            last = pe.matmul(bank[lane][h % 2][:, t * P:(t + 1) * P],
                                             qT[lane][head, t * P:(t + 1) * P],
                                             kT[lane][head, t * P:(t + 1) * P], start=False, stop=t == TILES - 1)
                            if t == TILES - 1:
                                last.then_inc(product[lane], 1)
                elif stage in ("prob_turn01", "prob_turn23"):
                    for h in (int(stage[-2]), int(stage[-1])):
                        pe.wait_ge(activated[lane], activated.nth("gnn1", i, f"prob{h}"))
                        if h < 2:
                            pe.wait_ge(vector[lane], vector.nth("gnn1", i, f"shift{h + 2}"))
                        else:
                            pe.wait_ge(copied[lane], copied.nth("gnn1", i, f"prob{h - 2}"))
                        for t in range(TILES):
                            last = pe.transpose(bank[lane][h % 2][:, t * P:(t + 1) * P], prob[lane][:, h, t, :], ident[:, :])
                        last.then_inc(transposed[lane], 1)
                elif stage == "mix":
                    pe.wait_ge(copied[lane], copied.nth("gnn1", i, "prob3"))
                    for t in range(TILES):
                        to = bank[lane][t // 2][:, 0:2 * HEADS * (DK + 1)].rearrange("p (t h d) -> p t h d", t=2, h=HEADS)
                        for h in range(HEADS):
                            last = pe.matmul(to[:, t % 2, h, :], probT[lane][:, h, t, :], v_one[lane][:, t, h, :],
                                             start=True, stop=True)
                    last.then_inc(product[lane], 1)
                elif stage == "o_turn":
                    pe.wait_ge(vector[lane], vector.nth("gnn1", i, "hn"))
                    for t in range(TILES):
                        last = pe.transpose(bank[lane][0][:, t * P:(t + 1) * P], hn[lane][:, t, :], ident[:, :])
                    last.then_inc(transposed[lane], 1)
                elif stage == "linear":
                    pe.wait_ge(copied[lane], copied.nth("gnn1", i, "o"))
                    linear(bank[lane][1], zT[lane], wo1[:, :], 2).then_inc(product[lane], 1)
                elif stage == "gate_turn":
                    turn("gnn1", i, lane, "gate", "gate")
                elif stage == "logits":
                    pe.wait_ge(copied[lane], copied.nth("gnn1", i, "gate"))
                    logits("gnn1", i, lane, lambda c, t: xnT[lane][:, t * P:(t + 1) * P], 1)
                elif stage == "ranks":
                    rank_products("gnn1", i, lane)

            staggered("gnn1", pe, gnn1_step)
            plan("gnn1")
            enter(pe, "exp1")
            exp("exp1")

        @block.scalar
        def _(act):
            act.wait_ge(consts, CONSTS)
            for g in CLASSES:
                flat = ids[g].rearrange("(p n) a -> p (n a)", p=P)
                for at in range(0, flat.shape[1], 260):
                    to = min(at + 260, flat.shape[1])
                    act.dma_start(flat[:, at:to], empty_slot[:, 0:to - at]).then_inc(cleared, 16)

            def copy_turned(phase, i, lane, event, dst):
                act.wait_ge(transposed[lane], transposed.nth(phase, i, event))
                act.activation(dst[:, :], bank[lane][0][:, :], ACT.Copy).then_inc(copied[lane], 1)

            def gate_tanh(phase, i, lane):
                act.wait_ge(vector[lane], vector.nth(phase, i, "diff"))
                act.activation(t_half[lane][:, :, :], ediff[lane][:, :, :], ACT.Tanh, scale=0.5)\
                    .then_inc(activated[lane], 1)

            def gnn0_step(stage, i, lane):
                if stage == "xn_copy":
                    copy_turned("gnn0", i, lane, "xn", xnT[lane])
                elif stage == "qk_v_copy":
                    act.wait_ge(product[lane], product.nth("gnn0", i, "qk"))
                    act.activation(qT[lane][:, :], bank[lane][0][:, :], ACT.Copy).then_inc(activated[lane], 1)
                elif stage == "prob":
                    act.wait_ge(vector[lane], vector.nth("gnn0", i, "max"))
                    for t in range(TILES):
                        last = act.activation(prob[lane][:, 0, t, :], bank[lane][1][:, t * P:(t + 1) * P], ACT.Exp,
                                              bias=far[lane][:, 0, t:t + 1], accum_out=den[lane][:, t:t + 1])
                    last.then_inc(activated[lane], 1)
                elif stage == "prob_copy":
                    copy_turned("gnn0", i, lane, "prob", probT[lane][:, 0, :, :].rearrange("p t f -> p (t f)"))
                elif stage == "tanh1":
                    act.wait_ge(vector[lane], vector.nth("gnn0", i, "hn"))
                    act.activation(th[lane], hn[lane][:, :, :], ACT.Tanh, scale=0.5).then_inc(activated[lane], 1)
                elif stage in ("z1_copy", "z2_copy"):
                    copy_turned("gnn0", i, lane, stage[:2], zT[lane])
                elif stage == "tanh2":
                    act.wait_ge(product[lane], product.nth("gnn0", i, "h1"))
                    act.activation(th[lane], tiles_of(bank[lane][1]), ACT.Tanh, scale=0.5).then_inc(activated[lane], 1)
                elif stage == "gate_copy":
                    copy_turned("gnn0", i, lane, "gate", xnT[lane])
                elif stage in ("gelu01", "gelu23"):
                    for c in (int(stage[-2]), int(stage[-1])):
                        act.wait_ge(product[lane], product.nth("gnn0", i, f"hid{c}"))
                        act.activation(hidden[lane][:, c, :, :], tiles_of(bank[lane][1 - c % 2]), ACT.Gelu,
                                       bias=cols[:, R_L0B1 + c:R_L0B1 + c + 1]).then_inc(activated[lane], 1)
                elif stage == "gate_tanh":
                    gate_tanh("gnn0", i, lane)

            def gnn1_step(stage, i, lane):
                if stage == "xn_copy":
                    copy_turned("gnn1", i, lane, "xn", xnT[lane])
                elif stage == "qk_copy":
                    act.wait_ge(product[lane], product.nth("gnn1", i, "q"))
                    act.activation(qT[lane][:, :], bank[lane][1][:, :], ACT.Identity, bias=bq_s[:, :], scale=QK_SCALE)\
                        .then_inc(activated[lane], 1)
                    act.wait_ge(product[lane], product.nth("gnn1", i, "k"))
                    act.activation(kT[lane][:, :], bank[lane][0][:, :], ACT.Identity, bias=cols[:, R_BK:R_BK + 1])\
                        .then_inc(activated[lane], 1)
                elif stage in ("prob01", "prob23"):
                    for h in (int(stage[-2]), int(stage[-1])):
                        act.wait_ge(vector[lane], vector.nth("gnn1", i, f"shift{h}"))
                        act.activation(prob[lane][:, h, :, :], prob[lane][:, h, :, :], ACT.Exp)\
                            .then_inc(activated[lane], 1)
                elif stage in ("prob_copy01", "prob_copy23"):
                    for h in (int(stage[-2]), int(stage[-1])):
                        act.wait_ge(transposed[lane], transposed.nth("gnn1", i, f"prob{h}"))
                        act.activation(probT[lane][:, h, :, :].rearrange("p t f -> p (t f)"), bank[lane][h % 2][:, :],
                                       ACT.Copy).then_inc(copied[lane], 1)
                elif stage == "o_copy":
                    copy_turned("gnn1", i, lane, "o", zT[lane])
                elif stage == "gate_copy":
                    copy_turned("gnn1", i, lane, "gate", xnT[lane])
                elif stage == "gate_tanh":
                    gate_tanh("gnn1", i, lane)

            act.preload_act_table(ACT.Exp)
            staggered("gnn0", act, gnn0_step)

            def exp(phase):
                def up_copy(i, r, lane):
                    up_v = w_up[lane][r].rearrange("p (k h) -> p k h", k=2)
                    for k, table in enumerate((t_lo[phase], t_hi)):
                        e = act.value_load(table[0:1, bass.ds(i * NR * NL + (r * NL + lane), 1)], min_val=0,
                                           max_val=EXPERTS - 1)
                        last = act.activation(up_v[:, k, :], w_up_all[:, bass.ds(e, 1), :].rearrange("p a h -> p (a h)"),
                                              ACT.Copy)
                    last.then_inc(activated[lane], 1)

                def step(i, r):
                    for lane in LANES:
                        act.wait_ge(product[lane], product.nth(phase, i, f"hid{r}"))
                        act.activation(hb[lane][r], tiles_of(bank[lane][1]), ACT.Gelu).then_inc(activated[lane], 1)
                        if phase == "exp1":
                            for j, q in later(phase, i, r, 1):
                                up_copy(j, q, lane)

                act.preload_act_table(ACT.Gelu)
                if phase == "exp1":
                    act.wait_ge(loaded, LOADED + 16 * 6)
                    for lane in LANES:
                        up_copy(0, 0, lane)
                rounds(phase, act, step)

            enter(act, "exp0")
            exp("exp0")
            enter(act, "gnn1")
            act.preload_act_table(ACT.Exp)
            staggered("gnn1", act, gnn1_step)
            enter(act, "exp1")
            exp("exp1")

        @block.vector
        def _(dve):
            count = [0]

            def step(ins):
                count[0] += 1
                ins.then_inc(prep_dve, 1)
                dve.wait_ge(prep_dve, count[0])

            dve.wait_ge(prep_pe, 1)
            step(dve.tensor_copy(cols[:, :], bank[0][0][:, 0:NCOL]))
            step(dve.tensor_scalar(qk0[:, :], bank[0][1][:, 0:P], 1.0 / math.sqrt(P), None, ALU.mult))
            step(dve.tensor_copy(wv0T[:, :], bank[1][0][:, 0:P]))
            step(dve.tensor_copy(w10T[:, :], bank[1][0][:, P:2 * P]))
            step(dve.tensor_copy(w20T[:, :], bank[1][0][:, 2 * P:3 * P]))
            assert count[0] == PREP_COPIED
            step(dve.tensor_scalar(w10s[:, :], w10T[:, :], cols[:, R_LN1W:R_LN1W + 1], None, ALU.mult))
            step(dve.tensor_scalar(w20s[:, :], w20T[:, :], cols[:, R_LN2W:R_LN2W + 1], None, ALU.mult))
            step(dve.tensor_scalar(bq_s[:, :], cols[:, R_BQ:R_BQ + 1], QK_SCALE, None, ALU.mult))
            dve.wait_ge(prep_pe, 2)
            step(dve.tensor_tensor(bias_row[:, :, :], bank[1][1][0:1, 0:3 * P].rearrange("a (b f) -> a b f", b=3),
                                   bias_in[:, :, :], ALU.add))
            for whole, rest, rest2, parts in (
                    (bias_row[:, :, :], bias_rest[:, :, :], bias_rest2[:, :, :], [bias_hi[:, j, :, :] for j in range(3)]),
                    (vec[:, :], vec_rest[:, :], vec_rest2[:, :], [vec_parts[:, j, :] for j in range(3)])):
                step(dve.tensor_copy(parts[0], whole))
                step(dve.tensor_tensor(rest, whole, parts[0], ALU.subtract))
                step(dve.tensor_copy(parts[1], rest))
                step(dve.tensor_tensor(rest2, rest, parts[1], ALU.subtract))
                step(dve.tensor_copy(parts[2], rest2))
            step(dve.memset(base[:, :], 0.0))
            assert count[0] == PREP_END

            def norm_stats(phase, i, k, lane, src, to):
                for t in range(TILES):
                    last = dve.bn_stats(bn[lane][:, t, :], src(t))
                last.then_inc(stats[lane], 1)
                dve.wait_ge(stats[lane], stats.nth(phase, i, k))
                dve.sem_inc(passed, 1)
                for t in range(TILES):
                    last = dve.bn_aggr(to(t), bn[lane][:, t, :])
                last.then_inc(mean_var[lane], 1)

            def norm_apply(phase, i, k, lane, src, mean, deviation):
                dve.wait_ge(rstd[lane], rstd.nth(phase, i, k))
                for t in range(TILES):
                    last = dve.tensor_scalar(z[lane][:, t, :], src(t), mean(t), deviation(t), ALU.subtract, ALU.mult)
                last.then_inc(normed[lane], 1)

            def ln_stats(phase, i, k, lane, src):
                norm_stats(phase, i, k, lane, src, lambda t: mv[lane][:, t, :])

            def ln_apply(phase, i, k, lane, src):
                norm_apply(phase, i, k, lane, src, lambda t: mv[lane][:, t, 0:1], lambda t: rstd_t[lane][:, t:t + 1])

            def gate_stats(phase, i, lane):
                norm_stats(phase, i, "gate", lane, lambda t: y_out[lane][:, t, 0:P],
                           lambda t: y_out[lane][:, t, MEAN:RSTD + 1])

            def gate_apply(phase, i, lane):
                norm_apply(phase, i, "gate", lane, lambda t: y_out[lane][:, t, 0:P],
                           lambda t: y_out[lane][:, t, MEAN:MEAN + 1], lambda t: y_out[lane][:, t, RSTD:RSTD + 1])

            def after(phase, i, lane, event):
                dve.wait_ge(vector[lane], vector.nth(phase, i, event))
                dve.sem_inc(passed, 1)

            def done(lane, ins):
                ins.then_inc(vector[lane], 1)

            def pick(phase, i, lane):
                dve.wait_ge(product[lane], product.nth(phase, i, "logits"))
                done(lane, dve.tensor_copy(logit[lane][:, :, :], bank[lane][1][:, 0:TILES * EXPERTS]
                                           .rearrange("p (t e) -> p t e", t=TILES)))
                after(phase, i, lane, "logit")
                for t in range(TILES):
                    last = dve.max(top[lane][:, t, :], logit[lane][:, t, :])
                done(lane, last)
                after(phase, i, lane, "top")
                done(lane, dve.tensor_tensor(ediff[lane][:, :, :], top[lane][:, :, :],
                                             top[lane][:, :, 0:1].to_broadcast((P, TILES, EXPERTS)), ALU.subtract))
                for t in range(TILES):
                    last = dve.max_index(top_i[lane][:, t, :], top[lane][:, t, :], logit[lane][:, t, :])
                done(lane, last)
                after(phase, i, lane, "index")
                if phase == "gnn1":
                    done(lane, dve.tensor_copy(idx[lane][:, :, :], top_i[lane][:, :, 0:2]))
                else:
                    done(lane, dve.tensor_copy(cls[lane][:, :], top_i[lane][:, :, 0]))

            def weigh(phase, i, lane):
                n, two = CLASSES[phase], phase == "gnn1"
                dve.wait_ge(activated[lane], activated.nth(phase, i, "gate"))
                dve.sem_inc(passed, 1)
                done(lane, dve.tensor_scalar(t_inv[lane][:, :, :], t_half[lane][:, :, :], -1.0, 1.0, ALU.mult, ALU.add))
                if two:
                    after(phase, i, lane, "idx")
                    i0, i1 = idx[lane][:, :, 0], idx[lane][:, :, 1]
                    dve.tensor_tensor(flip[lane][:, :], i0, i1, ALU.is_gt)
                    dve.tensor_tensor(pair[lane][:, :, 0], i0, i1, ALU.min)
                    done(lane, dve.tensor_tensor(pair[lane][:, :, 1], i0, i1, ALU.max))
                    after(phase, i, lane, "pair")
                    done(lane, dve.scalar_tensor_tensor(cls[lane][:, :], pair[lane][:, :, 0], float(EXPERTS),
                                                        pair[lane][:, :, 1], ALU.mult, ALU.add))
                after(phase, i, lane, "class" if two else "inv")
                done(lane, dve.tensor_tensor(onehot[lane][:, :, 0:n], iota_c[:, :, 0:n],
                                             cls[lane][:, :].unsqueeze(2).to_broadcast((P, TILES, n)), ALU.is_equal))
                done(lane, dve.reciprocal(t_inv[lane][:, :, :], t_inv[lane][:, :, :]))
                after(phase, i, lane, "recip")
                done(lane, dve.scalar_tensor_tensor(ediff[lane][:, :, :], t_half[lane][:, :, :], 1.0,
                                                    t_inv[lane][:, :, :], ALU.add, ALU.mult))
                after(phase, i, lane, "ex")
                done(lane, dve.tensor_reduce(gsum[lane][:, :], ediff[lane][:, :, :], AX.X, ALU.add))
                after(phase, i, lane, "sum")
                if not two:
                    done(lane, dve.reciprocal(y_out[lane][:, :, G0], gsum[lane][:, :]))
                    return
                done(lane, dve.reciprocal(p0[lane][:, :], gsum[lane][:, :]))
                after(phase, i, lane, "p0")
                done(lane, dve.tensor_tensor(p1[lane][:, :], ediff[lane][:, :, 1], p0[lane][:, :], ALU.mult))
                after(phase, i, lane, "p1")
                done(lane, dve.tensor_tensor(pdiff[lane][:, :], p1[lane][:, :], p0[lane][:, :], ALU.subtract))
                after(phase, i, lane, "pdiff")
                done(lane, dve.tensor_tensor(swap[lane][:, :], pdiff[lane][:, :], flip[lane][:, :], ALU.mult))
                after(phase, i, lane, "swap")
                dve.tensor_tensor(y_out[lane][:, :, G0], p0[lane][:, :], swap[lane][:, :], ALU.add)
                done(lane, dve.tensor_tensor(y_out[lane][:, :, G1], p1[lane][:, :], swap[lane][:, :], ALU.subtract))

            def slots(phase, i, lane):
                n = CLASSES[phase]
                rank_v = ranks[lane][:, 0:TILES * n].rearrange("p (t c) -> p t c", t=TILES)
                dve.wait_ge(product[lane], product.nth(phase, i, "ranks"))
                if lane:
                    dve.wait_ge(vector[lane - 1], vector.nth(phase, i, "base"))
                else:
                    dve.wait_ge(vector[NL - 1], vector.before(phase, i, "base"))
                dve.sem_inc(passed, 1)
                done(lane, dve.tensor_tensor(rank_v, bank[lane][0][:, 0:TILES * n]
                                             .rearrange("p (t c) -> p t c", t=TILES),
                                             base[:, 0:n].unsqueeze(1).to_broadcast((P, TILES, n)), ALU.add))
                after(phase, i, lane, "rank_all")
                done(lane, dve.tensor_tensor(base[:, 0:n], base[:, 0:n],
                                             bank[lane][0][:, TILES * 64:TILES * 64 + n], ALU.add))
                done(lane, dve.tensor_tensor(rank_v, rank_v, onehot[lane][:, :, 0:n], ALU.mult))
                after(phase, i, lane, "rank_own")
                done(lane, dve.tensor_reduce(rank[lane][:, :], rank_v, AX.X, ALU.add))
                after(phase, i, lane, "rank")
                dve.wait_ge(pooled[lane], pooled.before(phase, i, "numbered"))
                dve.sem_inc(passed, 1)
                done(lane, dve.scalar_tensor_tensor(slot[lane][:, :], cls[lane][:, :], float(tokens),
                                                    rank[lane][:, :], ALU.mult, ALU.add))

            planned = [0]

            def plan(phase):
                n, ex = CLASSES[phase], "exp" + phase[-1]
                nb = blocks[ex]
                at = 0 if phase == "gnn0" else 3

                def step(ins):
                    planned[0] += 1
                    ins.then_inc(plan_dve, 1)
                    dve.wait_ge(plan_dve, planned[0])

                for lane in LANES:
                    dve.wait_ge(vector[lane], vector.end(phase))
                planned[0] += 1
                dve.sem_inc(plan_dve, 1)
                dve.wait_ge(plan_pe, at + 1)
                step(dve.tensor_scalar(cnt_i[0:n, :], bank[0][0][0:n, 0:1], float(P - 1), None, ALU.add))
                step(dve.tensor_scalar(cnt_s[0:n, :], cnt_i[0:n, :], 7, None, ALU.arith_shift_right))
                step(dve.tensor_copy(nblk[0:n, :], cnt_s[0:n, :]))
                dve.wait_ge(plan_pe, at + 2)
                step(dve.tensor_copy(ends[0:n, :], bank[0][1][0:n, 0:1]))
                step(dve.tensor_scalar(past[0:n, 0:nb], iota_b[0:n, 0:nb], ends[0:n, :], None, ALU.is_ge))
                dve.wait_ge(plan_pe, at + 3)
                step(dve.tensor_copy(b_cls[:, 0:nb], bank[1][0][0:1, 0:nb]))
                step(dve.tensor_tensor(b_off[:, 0:nb], iota_b[0:1, 0:nb], bank[1][1][0:1, 0:nb], ALU.subtract))
                step(dve.tensor_scalar(b_tmp[:, 0:nb], b_off[:, 0:nb], float(P), None, ALU.mult))
                step(dve.scalar_tensor_tensor(t_off[ex][:, 0:nb], b_cls[:, 0:nb], float(tokens), b_tmp[:, 0:nb],
                                              ALU.mult, ALU.add))
                if phase == "gnn0":
                    step(dve.tensor_scalar(t_lo[ex][:, 0:nb], b_cls[:, 0:nb], float(n - 1), None, ALU.min))
                    step(dve.memset(base[:, :], 0.0))
                else:
                    step(dve.tensor_scalar(b_w[:, 0:nb], b_cls[:, 0:nb], float(n - 1), None, ALU.min))
                    step(dve.tensor_scalar(t_lo[ex][:, 0:nb], b_w[:, 0:nb], 3, None, ALU.arith_shift_right))
                    step(dve.tensor_scalar(t_hi[:, 0:nb], b_w[:, 0:nb], EXPERTS - 1, None, ALU.bitwise_and))
                assert planned[0] == sum(PLAN_STEPS[g] for g in ("gnn0", "gnn1")[:1 + (phase == "gnn1")])

            def exp(phase):
                def z_block(i, r):
                    for lane in LANES:
                        x_row = row_in[lane][r]
                        dve.wait_ge(gathered[lane], gathers(phase, i, r))
                        dve.tensor_scalar(zb[lane][r], x_row[:, 0:P], x_row[:, MEAN:MEAN + 1], x_row[:, RSTD:RSTD + 1],
                                          ALU.subtract, ALU.mult).then_inc(normed[lane], 1)

                def zT_block(i, r):
                    for lane in LANES:
                        dve.wait_ge(transposed[lane], transposed.nth(phase, i, f"z{r}"))
                        dve.tensor_copy(zbT[lane][r], bank[lane][0][:, 0:P]).then_inc(copied[lane], 1)

                def out_block(i, r):
                    two = phase == "exp1"
                    for lane in LANES:
                        x_row = row_in[lane][r]
                        dve.wait_ge(product[lane], product.nth(phase, i, f"y{r}"))
                        dve.scalar_tensor_tensor((part if two else yb)[lane][r], bank[lane][0][:, P:2 * P],
                                                 x_row[:, G0:G0 + 1], x_row[:, 0:P], ALU.mult, ALU.add)\
                            .then_inc(vector[lane], 1)
                        if two:
                            dve.wait_ge(vector[lane], vector.nth(phase, i, f"part{r}"))
                            dve.scalar_tensor_tensor(yb[lane][r], bank[lane][0][:, 2 * P:3 * P], x_row[:, G1:G1 + 1],
                                                     part[lane][r], ALU.mult, ALU.add).then_inc(vector[lane], 1)

                def step(i, r):
                    out_block(i, r)
                    for j, q in later(phase, i, r, 2):
                        zT_block(j, q)
                    for j, q in later(phase, i, r, NR):
                        z_block(j, q)

                z_block(0, 0)
                z_block(0, 1)
                zT_block(0, 0)
                z_block(0, 2)
                zT_block(0, 1)
                rounds(phase, dve, step)

            def gate_step(phase, stage, i, lane):
                if stage == "gate_apply":
                    gate_apply(phase, i, lane)
                elif stage == "pick":
                    pick(phase, i, lane)
                elif stage == "weigh":
                    weigh(phase, i, lane)
                elif stage == "slots":
                    slots(phase, i, lane)

            def x_tile(lane):
                return lambda t: x_in[lane][:, t, :]

            def gnn0_step(stage, i, lane):
                if stage == "ln0_stats":
                    dve.wait_ge(x_loaded[lane], x_loaded.nth("gnn0", i, "x"))
                    ln_stats("gnn0", i, "0", lane, x_tile(lane))
                elif stage == "ln0_apply":
                    ln_apply("gnn0", i, "0", lane, x_tile(lane))
                elif stage == "qk_v_copy":
                    dve.wait_ge(product[lane], product.nth("gnn0", i, "v"))
                    dve.tensor_copy(v[lane], tiles_of(bank[lane][1])).then_inc(vector[lane], 1)
                elif stage == "max":
                    dve.wait_ge(product[lane], product.nth("gnn0", i, "scores"))
                    dve.tensor_reduce(far[lane][:, 0, :], tiles_of(bank[lane][1]), AX.X, ALU.max, negate=True)\
                        .then_inc(vector[lane], 1)
                elif stage == "prob_turn":
                    dve.wait_ge(activated[lane], activated.nth("gnn0", i, "prob"))
                    dve.reciprocal(rden[lane][:, :, 0], den[lane][:, :]).then_inc(vector[lane], 1)
                elif stage == "attention":
                    dve.wait_ge(product[lane], product.nth("gnn0", i, "mixed"))
                    dve.wait_ge(vector[lane], vector.nth("gnn0", i, "rden"))
                    dve.tensor_tensor(hn[lane][:, :, :], tiles_of(bank[lane][1]),
                                      rden[lane][:, :, 0:1].to_broadcast((P, TILES, P)), ALU.mult)\
                        .then_inc(vector[lane], 1)
                elif stage == "swish1":
                    dve.wait_ge(activated[lane], activated.nth("gnn0", i, "th0"))
                    dve.scalar_tensor_tensor(sw[lane], th[lane], 1.0, hn[lane][:, :, :], ALU.add, ALU.mult)\
                        .then_inc(vector[lane], 1)
                    dve.wait_ge(vector[lane], vector.nth("gnn0", i, "sw0"))
                    ln_stats("gnn0", i, "1", lane, lambda t: sw[lane][:, t, :])
                elif stage == "swish2":
                    dve.wait_ge(activated[lane], activated.nth("gnn0", i, "th1"))
                    dve.scalar_tensor_tensor(sw[lane], th[lane], 1.0, tiles_of(bank[lane][1]), ALU.add, ALU.mult)\
                        .then_inc(vector[lane], 1)
                    dve.wait_ge(vector[lane], vector.nth("gnn0", i, "sw1"))
                    ln_stats("gnn0", i, "2", lane, lambda t: sw[lane][:, t, :])
                elif stage in ("ln1_apply", "ln2_apply"):
                    ln_apply("gnn0", i, stage[2], lane, lambda t: sw[lane][:, t, :])
                elif stage == "ln3_stats":
                    dve.wait_ge(product[lane], product.nth("gnn0", i, "h2"))
                    ln_stats("gnn0", i, "3", lane, lambda t: bank[lane][1][:, t * P:(t + 1) * P])
                elif stage == "ln3_apply":
                    ln_apply("gnn0", i, "3", lane, lambda t: bank[lane][1][:, t * P:(t + 1) * P])
                elif stage == "gate_stats":
                    dve.wait_ge(pooled[lane], pooled.nth("gnn0", i, "y"))
                    gate_stats("gnn0", i, lane)
                else:
                    gate_step("gnn0", stage, i, lane)

            dve.wait_ge(consts, CONSTS)
            staggered("gnn0", dve, gnn0_step)
            plan("gnn0")
            enter(dve, "exp0")
            exp("exp0")
            enter(dve, "gnn1")
            def gnn1_step(stage, i, lane):
                if stage == "ln0_stats":
                    dve.wait_ge(x_loaded[lane], x_loaded.nth("gnn1", i, "x"))
                    ln_stats("gnn1", i, "0", lane, x_tile(lane))
                elif stage == "ln0_apply":
                    ln_apply("gnn1", i, "0", lane, x_tile(lane))
                elif stage == "v_copy":
                    dve.wait_ge(product[lane], product.nth("gnn1", i, "v"))
                    dve.tensor_copy(v_one[lane][:, :, :, 0:DK],
                                    bank[lane][1][:, :].rearrange("p (t h d) -> p t h d", t=TILES, h=HEADS))\
                        .then_inc(vector[lane], 1)
                elif stage in ("shift01", "shift23"):
                    for h in (int(stage[-2]), int(stage[-1])):
                        dve.wait_ge(product[lane], product.nth("gnn1", i, f"scores{h}"))
                        dve.tensor_reduce(far[lane][:, h, :], tiles_of(bank[lane][h % 2]), AX.X, ALU.max)\
                            .then_inc(vector[lane], 1)
                        dve.wait_ge(vector[lane], vector.nth("gnn1", i, f"max{h}"))
                        dve.tensor_tensor(prob[lane][:, h, :, :], tiles_of(bank[lane][h % 2]),
                                          far[lane][:, h, :].unsqueeze(2).to_broadcast((P, TILES, P)), ALU.subtract)\
                            .then_inc(vector[lane], 1)
                elif stage == "attention":
                    dve.wait_ge(product[lane], product.nth("gnn1", i, "mixed"))
                    for half in range(2):
                        mix = bank[lane][half][:, 0:2 * HEADS * (DK + 1)].rearrange("p (t h d) -> p t h d", t=2, h=HEADS)
                        last = dve.reciprocal(rden[lane][:, 2 * half:2 * half + 2, :], mix[:, :, :, DK])
                    last.then_inc(vector[lane], 1)
                    dve.wait_ge(vector[lane], vector.nth("gnn1", i, "rden"))
                    for half in range(2):
                        mix = bank[lane][half][:, 0:2 * HEADS * (DK + 1)].rearrange("p (t h d) -> p (t h) d", t=2, h=HEADS)
                        last = dve.tensor_tensor(
                            hn[lane][:, 2 * half:2 * half + 2, :].rearrange("p t (h d) -> p (t h) d", h=HEADS),
                            mix[:, :, 0:DK],
                            rden[lane][:, 2 * half:2 * half + 2, :].rearrange("p t h -> p (t h)").unsqueeze(2)
                            .to_broadcast((P, 2 * HEADS, DK)), ALU.mult)
                    last.then_inc(vector[lane], 1)
                elif stage == "residual":
                    dve.wait_ge(product[lane], product.nth("gnn1", i, "h"))
                    dve.wait_ge(stored[lane], stored.before("gnn1", i, "y"))
                    dve.scalar_tensor_tensor(y_out[lane][:, :, 0:P], tiles_of(bank[lane][1]), 0.0, x_in[lane][:, :, :],
                                             ALU.max, ALU.add).then_inc(vector[lane], 1)
                    dve.wait_ge(vector[lane], vector.nth("gnn1", i, "y"))
                    gate_stats("gnn1", i, lane)
                else:
                    gate_step("gnn1", stage, i, lane)

            staggered("gnn1", dve, gnn1_step)
            plan("gnn1")
            enter(dve, "exp1")
            exp("exp1")


CONSTS = 17 + 5 * NL + 8
PREP_COPIED = 5
PREP_END = 20
PLAN_STEPS = {"gnn0": 12, "gnn1": 13}


def kernel(**inputs):
    import numpy as np
    import concourse.bacc as bacc
    from concourse.bass_utils import run_bass_kernel_spmd

    nc = bacc.Bacc("TRN2", target_bir_lowering=False, num_devices=1)
    arrays, aps = {}, {}
    for name in ["x", "adj"] + WEIGHTS:
        a = np.ascontiguousarray(inputs[name])
        arrays[f"in_{name}"] = a
        aps[name] = nc.dram_tensor(f"in_{name}", a.shape, mybir.dt.from_np(a.dtype), kind="ExternalInput").ap()
    out = nc.dram_tensor("out", inputs["x"].shape, F32, kind="ExternalOutput").ap()
    build(nc, aps["x"], aps["adj"], {n: aps[n] for n in WEIGHTS}, out)
    r = run_bass_kernel_spmd(nc, [arrays], core_ids=[0])
    return r.results[0]["out"]
```

```python
import math
from contextlib import ExitStack

import concourse.bass as bass
from concourse import mybir

F32 = mybir.dt.float32
BF16 = mybir.dt.bfloat16
I32 = mybir.dt.int32
U32 = mybir.dt.uint32
ALU = mybir.AluOpType
ACT = mybir.ActivationFunctionType
AX = mybir.AxisListType

P = 128
TILES = 4
W = TILES * P
NL = 4
LANES = range(NL)
NR = 4
ROUNDS = range(NR)
EPS = 1e-5
EXPERTS = 8
HID = 512
C = HID // P
HALF = HID // 2
HEADS = 4
DK = P // HEADS
QK_SCALE = 1.0 / math.sqrt(DK + 1e-09)
ROW = P + 4
MEAN, RSTD, G0, G1 = P, P + 1, P + 2, P + 3
CLASSES = {"gnn0": EXPERTS, "gnn1": EXPERTS * EXPERTS}
CLASS_BITS = 6
USED = {"gnn0": EXPERTS, "gnn1": EXPERTS * (EXPERTS - 1) // 2}

WEIGHTS = [
    "L0_gnn_Wq", "L0_gnn_Wk", "L0_gnn_Wv", "L0_gnn_ln1_w", "L0_gnn_ln1_b", "L0_gnn_W1", "L0_gnn_b1",
    "L0_gnn_ln2_w", "L0_gnn_ln2_b", "L0_gnn_W2", "L0_gnn_b2", "L0_gnn_lnf_w", "L0_gnn_lnf_b",
    "L0_ffn_W1", "L0_ffn_b1", "L0_ffn_Wg", "L0_ffn_bg", "L0_ffn_Wd", "L0_ffn_bd",
    "L1_gnn_Wq", "L1_gnn_bq", "L1_gnn_Wk", "L1_gnn_bk", "L1_gnn_Wv", "L1_gnn_bv", "L1_gnn_Wo", "L1_gnn_bo",
    "L1_ffn_gate_w", "L1_ffn_gate_b", "L1_ffn_W1", "L1_ffn_b1", "L1_ffn_W2", "L1_ffn_b2",
]

RANKING = ("rank_all", "base", "rank_own", "rank", "slot")
GATE0 = ("logit", "top", "diff", "index", "class", "inv", "onehot", "recip", "ex", "sum", "weights") + RANKING
GATE1 = ("logit", "top", "diff", "index", "idx", "inv", "pair", "class", "onehot", "recip", "ex", "sum", "p0", "p1",
         "pdiff", "swap", "weights") + RANKING
EVENTS = {
    "x_loaded": dict(gnn0=("x",), exp0=("ids0", "ids1", "ids2", "ids3"), gnn1=("x",), exp1=("ids0", "ids1", "ids2", "ids3")),
    "adj_loaded": dict(gnn0=("adj",), gnn1=("adj",)),
    "stored": dict(gnn0=("y",), gnn1=("y",)),
    "transposed": dict(gnn0=("xn", "prob", "z1", "z2", "gate"), exp0=("z0", "z1", "z2", "z3"),
                       gnn1=("xn", "prob0", "prob1", "prob2", "prob3", "o", "gate"), exp1=("z0", "z1", "z2", "z3")),
    "copied": dict(gnn0=("xn", "prob", "z1", "z2", "gate"), exp0=("z0", "z1", "z2", "z3"),
                   gnn1=("xn", "prob0", "prob1", "prob2", "prob3", "o", "gate"), exp1=("z0", "z1", "z2", "z3")),
    "product": dict(gnn0=("qk", "v", "scores", "mixed", "h1", "h2", "hid0", "hid1", "hid2", "hid3", "logits", "ranks"),
                    exp0=("hid0", "y0", "hid1", "y1", "hid2", "y2", "hid3", "y3"),
                    gnn1=("q", "k", "v", "scores0", "scores1", "scores2", "scores3", "mixed", "h", "logits", "ranks"),
                    exp1=("hid0", "y0", "hid1", "y1", "hid2", "y2", "hid3", "y3")),
    "activated": dict(gnn0=("qk", "v", "prob", "th0", "th1", "hid0", "hid1", "hid2", "hid3", "gate"),
                      exp0=("hid0", "hid1", "hid2", "hid3"),
                      gnn1=("q", "k", "v", "prob0", "prob1", "prob2", "prob3", "gate"), exp1=("hid0", "hid1", "hid2", "hid3")),
    "stats": dict(gnn0=("0", "1", "2", "3", "gate"), gnn1=("0", "gate")),
    "mean_var": dict(gnn0=("0", "1", "2", "3", "gate"), gnn1=("0", "gate")),
    "var_eps": dict(gnn0=("0", "1", "2", "3", "gate"), gnn1=("0", "gate")),
    "rstd": dict(gnn0=("0", "1", "2", "3", "gate"), gnn1=("0", "gate")),
    "normed": dict(gnn0=("0", "1", "2", "3", "gate"), exp0=("z0", "z1", "z2", "z3"), gnn1=("0", "gate"),
                   exp1=("z0", "z1", "z2", "z3")),
    "pooled": dict(gnn0=("mask", "kept"), gnn1=("mask", "mask_self")),
    "up_copied": dict(exp1=("up0", "up1", "up2", "up3")),
    "counted_on": dict(gnn0=("numbers",), gnn1=("numbers",)),
    "vector": dict(gnn0=("max", "rden", "hn", "sw0", "sw1", "y") + GATE0,
                   exp0=("out0", "out1", "out2", "out3"),
                   gnn1=("max0", "max1", "max2", "max3", "rden", "hn", "y")
                   + GATE1,
                   exp1=("part0", "out0", "part1", "out1", "part2", "out2", "part3", "out3")),
}
PHASES = ("gnn0", "exp0", "gnn1", "exp1")

STAGES = {
    "gnn0": {
        "ln0_stats": 0, "mask": 0, "ln0_rstd": 6, "keep": 10, "ln0_apply": 12, "xn_turn": 18, "load": 22,
        "xn_copy": 27, "qk_v": 31, "qk_copy": 40, "v_copy": 44, "scores": 48, "max": 56, "prob": 64,
        "prob_turn": 71, "rden": 71, "prob_copy": 75, "mix": 79, "attention": 88, "tanh1": 92, "swish1": 100,
        "ln1_rstd": 109, "ln1_apply": 115, "z1_turn": 122, "z1_copy": 126, "linear1": 138, "tanh2": 144,
        "swish2": 148, "ln2_rstd": 157, "ln2_apply": 174, "z2_turn": 182, "z2_copy": 189, "linear2": 193,
        "ln3_stats": 203, "ln3_rstd": 209, "ln3_scale": 209, "residual": 215, "gate_stats": 226, "gate_rstd": 232,
        "gate_apply": 240, "gate_turn": 250, "gate_copy": 254, "hidden01": 258, "gelu01": 267, "hidden23": 292,
        "gelu23": 301, "logits": 310, "pick": 328, "gate_tanh": 340, "classify": 346, "ranks": 356, "weigh": 359,
        "store": 363, "slots": 363, "scatter0": 368, "scatter1": 381, "scatter2": 387, "scatter3": 393,
        "number": 413,
    },
    "gnn1": {
        "ln0_stats": 0, "mask": 0, "ln0_rstd": 6, "mask_self": 10, "ln0_apply": 12, "xn_turn": 18, "xn_copy": 27,
        "qk": 31, "q_copy": 44, "k_copy": 48, "values": 48, "v_copy": 53, "scores01": 57, "max0": 72, "max1": 76,
        "prob0": 76, "prob1": 82, "scores23": 88, "max2": 98, "max3": 102, "prob2": 102, "prob3": 108,
        "prob_turn0": 108, "prob_turn1": 114, "prob_copy0": 114, "prob_copy1": 118, "prob_turn2": 119,
        "prob_turn3": 123, "prob_copy2": 128, "prob_copy3": 132, "mix": 136, "attention": 152, "o_turn": 164,
        "o_copy": 168, "linear": 178, "residual": 184, "gate_stats": 188, "load": 188, "gate_rstd": 194,
        "gate_apply": 200, "gate_turn": 218, "gate_copy": 222, "logits": 242, "pick": 246, "gate_tanh": 256,
        "classify": 260, "ranks": 269, "weigh": 291, "store": 297, "slots": 297, "scatter0": 304, "scatter1": 309,
        "scatter2": 314, "scatter3": 323, "number": 338,
    },
}
PERIOD = {"gnn0": 336, "gnn1": 272}
CREDIT = 32


def bf16_parts(value):
    import numpy as np
    parts, rest = [], np.float32(value)
    for _ in range(3):
        part = (rest.view(np.uint32) & np.uint32(0xFFFF0000)).view(np.float32)
        parts.append(float(part))
        rest = np.float32(rest - part)
    return parts


def build(nc, x, adj, w, out):
    batches = x.shape[0]
    tokens = batches * P
    groups = batches // TILES
    blocks = {}
    for phase, gate in (("exp0", "gnn0"), ("exp1", "gnn1")):
        need = tokens // P + USED[gate] - 1
        blocks[phase] = -(-need // (NR * NL)) * NR * NL
    iters = {"gnn0": groups // NL, "gnn1": groups // NL,
             "exp0": blocks["exp0"] // (NR * NL), "exp1": blocks["exp1"] // (NR * NL)}
    ctx = ExitStack()
    with ctx:
        def sb(name, shape, dt=F32):
            return ctx.enter_context(nc.sbuf_tensor(name, shape, dt))

        def lane_sb(name, shape, dt=F32):
            return [sb(f"{name}_{lane}", shape, dt) for lane in LANES]

        def sem(name):
            return ctx.enter_context(nc.semaphore(name))

        class Signal:

            def __init__(self, name, step=1):
                self.sems = [sem(f"{name}_{lane}") for lane in LANES]
                self.events, self.step, self.base, total = EVENTS[name], step, {}, CREDIT
                for phase in PHASES:
                    self.base[phase] = total
                    total += len(self.events.get(phase, ())) * iters[phase]

            def __getitem__(self, lane):
                return self.sems[lane]

            def nth(self, phase, i, event):
                names = self.events[phase]
                return (i * len(names) + (self.base[phase] + names.index(event) + 1)) * self.step

            def before(self, phase, i, event):
                names = self.events[phase]
                return (i * len(names) + (self.base[phase] + names.index(event) + 1 - len(names))) * self.step

            def end(self, phase):
                return (self.base[phase] + len(self.events.get(phase, ())) * iters[phase]) * self.step

        def dram(name, shape, dt=F32):
            return nc.dram_tensor(name, shape, dt, kind="Internal").ap()

        rows1, rows3 = dram("rows1", (tokens, ROW)), dram("rows3", (tokens, ROW))
        x2 = dram("x2", (tokens, P))
        out_rows = out.rearrange("b p f -> (b p) f")
        ids_len = {g: CLASSES[g] * tokens + blocks["exp" + g[-1]] * P for g in CLASSES}
        ids = {g: dram(f"ids_{g}", (ids_len[g], 1), I32) for g in CLASSES}
        row_parts = dram("row_parts", (3, 3, P), BF16)
        out_bias = {"exp0": dram("bd_parts", (3, EXPERTS, P), BF16), "exp1": dram("b2_parts", (3, EXPERTS, P), BF16)}

        def group(t):
            return t.rearrange("(g t p) f -> g p t f", t=TILES, p=P)

        x_g, x2_g = group(x.rearrange("b p f -> (b p) f")), group(x2)
        adj_g = group(adj.rearrange("b p f -> (b p) f"))
        rows_g = {"gnn0": group(rows1), "gnn1": group(rows3)}

        ident = sb("ident", [P, P])
        off_diag = sb("off_diag", [P, P], BF16)
        far0 = sb("far0", [P, 3, P], BF16)
        far1 = sb("far1", [P, P], BF16)
        earlier = sb("earlier", [P, P], BF16)
        all_ones = sb("all_ones", [P, P], BF16)
        upto = sb("upto", [64, 64])
        ones_col = sb("ones_col", [64, 1])
        ones3 = sb("ones3", [3, P], BF16)
        ones1 = sb("ones1", [1, P])
        half_neg = sb("half_neg", [P, TILES])
        eps_tile, eps4_tile = sb("eps_tile", [P, TILES]), sb("eps4_tile", [P, TILES])
        iota_c = sb("iota_c", [P, TILES, 64])
        NB = max(blocks.values())
        iota_b = sb("iota_b", [64, NB])
        empty_slot = sb("empty_slot", [P, 260], I32)
        number_step = sb("number_step", [P, TILES], I32)
        NCOL = 7 + C + 2 * EXPERTS
        R_LN1W, R_LN1B, R_LN2W, R_LN2B, R_BQ, R_BK, R_BV, R_L0B1 = range(8)
        R_L1B1 = R_L0B1 + C
        rows = sb("rows", [NCOL, P])
        cols = sb("cols", [P, NCOL])
        wq0, wk0, wv0 = sb("wq0", [P, P]), sb("wk0", [P, P]), sb("wv0", [P, P])
        w10, w20 = sb("w10", [P, P]), sb("w20", [P, P])
        qk0 = sb("qk0", [P, P])
        wv0T, w10T, w20T = sb("wv0T", [P, P]), sb("w10T", [P, P]), sb("w20T", [P, P])
        w10s, w20s = sb("w10s", [P, P]), sb("w20s", [P, P])
        lnf_w, lnf_b = sb("lnf_w", [P, P]), sb("lnf_b", [P, P])
        bias_hi = sb("bias_hi", [1, 3, 3, P], BF16)
        bias3 = sb("bias3", [3, 3, TILES, P], BF16)
        NV = 2 * EXPERTS
        V_BD, V_B2 = 0, EXPERTS
        vec_parts = sb("vec_parts", [NV, 3, P], BF16)
        wq1, wk1, wv1, wo1 = sb("wq1", [P, P]), sb("wk1", [P, P]), sb("wv1", [P, P]), sb("wo1", [P, P])
        bq_s = sb("bq_s", [P, 1])
        f0_w1 = sb("f0_w1", [P, HID])
        gate_w = {"gnn0": sb("f0_wg", [P, C, EXPERTS]), "gnn1": sb("f1_wg", [P, 1, EXPERTS])}
        gate_b = {"gnn0": sb("f0_bg", [1, TILES, EXPERTS]), "gnn1": sb("f1_bg", [1, TILES, EXPERTS])}

        base = sb("base", [P, 64])
        cnt_i, cnt_s = sb("cnt_i", [64, 1], I32), sb("cnt_s", [64, 1], I32)
        nblk, ends = sb("nblk", [64, 1]), sb("ends", [64, 1])
        b_w = sb("b_w", [1, NB])
        packed = [sb(f"packed_{k}", [1, NB // NL]) for k in range(2)]
        t_off = {p: sb(f"t_off_{p}", [1, NB], I32) for p in ("exp0", "exp1")}
        t_class = {p: sb(f"t_class_{p}", [1, NB // NL], I32) for p in ("exp0", "exp1")}

        x_in = lane_sb("x_in", [P, TILES, P])
        adj_in = lane_sb("adj_in", [P, TILES, P], I32)
        no_edge_all, no_edge1_all = (sb(n, [P, NL * TILES, P], BF16) for n in ("no_edge", "no_edge1"))
        no_edge, no_edge1 = ([t[:, lane * TILES:(lane + 1) * TILES, :] for lane in LANES]
                             for t in (no_edge_all, no_edge1_all))
        x_res = lane_sb("x_res", [P, TILES, P])
        bn = lane_sb("bn", [P, TILES, 6])
        mv = lane_sb("mv", [P, TILES, 2])
        var_eps, rstd_t = lane_sb("var_eps_t", [P, TILES]), lane_sb("rstd_t", [P, TILES])
        z = lane_sb("z", [P, TILES, P])
        zT = lane_sb("zT", [P, W])
        flat_z = [t[:, :, :].rearrange("p t f -> p (t f)") for t in z]
        past = flat_z[0][0:64, 0:NB]
        b_cls, b_off, b_tmp = flat_z[1][0:1, 0:NB], flat_z[2][0:1, 0:NB], flat_z[3][0:1, 0:NB]
        xnT = lane_sb("xnT", [P, W])
        qT, kT = lane_sb("qT", [P, W]), lane_sb("kT", [P, W])
        v_one = lane_sb("v_one", [P, TILES, HEADS, DK + 1])
        far = lane_sb("far", [P, HEADS, TILES])
        prob = lane_sb("prob", [P, HEADS, TILES, P])
        probT_all = sb("probT", [P, NL, HEADS, TILES, P])
        probT = [probT_all[:, lane, :, :, :] for lane in LANES]
        bias_in, bias_row, bias_rest = (prob[0][0:1, h, 0:3, :] for h in range(3))
        bias_rest2 = prob[0][0:1, 3, 0:3, :]
        vec, vec_rest, vec_rest2 = (prob[1][0:NV, h, 0, :] for h in range(3))
        hidden = prob
        v = [t[:, 1, :, :] for t in probT]
        th = [t[:, 2, :, :] for t in probT]
        sw = [t[:, 3, :, :] for t in probT]
        den = lane_sb("den", [P, TILES])
        rden = lane_sb("rden", [P, TILES, HEADS])
        hn = lane_sb("hn", [P, TILES, P])
        y_out = lane_sb("y_out", [P, TILES, ROW])
        logit, top, ediff, t_half, t_inv = (lane_sb(n, [P, TILES, EXPERTS])
                                            for n in ("logit", "top", "ediff", "t_half", "t_inv"))
        top_i = lane_sb("top_i", [P, TILES, 8], U32)
        idx, pair = lane_sb("idx", [P, TILES, 2]), lane_sb("pair", [P, TILES, 2])
        gsum, p0, p1, flip, cls, rank, slot_f = (lane_sb(n, [P, TILES])
                                                 for n in ("gsum", "p0", "p1", "flip", "cls", "rank", "slot_f"))
        pdiff, swap = lane_sb("pdiff", [P, TILES]), lane_sb("swap", [P, TILES])
        slot, number = lane_sb("slot", [P, TILES], I32), lane_sb("number", [P, TILES], I32)
        onehot = lane_sb("onehot", [P, TILES, 64], BF16)
        ranks = [t[:, 0:2, :].rearrange("p a b -> p (a b)") for t in hn]
        row_in = [[sb(f"row_in_{lane}_{r}", [P, ROW]) for r in ROUNDS] for lane in LANES]
        id_in = [[sb(f"id_in_{lane}_{r}", [P, 1], I32) for r in ROUNDS] for lane in LANES]
        zb = [[z[lane][:, r, :] for r in ROUNDS] for lane in LANES]
        zbT = [[zT[lane][:, r * P:(r + 1) * P] for r in ROUNDS] for lane in LANES]
        yb = [[y_out[lane][:, r, 0:P] for r in ROUNDS] for lane in LANES]
        half_all = probT_all[:, 0:2, :, :, :].rearrange("p l h t f -> p (l h t) f")
        w_down0 = half_all
        w_down1 = half_all[:, 0:2 * EXPERTS, :]
        w_up_all = half_all[:, 2 * EXPERTS:4 * EXPERTS, :].rearrange("p (e c) f -> p e (c f)", e=EXPERTS)
        w_up = [[probT_all[:, 2 + r, lane, :, :].rearrange("p t f -> p (t f)") for r in range(2)] + [qT[lane][:, :], kT[lane][:, :]]
                for lane in LANES]
        hb = [[prob[lane][:, r, :, :] for r in ROUNDS] for lane in LANES]
        part = [[hn[lane][:, r, :] for r in ROUNDS] for lane in LANES]
        down_b = no_edge1_all[0:3, 0:EXPERTS, :]

        bank = [[ctx.enter_context(nc.psum_tensor(f"bank{lane}_{b}", [P, W], F32)) for b in range(2)] for lane in LANES]

        def tiles_of(t):
            return t[:, :].rearrange("p (t f) -> p t f", t=TILES)

        passed = sem("wait_passed")
        loaded, consts, prep_pe, prep_dve = (sem(n) for n in ("weights_loaded", "consts_ready", "prep_products",
                                                              "prep_vector_steps"))
        parts_out, parts_in, cleared = sem("bias_parts_written"), sem("bias_parts_read"), sem("lists_cleared")
        plan_pe, plan_dve = sem("plan_products"), sem("plan_vector_steps")
        gathered = [sem(f"rows_gathered_{lane}") for lane in LANES]
        scattered = [sem(f"rows_scattered_{lane}") for lane in LANES]
        numbered = [sem(f"ids_scattered_{lane}") for lane in LANES]

        x_loaded, adj_loaded = Signal("x_loaded", 16), Signal("adj_loaded", 16)
        stored = Signal("stored", 16)
        transposed, copied, product, activated = (Signal(n) for n in ("transposed", "copied", "product", "activated"))
        stats, mean_var, normed = Signal("stats"), Signal("mean_var"), Signal("normed")
        ve_ready, rstd = Signal("var_eps"), Signal("rstd")
        pooled, vector, counted_on = Signal("pooled"), Signal("vector"), Signal("counted_on")
        up_copied = Signal("up_copied")

        def vrow(name):
            return w[name].rearrange("(a p) -> a p", a=1)

        weight_loads = [
            (wq0[:, :], w["L0_gnn_Wq"]), (wk0[:, :], w["L0_gnn_Wk"]), (wv0[:, :], w["L0_gnn_Wv"]),
            (w10[:, :], w["L0_gnn_W1"]), (w20[:, :], w["L0_gnn_W2"]),
            (lnf_w[:, :], vrow("L0_gnn_lnf_w").to_broadcast((P, P))),
            (lnf_b[:, :], vrow("L0_gnn_lnf_b").to_broadcast((P, P))),
            (wq1[:, :], w["L1_gnn_Wq"]), (wk1[:, :], w["L1_gnn_Wk"]), (wv1[:, :], w["L1_gnn_Wv"]),
            (wo1[:, :], w["L1_gnn_Wo"]),
            (rows[R_L0B1:R_L0B1 + C, :], w["L0_ffn_b1"].rearrange("(c p) -> c p", p=P)),
            (rows[R_L1B1:R_L1B1 + 2 * EXPERTS, :], w["L1_ffn_b1"].rearrange("e (c p) -> (e c) p", p=P)),
            (f0_w1[:, :], w["L0_ffn_W1"]),
            (gate_w["gnn0"][:, :, :], w["L0_ffn_Wg"].rearrange("(c p) e -> p c e", p=P)),
            (gate_w["gnn1"][:, 0, :], w["L1_ffn_gate_w"]),
            (vec[V_BD:V_BD + EXPERTS, :], w["L0_ffn_bd"]), (vec[V_B2:V_B2 + EXPERTS, :], w["L1_ffn_b2"]),
        ] + [
            (gate_b[g][:, t, :], w[n].rearrange("(a e) -> a e", a=1))
            for g, n in (("gnn0", "L0_ffn_bg"), ("gnn1", "L1_ffn_gate_b")) for t in range(TILES)
        ] + [
            (rows[r:r + 1, :], vrow(n))
            for r, n in ((R_LN1W, "L0_gnn_ln1_w"), (R_LN1B, "L0_gnn_ln1_b"), (R_LN2W, "L0_gnn_ln2_w"),
                         (R_LN2B, "L0_gnn_ln2_b"), (R_BQ, "L1_gnn_bq"), (R_BK, "L1_gnn_bk"), (R_BV, "L1_gnn_bv"))
        ] + [
            (bias_in[:, j, :], vrow(n)) for j, n in enumerate(("L0_gnn_b1", "L0_gnn_b2", "L1_gnn_bo"))
        ]
        LOADED = 16 * len(weight_loads)
        N_CLEAR = sum(-(-n // P // 260) for n in ids_len.values())

        def enter(eng, phase):
            last = PHASES[PHASES.index(phase) - 1]
            for signal in (x_loaded, adj_loaded, stored, product, copied, activated, vector, pooled, counted_on):
                for lane in LANES:
                    eng.wait_ge(signal[lane], signal.end(last))
            for lane in LANES:
                if last.startswith("gnn"):
                    eng.wait_ge(numbered[lane], numbers(last, iters[last] - 1))
                else:
                    eng.wait_ge(scattered[lane], scatters(last, iters[last] - 1, NR - 1))
            if last.startswith("gnn"):
                eng.wait_ge(plan_dve, sum(n for g, n in PLAN_STEPS.items() if g <= last))

        def numbers(phase, i):
            return (i + (0 if phase == "gnn0" else iters["gnn0"]) + 1) * TILES * 16

        def gathers(phase, i, r):
            return (i * NR + (NR * iters["exp0"] if phase == "exp1" else 0) + r + 1) * 16

        scatters = gathers

        def order(phase):
            stand = []
            for n, (stage, slot) in enumerate(STAGES[phase].items()):
                for lane in LANES:
                    back, at = divmod(slot + lane * PERIOD[phase] // NL, PERIOD[phase])
                    stand.append((at, -back, n, lane, stage))
            return [(-back, stage, lane) for at, back, n, lane, stage in sorted(stand)]

        def stages(phase, i, step):
            for back, stage, lane in order(phase):
                j = i - back
                if not isinstance(j, int) or 0 <= j < iters[phase]:
                    step(stage, j, lane)

        def staggered(phase, eng, step, peeled=0):
            lead = max(back for back, _, _ in order(phase))
            n = iters[phase]
            full = n - peeled if n - peeled > lead else lead
            for i in range(lead):
                stages(phase, i, step)
            if full > lead:
                with eng.Fori(lead, full) as i:
                    stages(phase, i, step)
            for i in range(full, n + lead):
                stages(phase, i, step)

        def classes(eng, phase, i, r):
            return eng.value_load(t_class[phase][0:1, bass.ds(i * NR + r, 1)], min_val=0,
                                  max_val=(1 << (CLASS_BITS * NL)) - 1)

        def experts_of(phase, packed_classes, lane):
            low = packed_classes & (EXPERTS - 1) if lane == 0 else (packed_classes >> (CLASS_BITS * lane)) & (EXPERTS - 1)
            if phase == "exp0":
                return [low]
            return [(packed_classes >> (CLASS_BITS * lane + CLASS_BITS // 2)) & (EXPERTS - 1), low]

        def later(phase, i, r, k):
            j, rr = i + (r + k) // NR, (r + k) % NR
            return [] if isinstance(i, int) and not 0 <= j < iters[phase] else [(j, rr)]

        def rounds(phase, eng, step):
            with eng.Fori(0, iters[phase] - 1) as i:
                for r in ROUNDS:
                    step(i, r)
            for r in ROUNDS:
                step(iters[phase] - 1, r)

        block = ctx.enter_context(nc.Block())

        @block.sync
        def _(sp):
            for signal in (x_loaded, adj_loaded, stored, transposed, copied, product, activated, stats, mean_var,
                           ve_ready, rstd, normed, pooled, vector, counted_on,
                           up_copied):
                for lane in LANES:
                    sp.sem_inc(signal[lane], CREDIT * signal.step)

            def load(phase, src, i, lane):
                sp.wait_ge(normed[lane], normed.before(phase, i, "0"))
                sp.sem_inc(passed, 1)
                if phase == "gnn0":
                    sp.wait_ge(pooled[lane], pooled.before(phase, i, "kept"))
                else:
                    sp.wait_ge(vector[lane], vector.before(phase, i, "y"))
                sp.sem_inc(passed, 1)
                sp.dma_start(x_in[lane][:, :, :], src[i * NL + lane]).then_inc(x_loaded[lane], 16)
                sp.wait_ge(pooled[lane], pooled.before(phase, i, "mask"))
                sp.sem_inc(passed, 1)
                sp.dma_start(adj_in[lane][:, :, :], adj_g[i * NL + lane]).then_inc(adj_loaded[lane], 16)

            def gnn(phase, src):
                n = iters[phase]

                def step(stage, i, lane):
                    if stage == "load" and not (isinstance(i, int) and i == n - 1):
                        load(phase, src, i + 1, lane)
                    if stage == "store":
                        sp.wait_ge(vector[lane], vector.nth(phase, i, "weights"))
                        sp.sem_inc(passed, 1)
                        sp.dma_start(rows_g[phase][i * NL + lane], y_out[lane][:, :, :]).then_inc(stored[lane], 16)

                staggered(phase, sp, step, peeled=1)

            gate_of = {"exp0": "gnn0", "exp1": "gnn1"}

            def number_load(phase, i, r, lane):
                at = sp.value_load(t_off[phase][0:1, bass.ds(i * NR * NL + (r * NL + lane), 1)], min_val=0,
                                   max_val=ids_len[gate_of[phase]] - P)
                if not isinstance(i, int) or i or r:
                    (j, q), = later(phase, i, r, -1)
                    sp.wait_ge(x_loaded[lane], x_loaded.nth(phase, j, f"ids{q}"))
                    sp.sem_inc(passed, 1)
                if not isinstance(i, int) or i:
                    sp.wait_ge(scattered[lane], scatters(phase, i - 1, r))
                    sp.sem_inc(passed, 1)
                sp.dma_start(id_in[lane][r][:, :], ids[gate_of[phase]][bass.ds(at, P), :]).then_inc(x_loaded[lane], 16)

            def exp(phase):
                if phase == "exp0":
                    sp.dma_start(w_down0, w["L0_ffn_Wd"].rearrange("e (c p) f -> p (e c) f", p=P)).then_inc(loaded, 16)
                else:
                    sp.dma_start(w_up_all, w["L1_ffn_W1"].rearrange("e d h -> d e h")).then_inc(loaded, 16)
                    sp.dma_start(w_down1, w["L1_ffn_W2"].rearrange("e (c p) f -> p (e c) f", p=P)).then_inc(loaded, 16)
                sp.dma_start(down_b[:, :, :], out_bias[phase]).then_inc(loaded, 16)
                for r in ROUNDS:
                    for lane in LANES:
                        number_load(phase, 0, r, lane)
                with sp.Fori(1, iters[phase]) as i:
                    for r in ROUNDS:
                        for lane in LANES:
                            number_load(phase, i, r, lane)

            for lane in LANES:
                load("gnn0", x_g, 0, lane)
            for dst, src in weight_loads:
                sp.dma_start(dst, src).then_inc(loaded, 16)

            sp.wait_ge(prep_dve, PREP_END)
            sp.dma_start(row_parts.rearrange("j b f -> (j b f)").rearrange("(a n) -> a n", a=1),
                         bias_hi[:, :, :, :].rearrange("a j b f -> a (j b f)")).then_inc(parts_out, 16)
            for dst, at, n in ((out_bias["exp0"], V_BD, EXPERTS), (out_bias["exp1"], V_B2, EXPERTS)):
                sp.dma_start(dst.rearrange("j e f -> e j f"), vec_parts[at:at + n, :, :]).then_inc(parts_out, 16)
            sp.wait_ge(parts_out, 16 * 3)
            for b in range(3):
                for t in range(TILES):
                    sp.dma_start(bias3[:, b, t, :], row_parts[:, b, :]).then_inc(parts_in, 16)

            gnn("gnn0", x_g)
            enter(sp, "exp0")
            exp("exp0")
            enter(sp, "gnn1")
            for lane in LANES:
                load("gnn1", x2_g, 0, lane)
            gnn("gnn1", x2_g)
            enter(sp, "exp1")
            exp("exp1")

        @block.gpsimd
        def _(pool):
            def fixed(ins):
                ins.then_inc(consts, 1)

            fixed(pool.memset(ident[:, :], 0.0))
            fixed(pool.memset(off_diag[:, :], 1.0))
            fixed(pool.memset(far0[:, :, :], 0.0))
            fixed(pool.memset(far1[:, :], 0.0))
            fixed(pool.memset(earlier[:, :], 1.0))
            fixed(pool.memset(upto[:, :], 1.0))
            fixed(pool.memset(all_ones[:, :], 1.0))
            fixed(pool.memset(ones_col[:, :], 1.0))
            fixed(pool.memset(ones3[:, :], 1.0))
            fixed(pool.memset(ones1[:, :], 1.0))
            fixed(pool.memset(half_neg[:, :], -0.5))
            fixed(pool.memset(eps_tile[:, :], EPS))
            fixed(pool.memset(eps4_tile[:, :], 4 * EPS))
            fixed(pool.memset(empty_slot[:, :], tokens))
            fixed(pool.memset(number_step[:, :], NL * W))
            fixed(pool.iota(iota_c[:, :, :], [[0, TILES], [1, 64]], base=0, channel_multiplier=0,
                            allow_small_or_imprecise_dtypes=True))
            fixed(pool.iota(iota_b[:, :], [[1, NB]], base=0, channel_multiplier=0,
                            allow_small_or_imprecise_dtypes=True))
            for lane in LANES:
                fixed(pool.iota(number[lane][:, :], [[P, TILES]], base=lane * W, channel_multiplier=1))
                fixed(pool.memset(v_one[lane][:, :, :, DK:DK + 1], 1.0))
                fixed(pool.memset(y_out[lane][:, :, :], 0.0))
                for r in ROUNDS:
                    fixed(pool.memset(row_in[lane][r][:, :], 0.0))
            pool.wait_ge(consts, CONSTS - 8)
            fills = [(ident[:, :], 1.0), (off_diag[:, :], 0.0), (far1[:, :], -1e30)]
            fills += [(far0[:, j, :], value) for j, value in enumerate(bf16_parts(-1e9))]
            for tile, fill in fills:
                fixed(pool.affine_select(out=tile, in_=tile, compare_op=ALU.not_equal, fill=fill, base=0,
                                         pattern=[[-1, P]], channel_multiplier=1))
            fixed(pool.affine_select(out=earlier[:, :], in_=earlier[:, :], compare_op=ALU.is_gt, fill=0.0, base=0,
                                     pattern=[[1, P]], channel_multiplier=-1))
            fixed(pool.affine_select(out=upto[:, :], in_=upto[:, :], compare_op=ALU.is_ge, fill=0.0, base=0,
                                     pattern=[[1, 64]], channel_multiplier=-1))

            def rstd_of(phase, lane, i, k, eps, var=None, to=None):
                pool.wait_ge(mean_var[lane], mean_var.nth(phase, i, k))
                pool.tensor_tensor(var_eps[lane][:, :], mv[lane][:, :, 1] if var is None else var, eps[:, :], ALU.add)\
                    .then_inc(ve_ready[lane], 1)
                pool.wait_ge(ve_ready[lane], ve_ready.nth(phase, i, k))
                pool.tensor_tensor(rstd_t[lane][:, :] if to is None else to, var_eps[lane][:, :], half_neg[:, :],
                                   ALU.pow).then_inc(rstd[lane], 1)

            def scatter(phase, i, lane, t):
                if t == 0:
                    pool.wait_ge(vector[lane], vector.nth(phase, i, "slot"))
                    pool.sem_inc(passed, 1)
                pool.indirect_dma_start(ids[phase], bass.IndirectOffsetOnAxis(slot[lane][:, t:t + 1], 0),
                                        number[lane][:, t:t + 1], None).then_inc(numbered[lane], 16)

            def next_numbers(phase, i, lane):
                pool.wait_ge(numbered[lane], numbers(phase, i))
                pool.tensor_tensor(number[lane][:, :], number[lane][:, :], number_step[:, :], ALU.add)\
                    .then_inc(counted_on[lane], 1)

            def mask(phase, i, lane, scores):
                pool.wait_ge(adj_loaded[lane], adj_loaded.nth(phase, i, "adj"))
                pool.wait_ge(product[lane], product.before(phase, i, scores))
                pool.sem_inc(passed, 1)
                pool.tensor_scalar(no_edge[lane], adj_in[lane][:, :, :], 0.0, None, ALU.is_equal)\
                    .then_inc(pooled[lane], 1)

            def gate_rstd(phase, i, lane):
                rstd_of(phase, lane, i, "gate", eps_tile, y_out[lane][:, :, RSTD], y_out[lane][:, :, RSTD])

            def gnn0_step(stage, i, lane):
                if stage == "ln0_rstd":
                    rstd_of("gnn0", lane, i, "0", eps_tile)
                elif stage == "mask":
                    mask("gnn0", i, lane, "scores")
                elif stage == "keep":
                    pool.wait_ge(vector[lane], vector.before("gnn0", i, "y"))
                    pool.wait_ge(x_loaded[lane], x_loaded.nth("gnn0", i, "x"))
                    pool.tensor_tensor(x_res[lane][:, :, :], x_in[lane][:, :, :],
                                       lnf_b[:, :].unsqueeze(1).to_broadcast((P, TILES, P)), ALU.add)\
                        .then_inc(pooled[lane], 1)
                elif stage in ("ln1_rstd", "ln2_rstd"):
                    rstd_of("gnn0", lane, i, stage[2], eps4_tile)
                elif stage == "ln3_rstd":
                    rstd_of("gnn0", lane, i, "3", eps_tile)
                elif stage == "gate_rstd":
                    gate_rstd("gnn0", i, lane)
                elif stage.startswith("scatter"):
                    scatter("gnn0", i, lane, int(stage[-1]))
                elif stage == "number":
                    next_numbers("gnn0", i, lane)

            def gnn1_step(stage, i, lane):
                if stage == "ln0_rstd":
                    rstd_of("gnn1", lane, i, "0", eps_tile)
                elif stage == "mask":
                    mask("gnn1", i, lane, "scores3")
                elif stage == "mask_self":
                    pool.wait_ge(pooled[lane], pooled.nth("gnn1", i, "mask"))
                    pool.tensor_tensor(no_edge1[lane], no_edge[lane],
                                       off_diag[:, :].unsqueeze(1).to_broadcast((P, TILES, P)), ALU.mult)\
                        .then_inc(pooled[lane], 1)
                elif stage == "gate_rstd":
                    gate_rstd("gnn1", i, lane)
                elif stage.startswith("scatter"):
                    scatter("gnn1", i, lane, int(stage[-1]))
                elif stage == "number":
                    next_numbers("gnn1", i, lane)

            pool.wait_ge(consts, CONSTS)
            pool.wait_ge(cleared, 16 * N_CLEAR)
            staggered("gnn0", pool, gnn0_step)

            def fetch(phase, i, r, lane):
                pool.wait_ge(x_loaded[lane], x_loaded.nth(phase, i, f"ids{r}"))
                if not isinstance(i, int) or i or r:
                    (j, q), = later(phase, i, r, -1)
                    pool.wait_ge(gathered[lane], gathers(phase, j, q))
                pool.sem_inc(passed, 1)
                pool.indirect_dma_start(row_in[lane][r][:, :], None, {"exp0": rows1, "exp1": rows3}[phase],
                                        bass.IndirectOffsetOnAxis(id_in[lane][r][:, 0:1], 0),
                                        bounds_check=tokens - 1, oob_is_err=False).then_inc(gathered[lane], 16)

            def put_back(phase, i, r, lane):
                pool.wait_ge(vector[lane], vector.nth(phase, i, f"out{r}"))
                pool.sem_inc(passed, 1)
                pool.indirect_dma_start({"exp0": x2, "exp1": out_rows}[phase],
                                        bass.IndirectOffsetOnAxis(id_in[lane][r][:, 0:1], 0), yb[lane][r], None,
                                        bounds_check=tokens - 1, oob_is_err=False).then_inc(scattered[lane], 16)

            def exp(phase):
                for r in range(NR - 1):
                    for lane in LANES:
                        fetch(phase, 0, r, lane)

                def step(i, r):
                    for j, q in later(phase, i, r, NR - 1):
                        for lane in LANES:
                            fetch(phase, j, q, lane)
                    for lane in LANES:
                        put_back(phase, i, r, lane)

                rounds(phase, pool, step)

            enter(pool, "exp0")
            exp("exp0")
            enter(pool, "gnn1")
            for lane in LANES:
                fixed(pool.iota(number[lane][:, :], [[P, TILES]], base=lane * W, channel_multiplier=1))
            pool.wait_ge(consts, CONSTS + NL)
            staggered("gnn1", pool, gnn1_step)
            enter(pool, "exp1")
            exp("exp1")
            for lane in LANES:
                pool.wait_ge(scattered[lane], scatters("exp1", iters["exp1"] - 1, NR - 1))

        @block.tensor
        def _(pe):
            pe.wait_ge(consts, CONSTS)
            pe.wait_ge(loaded, LOADED)
            b0, b1, b2, b3 = bank[0][0], bank[0][1], bank[1][0], bank[1][1]
            pe.transpose(b0[:, 0:NCOL], rows[:, :], ident[0:NCOL, 0:NCOL])
            pe.matmul(b1[:, 0:P], wq0[:, :], wk0[:, :], start=True, stop=True)
            pe.transpose(b2[:, 0:P], wv0[:, :], ident[:, :])
            pe.transpose(b2[:, P:2 * P], w10[:, :], ident[:, :])
            pe.transpose(b2[:, 2 * P:3 * P], w20[:, :], ident[:, :]).then_inc(prep_pe, 1)
            pe.wait_ge(prep_dve, PREP_COPIED)
            pe.matmul(b3[0:1, 0:P], cols[:, R_LN1B:R_LN1B + 1], w10T[:, :], start=True, stop=True)
            pe.matmul(b3[0:1, P:2 * P], cols[:, R_LN2B:R_LN2B + 1], w20T[:, :], start=True, stop=True)
            pe.matmul(b3[0:1, 2 * P:3 * P], cols[:, R_BV:R_BV + 1], wo1[:, :], start=True, stop=True)\
                .then_inc(prep_pe, 1)
            pe.wait_ge(prep_dve, PREP_END)
            pe.wait_ge(parts_in, 16 * 3 * TILES)

            def turn(phase, i, lane, k, event):
                pe.wait_ge(normed[lane], normed.nth(phase, i, k))
                for t in range(TILES):
                    last = pe.transpose(bank[lane][0][:, t * P:(t + 1) * P], z[lane][:, t, :], ident[:, :])
                last.then_inc(transposed[lane], 1)

            def linear(into, lhs, rhs, b):
                pe.matmul(into[:, :], ones3[:, :], bias3[:, b, :, :].rearrange("j t f -> j (t f)"), start=True, stop=False)
                for t in range(TILES):
                    last = pe.matmul(into[:, t * P:(t + 1) * P], lhs[:, t * P:(t + 1) * P], rhs,
                                     start=False, stop=t == TILES - 1)
                return last

            def values(lane, weights):
                for t in range(TILES):
                    last = pe.matmul(bank[lane][1][:, t * P:(t + 1) * P], xnT[lane][:, t * P:(t + 1) * P], weights,
                                     start=True, stop=True)
                return last

            def logits(phase, i, lane, lhs, chunks):
                into = bank[lane][1][:, 0:TILES * EXPERTS]
                pe.matmul(into, ones1[:, :], gate_b[phase][:, :, :].rearrange("a t e -> a (t e)"), start=True, stop=False)
                for t in range(TILES):
                    for c in range(chunks):
                        last = pe.matmul(into[:, t * EXPERTS:(t + 1) * EXPERTS], lhs(c, t), gate_w[phase][:, c, :],
                                         start=False, stop=t == TILES - 1 and c == chunks - 1)
                last.then_inc(product[lane], 1)

            def rank_products(phase, i, lane):
                n = CLASSES[phase]
                pe.wait_ge(vector[lane], vector.nth(phase, i, "onehot"))
                hot = onehot[lane][:, :, 0:n]
                into = bank[lane][1][:, 0:TILES * n].rearrange("p (t c) -> p t c", t=TILES)
                pe.matmul(into, earlier[:, :], hot, start=True, stop=False)
                for t in range(TILES - 1):
                    pe.matmul(into[:, t + 1:TILES, :], all_ones[:, :],
                              hot[:, t:t + 1, :].to_broadcast((P, TILES - 1 - t, n)), start=False, stop=t == TILES - 2)
                total = bank[lane][1][:, TILES * 64:TILES * 64 + n]
                for t in range(TILES):
                    last = pe.matmul(total, all_ones[:, :], hot[:, t, :], start=t == 0, stop=t == TILES - 1,
                                     skip_group_check=True)
                last.then_inc(product[lane], 1)

            def plan(phase):
                n, nb = CLASSES[phase], blocks["exp" + phase[-1]]
                at = 0 if phase == "gnn0" else PLAN_STEPS["gnn0"]
                pe.wait_ge(plan_dve, at + 1)
                pe.transpose(bank[0][0][0:n, 0:P], base[:, 0:n], ident[:, :]).then_inc(plan_pe, 1)
                pe.wait_ge(plan_dve, at + 4)
                pe.matmul(bank[0][1][0:n, 0:1], upto[0:n, 0:n], nblk[0:n, :], start=True, stop=True).then_inc(plan_pe, 1)
                pe.wait_ge(plan_dve, at + 6)
                pe.matmul(bank[1][0][0:1, 0:nb], ones_col[0:n, :], past[0:n, 0:nb], start=True, stop=True)
                pe.matmul(bank[1][1][0:1, 0:nb], nblk[0:n, :], past[0:n, 0:nb], start=True, stop=True)\
                    .then_inc(plan_pe, 1)

            def gnn0_step(stage, i, lane):
                if stage == "xn_turn":
                    pe.wait_ge(activated[lane], activated.before("gnn0", i, f"hid{C - 1}"))
                    turn("gnn0", i, lane, "0", "xn")
                elif stage == "qk_v":
                    pe.wait_ge(copied[lane], copied.nth("gnn0", i, "xn"))
                    pe.wait_ge(vector[lane], vector.before("gnn0", i, "base"))
                    pe.matmul(bank[lane][0][:, :], qk0[:, :], xnT[lane][:, :], start=True, stop=True)\
                        .then_inc(product[lane], 1)
                    values(lane, wv0T[:, :]).then_inc(product[lane], 1)
                elif stage == "scores":
                    pe.wait_ge(pooled[lane], pooled.nth("gnn0", i, "mask"))
                    pe.wait_ge(activated[lane], activated.nth("gnn0", i, "v"))
                    for j in range(3):
                        pe.matmul(bank[lane][1][:, :], far0[:, j, :],
                                  no_edge[lane].rearrange("p t f -> p (t f)"), start=j == 0, stop=False)
                    for t in range(TILES):
                        last = pe.matmul(bank[lane][1][:, t * P:(t + 1) * P], qT[lane][:, t * P:(t + 1) * P],
                                         xnT[lane][:, t * P:(t + 1) * P], start=False, stop=t == TILES - 1)
                    last.then_inc(product[lane], 1)
                elif stage == "prob_turn":
                    pe.wait_ge(activated[lane], activated.nth("gnn0", i, "prob"))
                    for t in range(TILES):
                        last = pe.transpose(bank[lane][0][:, t * P:(t + 1) * P], prob[lane][:, 0, t, :], ident[:, :])
                    last.then_inc(transposed[lane], 1)
                elif stage == "mix":
                    pe.wait_ge(copied[lane], copied.nth("gnn0", i, "prob"))
                    for t in range(TILES):
                        last = pe.matmul(bank[lane][1][:, t * P:(t + 1) * P], probT[lane][:, 0, t, :], v[lane][:, t, :],
                                         start=True, stop=True)
                    last.then_inc(product[lane], 1)
                elif stage in ("z1_turn", "z2_turn"):
                    turn("gnn0", i, lane, stage[1], stage[:2])
                elif stage in ("linear1", "linear2"):
                    k = int(stage[-1])
                    pe.wait_ge(copied[lane], copied.nth("gnn0", i, f"z{k}"))
                    linear(bank[lane][1], zT[lane], (w10s, w20s)[k - 1][:, :], k - 1).then_inc(product[lane], 1)
                elif stage == "gate_turn":
                    turn("gnn0", i, lane, "gate", "gate")
                elif stage in ("hidden01", "hidden23"):
                    if stage == "hidden01":
                        pe.wait_ge(copied[lane], copied.nth("gnn0", i, "gate"))
                    for c in (int(stage[-2]), int(stage[-1])):
                        if c >= 2:
                            pe.wait_ge(activated[lane], activated.nth("gnn0", i, f"hid{c - 2}"))
                        pe.matmul(bank[lane][1 - c % 2][:, :], f0_w1[:, c * P:(c + 1) * P], xnT[lane][:, :],
                                  start=True, stop=True).then_inc(product[lane], 1)
                elif stage == "logits":
                    pe.wait_ge(activated[lane], activated.nth("gnn0", i, f"hid{C - 1}"))
                    logits("gnn0", i, lane, lambda c, t: hidden[lane][:, c, t, :], C)
                elif stage == "ranks":
                    rank_products("gnn0", i, lane)

            staggered("gnn0", pe, gnn0_step)
            plan("gnn0")

            def exp(phase):
                two = phase == "exp1"

                def row(table, at):
                    return table[:, bass.ds(at, 1), :].rearrange("p a f -> p (a f)")

                def z_turn(i, r, lane):
                    pe.wait_ge(normed[lane], normed.nth(phase, i, f"z{r}"))
                    for j, q in later(phase, i, r, -1):
                        pe.wait_ge(activated[lane], activated.nth(phase, j, f"hid{q}"))
                    pe.transpose(bank[lane][1][:, 0:P], zb[lane][r], ident[:, :]).then_inc(transposed[lane], 1)

                def up(i, r, lane):
                    pe.wait_ge(copied[lane], copied.nth(phase, i, f"z{r}"))
                    if two:
                        pe.wait_ge(up_copied[lane], up_copied.nth(phase, i, f"up{r}"))
                    weights = w_up[lane][r] if two else f0_w1[:, :]
                    for c in range(C):
                        last = pe.matmul(bank[lane][1][:, c * P:(c + 1) * P], weights[:, c * P:(c + 1) * P],
                                         zbT[lane][r], start=True, stop=True)
                    last.then_inc(product[lane], 1)

                def down(i, r, lane, experts):
                    pe.wait_ge(activated[lane], activated.nth(phase, i, f"hid{r}"))
                    for j, q in later(phase, i, r, -1):
                        pe.wait_ge(vector[lane], vector.nth(phase, j, f"out{q}"))
                    n = C // len(experts)
                    for k, e in enumerate(experts):
                        to = bank[lane][0][:, k * P:(k + 1) * P]
                        pe.matmul(to, ones3[:, :], row(down_b, e), start=True, stop=False)
                        for c in range(n):
                            last = pe.matmul(to, hb[lane][r][:, k * n + c, :],
                                             row(w_down1 if two else w_down0, e * n + c), start=False, stop=c == n - 1)
                    last.then_inc(product[lane], 1)

                def step(i, r):
                    here = classes(pe, phase, i, r)
                    for lane in LANES:
                        for j, q in later(phase, i, r, 1):
                            z_turn(j, q, lane)
                        down(i, r, lane, experts_of(phase, here, lane))
                    for j, q in later(phase, i, r, 1):
                        for lane in LANES:
                            up(j, q, lane)

                for lane in LANES:
                    z_turn(0, 0, lane)
                pe.wait_ge(loaded, LOADED + 16 * (5 if two else 2))
                for lane in LANES:
                    up(0, 0, lane)
                rounds(phase, pe, step)

            enter(pe, "exp0")
            exp("exp0")
            enter(pe, "gnn1")
            def gnn1_step(stage, i, lane):
                if stage == "xn_turn":
                    turn("gnn1", i, lane, "0", "xn")
                elif stage == "qk":
                    pe.wait_ge(copied[lane], copied.nth("gnn1", i, "xn"))
                    pe.wait_ge(vector[lane], vector.before("gnn1", i, "base"))
                    pe.matmul(bank[lane][1][:, :], wq1[:, :], xnT[lane][:, :], start=True, stop=True)\
                        .then_inc(product[lane], 1)
                    pe.matmul(bank[lane][0][:, :], wk1[:, :], xnT[lane][:, :], start=True, stop=True)\
                        .then_inc(product[lane], 1)
                elif stage == "values":
                    pe.wait_ge(activated[lane], activated.nth("gnn1", i, "q"))
                    values(lane, wv1[:, :]).then_inc(product[lane], 1)
                elif stage in ("scores01", "scores23"):
                    two = (int(stage[-2]), int(stage[-1]))
                    if two[0] == 0:
                        pe.wait_ge(pooled[lane], pooled.nth("gnn1", i, "mask_self"))
                        pe.wait_ge(activated[lane], activated.nth("gnn1", i, "v"))
                    for h in two:
                        if h >= 2:
                            pe.wait_ge(activated[lane], activated.nth("gnn1", i, f"prob{h - 2}"))
                        pe.matmul(bank[lane][h % 2][:, :], far1[:, :],
                                  no_edge1[lane].rearrange("p t f -> p (t f)"), start=True, stop=False)
                    for t in range(TILES):
                        for h in two:
                            head = slice(h * DK, (h + 1) * DK)
                            last = pe.matmul(bank[lane][h % 2][:, t * P:(t + 1) * P],
                                             qT[lane][head, t * P:(t + 1) * P],
                                             kT[lane][head, t * P:(t + 1) * P], start=False, stop=t == TILES - 1)
                            if t == TILES - 1:
                                last.then_inc(product[lane], 1)
                elif stage.startswith("prob_turn"):
                    h = int(stage[-1])
                    if h < 2:
                        pe.wait_ge(activated[lane], activated.nth("gnn1", i, f"prob{h + 2}"))
                    else:
                        pe.wait_ge(copied[lane], copied.nth("gnn1", i, f"prob{h - 2}"))
                    for t in range(TILES):
                        last = pe.transpose(bank[lane][h % 2][:, t * P:(t + 1) * P], prob[lane][:, h, t, :], ident[:, :])
                    last.then_inc(transposed[lane], 1)
                elif stage == "mix":
                    pe.wait_ge(copied[lane], copied.nth("gnn1", i, "prob3"))
                    for t in range(TILES):
                        to = bank[lane][t // 2][:, 0:2 * HEADS * (DK + 1)].rearrange("p (t h d) -> p t h d", t=2, h=HEADS)
                        for h in range(HEADS):
                            last = pe.matmul(to[:, t % 2, h, :], probT[lane][:, h, t, :], v_one[lane][:, t, h, :],
                                             start=True, stop=True)
                    last.then_inc(product[lane], 1)
                elif stage == "o_turn":
                    pe.wait_ge(vector[lane], vector.nth("gnn1", i, "hn"))
                    for t in range(TILES):
                        last = pe.transpose(bank[lane][0][:, t * P:(t + 1) * P], hn[lane][:, t, :], ident[:, :])
                    last.then_inc(transposed[lane], 1)
                elif stage == "linear":
                    pe.wait_ge(copied[lane], copied.nth("gnn1", i, "o"))
                    linear(bank[lane][1], zT[lane], wo1[:, :], 2).then_inc(product[lane], 1)
                elif stage == "gate_turn":
                    turn("gnn1", i, lane, "gate", "gate")
                elif stage == "logits":
                    pe.wait_ge(copied[lane], copied.nth("gnn1", i, "gate"))
                    logits("gnn1", i, lane, lambda c, t: xnT[lane][:, t * P:(t + 1) * P], 1)
                elif stage == "ranks":
                    rank_products("gnn1", i, lane)

            staggered("gnn1", pe, gnn1_step)
            plan("gnn1")
            enter(pe, "exp1")
            exp("exp1")

        @block.scalar
        def _(act):
            act.wait_ge(consts, CONSTS)
            for g in CLASSES:
                flat = ids[g].rearrange("(p n) a -> p (n a)", p=P)
                for at in range(0, flat.shape[1], 260):
                    to = min(at + 260, flat.shape[1])
                    act.dma_start(flat[:, at:to], empty_slot[:, 0:to - at]).then_inc(cleared, 16)

            def copy_turned(phase, i, lane, event, dst):
                act.wait_ge(transposed[lane], transposed.nth(phase, i, event))
                act.activation(dst[:, :], bank[lane][0][:, :], ACT.Copy).then_inc(copied[lane], 1)

            def gate_tanh(phase, i, lane):
                act.wait_ge(vector[lane], vector.nth(phase, i, "diff"))
                act.activation(t_half[lane][:, :, :], ediff[lane][:, :, :], ACT.Tanh, scale=0.5)\
                    .then_inc(activated[lane], 1)

            def gnn0_step(stage, i, lane):
                if stage == "xn_copy":
                    act.wait_ge(product[lane], product.before("gnn0", i, "hid3"))
                    copy_turned("gnn0", i, lane, "xn", xnT[lane])
                elif stage == "qk_copy":
                    act.wait_ge(product[lane], product.nth("gnn0", i, "qk"))
                    act.activation(qT[lane][:, :], bank[lane][0][:, :], ACT.Copy).then_inc(activated[lane], 1)
                elif stage == "v_copy":
                    act.wait_ge(product[lane], product.nth("gnn0", i, "v"))
                    act.activation(v[lane], tiles_of(bank[lane][1]), ACT.Copy).then_inc(activated[lane], 1)
                elif stage == "prob":
                    act.wait_ge(vector[lane], vector.nth("gnn0", i, "max"))
                    for t in range(TILES):
                        last = act.activation(prob[lane][:, 0, t, :], bank[lane][1][:, t * P:(t + 1) * P], ACT.Exp,
                                              bias=far[lane][:, 0, t:t + 1], accum_out=den[lane][:, t:t + 1])
                    last.then_inc(activated[lane], 1)
                elif stage == "prob_copy":
                    copy_turned("gnn0", i, lane, "prob", probT[lane][:, 0, :, :].rearrange("p t f -> p (t f)"))
                elif stage == "tanh1":
                    act.wait_ge(vector[lane], vector.nth("gnn0", i, "hn"))
                    act.activation(th[lane], hn[lane][:, :, :], ACT.Tanh, scale=0.5).then_inc(activated[lane], 1)
                elif stage in ("z1_copy", "z2_copy"):
                    copy_turned("gnn0", i, lane, stage[:2], zT[lane])
                elif stage == "tanh2":
                    act.wait_ge(product[lane], product.nth("gnn0", i, "h1"))
                    act.activation(th[lane], tiles_of(bank[lane][1]), ACT.Tanh, scale=0.5).then_inc(activated[lane], 1)
                elif stage == "gate_copy":
                    copy_turned("gnn0", i, lane, "gate", xnT[lane])
                elif stage in ("gelu01", "gelu23"):
                    for c in (int(stage[-2]), int(stage[-1])):
                        act.wait_ge(product[lane], product.nth("gnn0", i, f"hid{c}"))
                        act.activation(hidden[lane][:, c, :, :], tiles_of(bank[lane][1 - c % 2]), ACT.Gelu,
                                       bias=cols[:, R_L0B1 + c:R_L0B1 + c + 1]).then_inc(activated[lane], 1)
                elif stage == "gate_tanh":
                    gate_tanh("gnn0", i, lane)

            def gnn1_step(stage, i, lane):
                if stage == "xn_copy":
                    act.wait_ge(product[lane], product.before("gnn1", i, "logits"))
                    copy_turned("gnn1", i, lane, "xn", xnT[lane])
                elif stage == "q_copy":
                    act.wait_ge(product[lane], product.nth("gnn1", i, "q"))
                    act.activation(qT[lane][:, :], bank[lane][1][:, :], ACT.Identity, bias=bq_s[:, :], scale=QK_SCALE)\
                        .then_inc(activated[lane], 1)
                elif stage == "k_copy":
                    act.wait_ge(product[lane], product.nth("gnn1", i, "k"))
                    act.activation(kT[lane][:, :], bank[lane][0][:, :], ACT.Identity, bias=cols[:, R_BK:R_BK + 1])\
                        .then_inc(activated[lane], 1)
                elif stage == "v_copy":
                    act.wait_ge(product[lane], product.nth("gnn1", i, "v"))
                    act.activation(v_one[lane][:, :, :, 0:DK],
                                   bank[lane][1][:, :].rearrange("p (t h d) -> p t h d", t=TILES, h=HEADS), ACT.Copy)\
                        .then_inc(activated[lane], 1)
                elif stage in ("prob0", "prob1", "prob2", "prob3"):
                    h = int(stage[-1])
                    act.wait_ge(vector[lane], vector.nth("gnn1", i, f"max{h}"))
                    for t in range(TILES):
                        last = act.activation(prob[lane][:, h, t, :], bank[lane][h % 2][:, t * P:(t + 1) * P], ACT.Exp,
                                              bias=far[lane][:, h, t:t + 1])
                    last.then_inc(activated[lane], 1)
                elif stage.startswith("prob_copy"):
                    h = int(stage[-1])
                    act.wait_ge(transposed[lane], transposed.nth("gnn1", i, f"prob{h}"))
                    act.activation(probT[lane][:, h, :, :].rearrange("p t f -> p (t f)"), bank[lane][h % 2][:, :],
                                   ACT.Copy).then_inc(copied[lane], 1)
                elif stage == "o_copy":
                    copy_turned("gnn1", i, lane, "o", zT[lane])
                elif stage == "gate_copy":
                    copy_turned("gnn1", i, lane, "gate", xnT[lane])
                elif stage == "gate_tanh":
                    gate_tanh("gnn1", i, lane)

            act.preload_act_table(ACT.Exp)
            staggered("gnn0", act, gnn0_step)

            def exp(phase):
                def step(i, r):
                    here = classes(act, phase, i, r) if phase == "exp1" else None
                    for lane in LANES:
                        first = [R_L0B1] if phase == "exp0" else [e * 2 + R_L1B1 for e in experts_of(phase, here, lane)]
                        n = C // len(first)
                        act.wait_ge(product[lane], product.nth(phase, i, f"hid{r}"))
                        for c in range(C):
                            last = act.activation(hb[lane][r][:, c, :], bank[lane][1][:, c * P:(c + 1) * P], ACT.Gelu,
                                                  bias=cols[:, bass.ds(first[c // n] + c % n, 1)])
                        last.then_inc(activated[lane], 1)

                act.preload_act_table(ACT.Gelu)
                rounds(phase, act, step)

            enter(act, "exp0")
            exp("exp0")
            enter(act, "gnn1")
            act.preload_act_table(ACT.Exp)
            staggered("gnn1", act, gnn1_step)
            enter(act, "exp1")
            exp("exp1")

        @block.vector
        def _(dve):
            count = [0]

            def step(ins):
                count[0] += 1
                ins.then_inc(prep_dve, 1)
                dve.wait_ge(prep_dve, count[0])

            dve.wait_ge(prep_pe, 1)
            step(dve.tensor_copy(cols[:, :], bank[0][0][:, 0:NCOL]))
            step(dve.tensor_scalar(qk0[:, :], bank[0][1][:, 0:P], 1.0 / math.sqrt(P), None, ALU.mult))
            step(dve.tensor_copy(wv0T[:, :], bank[1][0][:, 0:P]))
            step(dve.tensor_copy(w10T[:, :], bank[1][0][:, P:2 * P]))
            step(dve.tensor_copy(w20T[:, :], bank[1][0][:, 2 * P:3 * P]))
            assert count[0] == PREP_COPIED
            step(dve.tensor_scalar(w10s[:, :], w10T[:, :], cols[:, R_LN1W:R_LN1W + 1], None, ALU.mult))
            step(dve.tensor_scalar(w20s[:, :], w20T[:, :], cols[:, R_LN2W:R_LN2W + 1], None, ALU.mult))
            step(dve.tensor_scalar(bq_s[:, :], cols[:, R_BQ:R_BQ + 1], QK_SCALE, None, ALU.mult))
            dve.wait_ge(prep_pe, 2)
            step(dve.tensor_tensor(bias_row[:, :, :], bank[1][1][0:1, 0:3 * P].rearrange("a (b f) -> a b f", b=3),
                                   bias_in[:, :, :], ALU.add))
            for whole, rest, rest2, parts in (
                    (bias_row[:, :, :], bias_rest[:, :, :], bias_rest2[:, :, :], [bias_hi[:, j, :, :] for j in range(3)]),
                    (vec[:, :], vec_rest[:, :], vec_rest2[:, :], [vec_parts[:, j, :] for j in range(3)])):
                step(dve.tensor_copy(parts[0], whole))
                step(dve.tensor_tensor(rest, whole, parts[0], ALU.subtract))
                step(dve.tensor_copy(parts[1], rest))
                step(dve.tensor_tensor(rest2, rest, parts[1], ALU.subtract))
                step(dve.tensor_copy(parts[2], rest2))
            step(dve.memset(base[:, :], 0.0))
            assert count[0] == PREP_END

            def norm_stats(phase, i, k, lane, src, to):
                if k == "0":
                    dve.wait_ge(mean_var[lane], mean_var.before(phase, i, "gate"))
                    dve.sem_inc(passed, 1)
                for t in range(TILES):
                    last = dve.bn_stats(bn[lane][:, t, :], src(t))
                last.then_inc(stats[lane], 1)
                dve.wait_ge(stats[lane], stats.nth(phase, i, k))
                dve.sem_inc(passed, 1)
                for t in range(TILES):
                    last = dve.bn_aggr(to(t), bn[lane][:, t, :])
                last.then_inc(mean_var[lane], 1)

            def norm_apply(phase, i, k, lane, src, mean, deviation):
                dve.wait_ge(rstd[lane], rstd.nth(phase, i, k))
                if k == "0":
                    dve.wait_ge(transposed[lane], transposed.before(phase, i, "gate"))
                    dve.sem_inc(passed, 1)
                for t in range(TILES):
                    last = dve.tensor_scalar(z[lane][:, t, :], src(t), mean(t), deviation(t), ALU.subtract, ALU.mult)
                last.then_inc(normed[lane], 1)

            def ln_stats(phase, i, k, lane, src):
                norm_stats(phase, i, k, lane, src, lambda t: mv[lane][:, t, :])

            def ln_apply(phase, i, k, lane, src):
                norm_apply(phase, i, k, lane, src, lambda t: mv[lane][:, t, 0:1], lambda t: rstd_t[lane][:, t:t + 1])

            def gate_stats(phase, i, lane):
                norm_stats(phase, i, "gate", lane, lambda t: y_out[lane][:, t, 0:P],
                           lambda t: y_out[lane][:, t, MEAN:RSTD + 1])

            def gate_apply(phase, i, lane):
                norm_apply(phase, i, "gate", lane, lambda t: y_out[lane][:, t, 0:P],
                           lambda t: y_out[lane][:, t, MEAN:MEAN + 1], lambda t: y_out[lane][:, t, RSTD:RSTD + 1])

            def after(phase, i, lane, event):
                dve.wait_ge(vector[lane], vector.nth(phase, i, event))
                dve.sem_inc(passed, 1)

            def done(lane, ins):
                ins.then_inc(vector[lane], 1)

            def pick(phase, i, lane):
                dve.wait_ge(product[lane], product.nth(phase, i, "logits"))
                done(lane, dve.tensor_copy(logit[lane][:, :, :], bank[lane][1][:, 0:TILES * EXPERTS]
                                           .rearrange("p (t e) -> p t e", t=TILES)))
                after(phase, i, lane, "logit")
                for t in range(TILES):
                    last = dve.max(top[lane][:, t, :], logit[lane][:, t, :])
                done(lane, last)
                after(phase, i, lane, "top")
                done(lane, dve.tensor_tensor(ediff[lane][:, :, :], top[lane][:, :, :],
                                             top[lane][:, :, 0:1].to_broadcast((P, TILES, EXPERTS)), ALU.subtract))
                for t in range(TILES):
                    last = dve.max_index(top_i[lane][:, t, :], top[lane][:, t, :], logit[lane][:, t, :])
                done(lane, last)
                after(phase, i, lane, "index")
                if phase == "gnn1":
                    done(lane, dve.tensor_copy(idx[lane][:, :, :], top_i[lane][:, :, 0:2]))
                else:
                    done(lane, dve.tensor_copy(cls[lane][:, :], top_i[lane][:, :, 0]))

            def classify(phase, i, lane):
                n, two = CLASSES[phase], phase == "gnn1"
                dve.wait_ge(activated[lane], activated.nth(phase, i, "gate"))
                dve.sem_inc(passed, 1)
                done(lane, dve.tensor_scalar(t_inv[lane][:, :, :], t_half[lane][:, :, :], -1.0, 1.0, ALU.mult, ALU.add))
                if two:
                    after(phase, i, lane, "idx")
                    i0, i1 = idx[lane][:, :, 0], idx[lane][:, :, 1]
                    dve.tensor_tensor(flip[lane][:, :], i0, i1, ALU.is_gt)
                    dve.tensor_tensor(pair[lane][:, :, 0], i0, i1, ALU.min)
                    done(lane, dve.tensor_tensor(pair[lane][:, :, 1], i0, i1, ALU.max))
                    after(phase, i, lane, "pair")
                    done(lane, dve.scalar_tensor_tensor(cls[lane][:, :], pair[lane][:, :, 0], float(EXPERTS),
                                                        pair[lane][:, :, 1], ALU.mult, ALU.add))
                after(phase, i, lane, "class" if two else "inv")
                done(lane, dve.tensor_tensor(onehot[lane][:, :, 0:n], iota_c[:, :, 0:n],
                                             cls[lane][:, :].unsqueeze(2).to_broadcast((P, TILES, n)), ALU.is_equal))
                done(lane, dve.reciprocal(t_inv[lane][:, :, :], t_inv[lane][:, :, :]))

            def weigh(phase, i, lane):
                after(phase, i, lane, "recip")
                done(lane, dve.scalar_tensor_tensor(ediff[lane][:, :, :], t_half[lane][:, :, :], 1.0,
                                                    t_inv[lane][:, :, :], ALU.add, ALU.mult))
                after(phase, i, lane, "ex")
                done(lane, dve.tensor_reduce(gsum[lane][:, :], ediff[lane][:, :, :], AX.X, ALU.add))
                after(phase, i, lane, "sum")
                if phase == "gnn0":
                    done(lane, dve.reciprocal(y_out[lane][:, :, G0], gsum[lane][:, :]))
                    return
                done(lane, dve.reciprocal(p0[lane][:, :], gsum[lane][:, :]))
                after(phase, i, lane, "p0")
                done(lane, dve.tensor_tensor(p1[lane][:, :], ediff[lane][:, :, 1], p0[lane][:, :], ALU.mult))
                after(phase, i, lane, "p1")
                done(lane, dve.tensor_tensor(pdiff[lane][:, :], p1[lane][:, :], p0[lane][:, :], ALU.subtract))
                after(phase, i, lane, "pdiff")
                done(lane, dve.tensor_tensor(swap[lane][:, :], pdiff[lane][:, :], flip[lane][:, :], ALU.mult))
                after(phase, i, lane, "swap")
                dve.tensor_tensor(y_out[lane][:, :, G0], p0[lane][:, :], swap[lane][:, :], ALU.add)
                done(lane, dve.tensor_tensor(y_out[lane][:, :, G1], p1[lane][:, :], swap[lane][:, :], ALU.subtract))

            def slots(phase, i, lane):
                n = CLASSES[phase]
                rank_v = ranks[lane][:, 0:TILES * n].rearrange("p (t c) -> p t c", t=TILES)
                dve.wait_ge(product[lane], product.nth(phase, i, "ranks"))
                if lane:
                    dve.wait_ge(vector[lane - 1], vector.nth(phase, i, "base"))
                else:
                    dve.wait_ge(vector[NL - 1], vector.before(phase, i, "base"))
                dve.sem_inc(passed, 1)
                done(lane, dve.tensor_tensor(rank_v, bank[lane][1][:, 0:TILES * n]
                                             .rearrange("p (t c) -> p t c", t=TILES),
                                             base[:, 0:n].unsqueeze(1).to_broadcast((P, TILES, n)), ALU.add))
                after(phase, i, lane, "rank_all")
                done(lane, dve.tensor_tensor(base[:, 0:n], base[:, 0:n],
                                             bank[lane][1][:, TILES * 64:TILES * 64 + n], ALU.add))
                done(lane, dve.tensor_tensor(rank_v, rank_v, onehot[lane][:, :, 0:n], ALU.mult))
                after(phase, i, lane, "rank_own")
                done(lane, dve.tensor_reduce(rank[lane][:, :], rank_v, AX.X, ALU.add))
                after(phase, i, lane, "rank")
                dve.wait_ge(counted_on[lane], counted_on.before(phase, i, "numbers"))
                dve.sem_inc(passed, 1)
                done(lane, dve.scalar_tensor_tensor(slot[lane][:, :], cls[lane][:, :], float(tokens),
                                                    rank[lane][:, :], ALU.mult, ALU.add))

            planned = [0]

            def plan(phase):
                n, ex = CLASSES[phase], "exp" + phase[-1]
                nb = blocks[ex]
                at = 0 if phase == "gnn0" else 3

                def step(ins):
                    planned[0] += 1
                    ins.then_inc(plan_dve, 1)
                    dve.wait_ge(plan_dve, planned[0])

                for lane in LANES:
                    dve.wait_ge(vector[lane], vector.end(phase))
                planned[0] += 1
                dve.sem_inc(plan_dve, 1)
                dve.wait_ge(plan_pe, at + 1)
                step(dve.tensor_scalar(cnt_i[0:n, :], bank[0][0][0:n, 0:1], float(P - 1), None, ALU.add))
                step(dve.tensor_scalar(cnt_s[0:n, :], cnt_i[0:n, :], 7, None, ALU.arith_shift_right))
                step(dve.tensor_copy(nblk[0:n, :], cnt_s[0:n, :]))
                dve.wait_ge(plan_pe, at + 2)
                step(dve.tensor_copy(ends[0:n, :], bank[0][1][0:n, 0:1]))
                step(dve.tensor_scalar(past[0:n, 0:nb], iota_b[0:n, 0:nb], ends[0:n, :], None, ALU.is_ge))
                dve.wait_ge(plan_pe, at + 3)
                step(dve.tensor_copy(b_cls[:, 0:nb], bank[1][0][0:1, 0:nb]))
                step(dve.tensor_tensor(b_off[:, 0:nb], iota_b[0:1, 0:nb], bank[1][1][0:1, 0:nb], ALU.subtract))
                step(dve.tensor_scalar(b_tmp[:, 0:nb], b_off[:, 0:nb], float(P), None, ALU.mult))
                step(dve.scalar_tensor_tensor(t_off[ex][:, 0:nb], b_cls[:, 0:nb], float(tokens), b_tmp[:, 0:nb],
                                              ALU.mult, ALU.add))
                step(dve.tensor_scalar(b_w[:, 0:nb], b_cls[:, 0:nb], float(n - 1), None, ALU.min))
                by_lane = b_w[:, 0:nb].rearrange("a (b l) -> a b l", l=NL)
                most = by_lane[:, :, NL - 1]
                for lane in range(NL - 2, -1, -1):
                    to = (packed[lane % 2] if lane else t_class[ex])[:, 0:nb // NL]
                    step(dve.scalar_tensor_tensor(to, most, float(1 << CLASS_BITS), by_lane[:, :, lane], ALU.mult,
                                                  ALU.add))
                    most = to
                if phase == "gnn0":
                    step(dve.memset(base[:, :], 0.0))
                assert planned[0] == sum(PLAN_STEPS[g] for g in ("gnn0", "gnn1")[:1 + (phase == "gnn1")])

            def exp(phase):
                def z_block(i, r):
                    for lane in LANES:
                        x_row = row_in[lane][r]
                        dve.wait_ge(gathered[lane], gathers(phase, i, r))
                        dve.tensor_scalar(zb[lane][r], x_row[:, 0:P], x_row[:, MEAN:MEAN + 1], x_row[:, RSTD:RSTD + 1],
                                          ALU.subtract, ALU.mult).then_inc(normed[lane], 1)

                def zT_block(i, r):
                    for lane in LANES:
                        dve.wait_ge(transposed[lane], transposed.nth(phase, i, f"z{r}"))
                        dve.tensor_copy(zbT[lane][r], bank[lane][1][:, 0:P]).then_inc(copied[lane], 1)

                def out_block(i, r):
                    two = phase == "exp1"
                    for lane in LANES:
                        x_row = row_in[lane][r]
                        dve.wait_ge(product[lane], product.nth(phase, i, f"y{r}"))
                        dve.scalar_tensor_tensor((part if two else yb)[lane][r], bank[lane][0][:, 0:P],
                                                 x_row[:, G0:G0 + 1], x_row[:, 0:P], ALU.mult, ALU.add)\
                            .then_inc(vector[lane], 1)
                        if two:
                            dve.wait_ge(vector[lane], vector.nth(phase, i, f"part{r}"))
                            dve.scalar_tensor_tensor(yb[lane][r], bank[lane][0][:, P:2 * P], x_row[:, G1:G1 + 1],
                                                     part[lane][r], ALU.mult, ALU.add).then_inc(vector[lane], 1)

                def up_copy(i, r):
                    if phase == "exp0":
                        return
                    here = classes(dve, phase, i, r)
                    for lane in LANES:
                        up_v = w_up[lane][r].rearrange("p (k h) -> p k h", k=2)
                        experts = experts_of(phase, here, lane)
                        for k, e in enumerate(experts):
                            last = dve.tensor_copy(up_v[:, k, :],
                                                   w_up_all[:, bass.ds(e, 1), :].rearrange("p a h -> p (a h)"))
                        last.then_inc(up_copied[lane], 1)

                def step(i, r):
                    for j, q in later(phase, i, r, 1):
                        zT_block(j, q)
                    out_block(i, r)
                    for j, q in later(phase, i, r, 2):
                        z_block(j, q)
                        up_copy(j, q)

                z_block(0, 0)
                zT_block(0, 0)
                if phase == "exp1":
                    dve.wait_ge(loaded, LOADED + 16 * 5)
                up_copy(0, 0)
                z_block(0, 1)
                up_copy(0, 1)
                rounds(phase, dve, step)

            def gate_step(phase, stage, i, lane):
                if stage == "gate_apply":
                    gate_apply(phase, i, lane)
                elif stage == "pick":
                    pick(phase, i, lane)
                elif stage == "classify":
                    classify(phase, i, lane)
                elif stage == "weigh":
                    weigh(phase, i, lane)
                elif stage == "slots":
                    slots(phase, i, lane)

            def x_tile(lane):
                return lambda t: x_in[lane][:, t, :]

            def gnn0_step(stage, i, lane):
                if stage == "ln0_stats":
                    dve.wait_ge(x_loaded[lane], x_loaded.nth("gnn0", i, "x"))
                    ln_stats("gnn0", i, "0", lane, x_tile(lane))
                elif stage == "ln0_apply":
                    ln_apply("gnn0", i, "0", lane, x_tile(lane))
                elif stage == "max":
                    dve.wait_ge(product[lane], product.nth("gnn0", i, "scores"))
                    dve.tensor_reduce(far[lane][:, 0, :], tiles_of(bank[lane][1]), AX.X, ALU.max, negate=True)\
                        .then_inc(vector[lane], 1)
                elif stage == "rden":
                    dve.wait_ge(activated[lane], activated.nth("gnn0", i, "prob"))
                    dve.reciprocal(rden[lane][:, :, 0], den[lane][:, :]).then_inc(vector[lane], 1)
                elif stage == "attention":
                    dve.wait_ge(product[lane], product.nth("gnn0", i, "mixed"))
                    dve.wait_ge(vector[lane], vector.nth("gnn0", i, "rden"))
                    dve.tensor_tensor(hn[lane][:, :, :], tiles_of(bank[lane][1]),
                                      rden[lane][:, :, 0:1].to_broadcast((P, TILES, P)), ALU.mult)\
                        .then_inc(vector[lane], 1)
                elif stage == "swish1":
                    dve.wait_ge(activated[lane], activated.nth("gnn0", i, "th0"))
                    dve.scalar_tensor_tensor(sw[lane], th[lane], 1.0, hn[lane][:, :, :], ALU.add, ALU.mult)\
                        .then_inc(vector[lane], 1)
                    dve.wait_ge(vector[lane], vector.nth("gnn0", i, "sw0"))
                    ln_stats("gnn0", i, "1", lane, lambda t: sw[lane][:, t, :])
                elif stage == "swish2":
                    dve.wait_ge(activated[lane], activated.nth("gnn0", i, "th1"))
                    dve.scalar_tensor_tensor(sw[lane], th[lane], 1.0, tiles_of(bank[lane][1]), ALU.add, ALU.mult)\
                        .then_inc(vector[lane], 1)
                    dve.wait_ge(vector[lane], vector.nth("gnn0", i, "sw1"))
                    ln_stats("gnn0", i, "2", lane, lambda t: sw[lane][:, t, :])
                elif stage in ("ln1_apply", "ln2_apply"):
                    ln_apply("gnn0", i, stage[2], lane, lambda t: sw[lane][:, t, :])
                elif stage == "ln3_stats":
                    dve.wait_ge(product[lane], product.nth("gnn0", i, "h2"))
                    ln_stats("gnn0", i, "3", lane, lambda t: bank[lane][1][:, t * P:(t + 1) * P])
                elif stage == "ln3_scale":
                    dve.wait_ge(mean_var[lane], mean_var.nth("gnn0", i, "3"))
                    for t in range(TILES):
                        last = dve.scalar_tensor_tensor(z[lane][:, t, :], bank[lane][1][:, t * P:(t + 1) * P],
                                                        mv[lane][:, t, 0:1], lnf_w[:, :], ALU.subtract, ALU.mult)
                    last.then_inc(normed[lane], 1)
                elif stage == "residual":
                    dve.wait_ge(rstd[lane], rstd.nth("gnn0", i, "3"))
                    dve.wait_ge(normed[lane], normed.nth("gnn0", i, "3"))
                    dve.wait_ge(pooled[lane], pooled.nth("gnn0", i, "kept"))
                    dve.wait_ge(stored[lane], stored.before("gnn0", i, "y"))
                    dve.sem_inc(passed, 1)
                    for t in range(TILES):
                        last = dve.scalar_tensor_tensor(y_out[lane][:, t, 0:P], z[lane][:, t, :],
                                                        rstd_t[lane][:, t:t + 1], x_res[lane][:, t, :],
                                                        ALU.mult, ALU.add)
                    last.then_inc(vector[lane], 1)
                elif stage == "gate_stats":
                    dve.wait_ge(vector[lane], vector.nth("gnn0", i, "y"))
                    gate_stats("gnn0", i, lane)
                else:
                    gate_step("gnn0", stage, i, lane)

            dve.wait_ge(consts, CONSTS)
            staggered("gnn0", dve, gnn0_step)
            plan("gnn0")
            enter(dve, "exp0")
            exp("exp0")
            enter(dve, "gnn1")
            def gnn1_step(stage, i, lane):
                if stage == "ln0_stats":
                    dve.wait_ge(x_loaded[lane], x_loaded.nth("gnn1", i, "x"))
                    ln_stats("gnn1", i, "0", lane, x_tile(lane))
                elif stage == "ln0_apply":
                    ln_apply("gnn1", i, "0", lane, x_tile(lane))
                elif stage.startswith("max"):
                    h = int(stage[-1])
                    dve.wait_ge(product[lane], product.nth("gnn1", i, f"scores{h}"))
                    dve.tensor_reduce(far[lane][:, h, :], tiles_of(bank[lane][h % 2]), AX.X, ALU.max, negate=True)\
                        .then_inc(vector[lane], 1)
                elif stage == "attention":
                    dve.wait_ge(product[lane], product.nth("gnn1", i, "mixed"))
                    for half in range(2):
                        mix = bank[lane][half][:, 0:2 * HEADS * (DK + 1)].rearrange("p (t h d) -> p t h d", t=2, h=HEADS)
                        last = dve.reciprocal(rden[lane][:, 2 * half:2 * half + 2, :], mix[:, :, :, DK])
                    last.then_inc(vector[lane], 1)
                    dve.wait_ge(vector[lane], vector.nth("gnn1", i, "rden"))
                    for half in range(2):
                        mix = bank[lane][half][:, 0:2 * HEADS * (DK + 1)].rearrange("p (t h d) -> p (t h) d", t=2, h=HEADS)
                        last = dve.tensor_tensor(
                            hn[lane][:, 2 * half:2 * half + 2, :].rearrange("p t (h d) -> p (t h) d", h=HEADS),
                            mix[:, :, 0:DK],
                            rden[lane][:, 2 * half:2 * half + 2, :].rearrange("p t h -> p (t h)").unsqueeze(2)
                            .to_broadcast((P, 2 * HEADS, DK)), ALU.mult)
                    last.then_inc(vector[lane], 1)
                elif stage == "residual":
                    dve.wait_ge(product[lane], product.nth("gnn1", i, "h"))
                    dve.wait_ge(stored[lane], stored.before("gnn1", i, "y"))
                    dve.scalar_tensor_tensor(y_out[lane][:, :, 0:P], tiles_of(bank[lane][1]), 0.0, x_in[lane][:, :, :],
                                             ALU.max, ALU.add).then_inc(vector[lane], 1)
                elif stage == "gate_stats":
                    dve.wait_ge(vector[lane], vector.nth("gnn1", i, "y"))
                    gate_stats("gnn1", i, lane)
                else:
                    gate_step("gnn1", stage, i, lane)

            staggered("gnn1", dve, gnn1_step)
            plan("gnn1")
            enter(dve, "exp1")
            exp("exp1")


CONSTS = 17 + (3 + NR) * NL + 8
PREP_COPIED = 5
PREP_END = 20
PLAN_STEPS = {"gnn0": 15, "gnn1": 14}


def kernel(**inputs):
    import numpy as np
    import concourse.bacc as bacc
    from concourse.bass_utils import run_bass_kernel_spmd

    nc = bacc.Bacc("TRN2", target_bir_lowering=False, num_devices=1)
    arrays, aps = {}, {}
    for name in ["x", "adj"] + WEIGHTS:
        a = np.ascontiguousarray(inputs[name])
        arrays[f"in_{name}"] = a
        aps[name] = nc.dram_tensor(f"in_{name}", a.shape, mybir.dt.from_np(a.dtype), kind="ExternalInput").ap()
    out = nc.dram_tensor("out", inputs["x"].shape, F32, kind="ExternalOutput").ap()
    build(nc, aps["x"], aps["adj"], {n: aps[n] for n in WEIGHTS}, out)
    r = run_bass_kernel_spmd(nc, [arrays], core_ids=[0])
    return r.results[0]["out"]
```
